# Optimizing a Trainium2 kernel written in Bass

```python
import numpy as np
import jax
import jax.numpy as jnp

def _softmax(x, axis=-1):
    return jax.nn.softmax(x, axis=axis)

def _gelu(x):
    return jax.nn.gelu(x, approximate=True)

def _silu(x):
    return jax.nn.silu(x)

def _sigmoid(x):
    return jax.nn.sigmoid(x)

def _layernorm(x, axis=-1, eps=1e-05):
    m = jnp.mean(x, axis=axis, keepdims=True)
    v = jnp.var(x, axis=axis, keepdims=True)
    return (x - m) / jnp.sqrt(v + eps)

def _scatter_add(tgt, idx, src, axis=0):
    return tgt.at[idx].add(src)

def _segment_sum(src, seg, n):
    return jax.ops.segment_sum(src, seg, n)
kernel_name = 'mk_flamingo_gated_d2_seqx_r4_44deeb'

def setup_inputs(seed: int=0):
    np.random.seed(seed)
    _w = jnp.asarray

    def _rec_inputs():
        import jax
        import jax.numpy as jnp
        _rk = jax.random.key(seed)
        x = 0.002226 + 0.9996 * jax.random.normal(jax.random.fold_in(_rk, 1), (8, 256, 256), jnp.float32)
        _lenS = 256 - jax.random.randint(jax.random.fold_in(_rk, 7), (8,), 0, max(1, 256 // 4) + 1, jnp.int32)
        _lenS2 = 256 - jax.random.randint(jax.random.fold_in(_rk, 8), (8,), 0, max(1, 256 // 4) + 1, jnp.int32)
        _ctx_1024P = jax.random.normal(jax.random.fold_in(_rk, 11), (8, 16, 256), jnp.float32)
        _ctx_1024c = jax.random.dirichlet(jax.random.fold_in(_rk, 511), 0.3 * jnp.ones((16,), jnp.float32), (8, 256))
        _ctx_1024t = jnp.einsum('bsk,bkd->bsd', _ctx_1024c, _ctx_1024P)
        _ctx_1024t = _ctx_1024t * jax.lax.rsqrt(jnp.mean(jnp.square(_ctx_1024t)) + 1e-12) * 0.953939
        ctx_1024 = -7.10856e-05 + 0.999911 * (_ctx_1024t + 0.3 * jax.random.normal(jax.random.fold_in(_rk, 611), (8, 256, 256), jnp.float32))
        _validS = jnp.arange(256)[None, :] < _lenS[:, None]
        _validS2 = jnp.arange(256)[None, :] < _lenS2[:, None]
        _causal = jnp.tril(jnp.ones((256, 256), dtype=bool))
        mask_BxS2_bk0 = jnp.logical_not(jnp.broadcast_to(_validS2[:, :], (8, 256)))
        mask_BxS2_ff1 = jnp.where(jnp.ones((8, 256), dtype=bool), 1.0, 0.0).astype(jnp.float32)
        _g = jax.random.normal(jax.random.fold_in(_rk, 9001), (2, 2), jnp.float32)
        _g = jnp.sign(_g) * jnp.maximum(jnp.abs(_g), 1.0) + (_g == 0) * 1.0
        g_xattn = _g[0]
        g_ffn = _g[1]
        return (x, ctx_1024, mask_BxS2_bk0, mask_BxS2_ff1, g_xattn, g_ffn)
    x, ctx_1024, mask_BxS2_bk0, mask_BxS2_ff1, g_xattn, g_ffn = _rec_inputs()

    def _L0_xattn_setup():
        import jax, jax.numpy as jnp
        import numpy as np
        DIM, DIM_HEAD, HEADS, SCALE = (256, 64, 8, 8.0)
        INNER = DIM_HEAD * HEADS
        LN_EPS = 1e-05
        L2_EPS = 1e-12

        def layer_norm(x, w, b):
            mu = jnp.mean(x, axis=-1, keepdims=True)
            var = jnp.mean(jnp.square(x - mu), axis=-1, keepdims=True)
            return (x - mu) * jax.lax.rsqrt(var + LN_EPS) * w + b

        def l2norm(t):
            n = jnp.sqrt(jnp.sum(jnp.square(t), axis=-1, keepdims=True))
            return t / jnp.maximum(n, L2_EPS)
        key = jax.random.key(seed)
        ks = jax.random.split(key, 8)
        b, n, m = (8, 2048, 64)
        x = jax.random.normal(ks[0], (b, n, DIM), dtype=jnp.float32)
        latents = jax.random.normal(ks[1], (b, m, DIM), dtype=jnp.float32)
        mask = jax.random.randint(ks[2], (b, n), 0, 2) > 0
        Wq = jax.random.normal(ks[3], (DIM, INNER), dtype=jnp.float32) * DIM ** (-0.5)
        Wkv = jax.random.normal(ks[4], (DIM, 2 * INNER), dtype=jnp.float32) * DIM ** (-0.5)
        Wo = jax.random.normal(ks[5], (INNER, DIM), dtype=jnp.float32) * INNER ** (-0.5)
        return {'x': x, 'latents': latents, 'mask': mask, 'ln_x_w': jnp.ones((DIM,)), 'ln_x_b': jnp.zeros((DIM,)), 'ln_l_w': jnp.ones((DIM,)), 'ln_l_b': jnp.zeros((DIM,)), 'Wq': Wq, 'Wkv': Wkv, 'q_scale': jnp.ones((DIM_HEAD,)), 'k_scale': jnp.ones((DIM_HEAD,)), 'Wo': Wo, 'ln_o_w': jnp.ones((DIM,)), 'ln_o_b': jnp.zeros((DIM,))}
    _L0_xattn_all = _L0_xattn_setup()
    _L0_xattn_in = {k: v for k, v in _L0_xattn_all.items() if k in ('ln_x_w', 'ln_x_b', 'ln_l_w', 'ln_l_b', 'Wq', 'Wkv', 'q_scale', 'k_scale', 'Wo', 'ln_o_w', 'ln_o_b')}
    del _L0_xattn_all

    def _L0_ffn_setup():
        import jax, jax.numpy as jnp
        import numpy as np
        N_HEAD = 16
        N_ACTIVE = 4
        D_MODEL = 256
        D_ATTN = 64
        B = 4
        S = 512
        key = jax.random.key(seed)
        ks = jax.random.split(key, 6)
        sc = 1.0 / np.sqrt(D_MODEL).astype(np.float32)
        return {'x': jax.random.normal(ks[0], (B, S, D_MODEL), jnp.float32), 'Wq': jax.random.normal(ks[1], (D_MODEL, N_HEAD * D_ATTN), jnp.float32) * sc, 'bq': jnp.zeros((N_HEAD * D_ATTN,), jnp.float32), 'Wk': jax.random.normal(ks[2], (D_MODEL, N_HEAD * D_ATTN), jnp.float32) * sc, 'bk': jnp.zeros((N_HEAD * D_ATTN,), jnp.float32), 'Wv': jax.random.normal(ks[3], (D_MODEL, N_HEAD * D_ATTN), jnp.float32) * sc, 'bv': jnp.zeros((N_HEAD * D_ATTN,), jnp.float32), 'Wr': jax.random.normal(ks[4], (D_MODEL, N_HEAD), jnp.float32) * sc, 'br': jnp.zeros((N_HEAD,), jnp.float32), 'Wo': jax.random.normal(ks[5], (N_ACTIVE * D_ATTN, D_MODEL), jnp.float32) * (1.0 / np.sqrt(N_ACTIVE * D_ATTN).astype(np.float32)), 'bo': jnp.zeros((D_MODEL,), jnp.float32)}
    _L0_ffn_all = _L0_ffn_setup()
    _L0_ffn_in = {k: v for k, v in _L0_ffn_all.items() if k in ('Wq', 'bq', 'Wk', 'bk', 'Wv', 'bv', 'Wr', 'br', 'Wo', 'bo')}
    del _L0_ffn_all

    def _L1_xattn_setup():
        import jax, jax.numpy as jnp
        import numpy as np
        D_MODEL = 256
        HEADS = 16
        DEPTH = D_MODEL // HEADS
        B, S = (4, 1024)
        EPS_K = 1e-06
        EPS_LN = 1e-06

        def _layernorm(x, g, b):
            m = jnp.mean(x, axis=-1, keepdims=True)
            var = jnp.var(x, axis=-1, keepdims=True)
            return (x - m) * jax.lax.rsqrt(var + EPS_LN) * g + b

        def _split_heads(x):
            bsz, sl, _ = x.shape
            return x.reshape(bsz, sl, HEADS, DEPTH).transpose(0, 2, 1, 3)
        key = jax.random.key(seed)
        ks = jax.random.split(key, 8)
        lecun = 1.0 / np.sqrt(D_MODEL)
        glorot = np.sqrt(2.0 / (D_MODEL + D_MODEL))
        return {'q': jax.random.normal(ks[0], (B, S, D_MODEL), jnp.float32), 'k': jax.random.normal(ks[1], (B, S, D_MODEL), jnp.float32), 'v': jax.random.normal(ks[2], (B, S, D_MODEL), jnp.float32), 'mask': jnp.ones((B, S), jnp.float32), 'wq': jax.random.normal(ks[3], (D_MODEL, D_MODEL), jnp.float32) * lecun, 'wk': jax.random.normal(ks[4], (D_MODEL, D_MODEL), jnp.float32) * lecun, 'wv': jax.random.normal(ks[5], (D_MODEL, D_MODEL), jnp.float32) * lecun, 'ln_gamma': jnp.ones((D_MODEL,), jnp.float32), 'ln_beta': jnp.zeros((D_MODEL,), jnp.float32), 'dense_w': jax.random.normal(ks[6], (D_MODEL, D_MODEL), jnp.float32) * glorot, 'dense_b': jnp.zeros((D_MODEL,), jnp.float32)}
    _L1_xattn_all = _L1_xattn_setup()
    _L1_xattn_in = {k: v for k, v in _L1_xattn_all.items() if k in ('wq', 'wk', 'wv', 'ln_gamma', 'ln_beta', 'dense_w', 'dense_b')}
    del _L1_xattn_all

    def _L1_ffn_setup():
        import jax, jax.numpy as jnp
        import numpy as np
        SINKHORN_ITERS = 8
        TEMPERATURE = 1.0
        EPS = 1e-06

        def sinkhorn(t):
            t = jnp.log(jnp.clip(t, EPS)) / TEMPERATURE
            for _ in range(SINKHORN_ITERS):
                t = t - jax.nn.logsumexp(t, axis=-2, keepdims=True)
                t = t - jax.nn.logsumexp(t, axis=-1, keepdims=True)
            return jnp.exp(t)
        key = jax.random.key(seed)
        k1, k2, k3 = jax.random.split(key, 3)
        B, N, D, E = (4, 1024, 256, 8)
        x = jax.random.normal(k1, (B, N, D), dtype=jnp.float32)
        gate_w = jax.random.normal(k2, (D, E), dtype=jnp.float32) * D ** (-0.5)
        experts = jax.random.normal(k3, (E, D, D), dtype=jnp.float32) * D ** (-0.5)
        return {'x': x, 'gate_w': gate_w, 'experts': experts}
    _L1_ffn_all = _L1_ffn_setup()
    _L1_ffn_in = {k: v for k, v in _L1_ffn_all.items() if k in ('gate_w', 'experts')}
    del _L1_ffn_all
    return {'x': x, 'ctx_1024': ctx_1024, 'mask_BxS2_bk0': mask_BxS2_bk0, 'mask_BxS2_ff1': mask_BxS2_ff1, 'g_xattn': g_xattn, 'g_ffn': g_ffn, 'L0_xattn_ln_x_w': _L0_xattn_in['ln_x_w'], 'L0_xattn_ln_x_b': _L0_xattn_in['ln_x_b'], 'L0_xattn_ln_l_w': _L0_xattn_in['ln_l_w'], 'L0_xattn_ln_l_b': _L0_xattn_in['ln_l_b'], 'L0_xattn_Wq': _L0_xattn_in['Wq'], 'L0_xattn_Wkv': _L0_xattn_in['Wkv'], 'L0_xattn_q_scale': _L0_xattn_in['q_scale'], 'L0_xattn_k_scale': _L0_xattn_in['k_scale'], 'L0_xattn_Wo': _L0_xattn_in['Wo'], 'L0_xattn_ln_o_w': _L0_xattn_in['ln_o_w'], 'L0_xattn_ln_o_b': _L0_xattn_in['ln_o_b'], 'L0_ffn_Wq': _L0_ffn_in['Wq'], 'L0_ffn_bq': _L0_ffn_in['bq'], 'L0_ffn_Wk': _L0_ffn_in['Wk'], 'L0_ffn_bk': _L0_ffn_in['bk'], 'L0_ffn_Wv': _L0_ffn_in['Wv'], 'L0_ffn_bv': _L0_ffn_in['bv'], 'L0_ffn_Wr': _L0_ffn_in['Wr'], 'L0_ffn_br': _L0_ffn_in['br'], 'L0_ffn_Wo': _L0_ffn_in['Wo'], 'L0_ffn_bo': _L0_ffn_in['bo'], 'L1_xattn_wq': _L1_xattn_in['wq'], 'L1_xattn_wk': _L1_xattn_in['wk'], 'L1_xattn_wv': _L1_xattn_in['wv'], 'L1_xattn_ln_gamma': _L1_xattn_in['ln_gamma'], 'L1_xattn_ln_beta': _L1_xattn_in['ln_beta'], 'L1_xattn_dense_w': _L1_xattn_in['dense_w'], 'L1_xattn_dense_b': _L1_xattn_in['dense_b'], 'L1_ffn_gate_w': _L1_ffn_in['gate_w'], 'L1_ffn_experts': _L1_ffn_in['experts']}

def reference(x, ctx_1024, mask_BxS2_bk0, mask_BxS2_ff1, g_xattn, g_ffn, L0_xattn_ln_x_w, L0_xattn_ln_x_b, L0_xattn_ln_l_w, L0_xattn_ln_l_b, L0_xattn_Wq, L0_xattn_Wkv, L0_xattn_q_scale, L0_xattn_k_scale, L0_xattn_Wo, L0_xattn_ln_o_w, L0_xattn_ln_o_b, L0_ffn_Wq, L0_ffn_bq, L0_ffn_Wk, L0_ffn_bk, L0_ffn_Wv, L0_ffn_bv, L0_ffn_Wr, L0_ffn_br, L0_ffn_Wo, L0_ffn_bo, L1_xattn_wq, L1_xattn_wk, L1_xattn_wv, L1_xattn_ln_gamma, L1_xattn_ln_beta, L1_xattn_dense_w, L1_xattn_dense_b, L1_ffn_gate_w, L1_ffn_experts):
    import jax
    import jax.numpy as jnp

    def _L0_xattn_ref(x, latents, mask, ln_x_w, ln_x_b, ln_l_w, ln_l_b, Wq, Wkv, q_scale, k_scale, Wo, ln_o_w, ln_o_b):
        import jax, jax.numpy as jnp
        import numpy as np
        DIM, DIM_HEAD, HEADS, SCALE = (256, 64, 8, 8.0)
        INNER = DIM_HEAD * HEADS
        LN_EPS = 1e-05
        L2_EPS = 1e-12

        def layer_norm(x, w, b):
            mu = jnp.mean(x, axis=-1, keepdims=True)
            var = jnp.mean(jnp.square(x - mu), axis=-1, keepdims=True)
            return (x - mu) * jax.lax.rsqrt(var + LN_EPS) * w + b

        def l2norm(t):
            n = jnp.sqrt(jnp.sum(jnp.square(t), axis=-1, keepdims=True))
            return t / jnp.maximum(n, L2_EPS)
        b, n, _ = x.shape
        m = latents.shape[1]
        x = layer_norm(x, ln_x_w, ln_x_b)
        latents = layer_norm(latents, ln_l_w, ln_l_b)
        q = latents @ Wq
        kv_input = jnp.concatenate([x, latents], axis=1)
        kv = kv_input @ Wkv
        k, v = jnp.split(kv, 2, axis=-1)

        def to_heads(t):
            return t.reshape(t.shape[0], t.shape[1], HEADS, DIM_HEAD).transpose(0, 2, 1, 3)
        q, k, v = map(to_heads, (q, k, v))
        q = l2norm(q) * q_scale
        k = l2norm(k) * k_scale
        sim = jnp.einsum('bhid,bhjd->bhij', q, k) * SCALE
        full_mask = jnp.concatenate([mask, jnp.ones((b, m), dtype=bool)], axis=1)[:, None, None, :]
        max_neg = -jnp.finfo(sim.dtype).max
        sim = jnp.where(full_mask, sim, max_neg)
        attn = jax.nn.softmax(sim.astype(jnp.float32), axis=-1).astype(sim.dtype)
        out = jnp.einsum('bhij,bhjd->bhid', attn, v)
        out = out.transpose(0, 2, 1, 3).reshape(b, m, INNER)
        return layer_norm(out @ Wo, ln_o_w, ln_o_b)

    def _L0_ffn_ref(x, Wq, bq, Wk, bk, Wv, bv, Wr, br, Wo, bo):
        import jax, jax.numpy as jnp
        import numpy as np
        N_HEAD = 16
        N_ACTIVE = 4
        D_MODEL = 256
        D_ATTN = 64
        B = 4
        S = 512
        b, s, _ = x.shape
        dist = jax.nn.softmax(jnp.mean(x @ Wr + br, axis=1), axis=-1)
        _, idx = jax.lax.top_k(dist, N_ACTIVE)
        idx = jnp.sort(idx, axis=-1)

        def proj(W, bias):
            return (x @ W + bias).reshape(b, s, N_HEAD, D_ATTN).transpose(0, 2, 1, 3)
        Q = proj(Wq, bq)
        K = proj(Wk, bk)
        V = proj(Wv, bv)
        gather = lambda t: jnp.take_along_axis(t, idx[:, :, None, None], axis=1)
        Qs, Ks, Vs = (gather(Q), gather(K), gather(V))
        scale = 1.0 / jnp.sqrt(jnp.asarray(D_ATTN, x.dtype))
        score = jax.nn.softmax(jnp.einsum('bhqd,bhkd->bhqk', Qs, Ks) * scale, axis=-1)
        O = jnp.einsum('bhqk,bhkd->bhqd', score, Vs)
        O = O.transpose(0, 2, 1, 3).reshape(b, s, N_ACTIVE * D_ATTN)
        return O @ Wo + bo

    def _L1_xattn_ref(q, k, v, mask, wq, wk, wv, ln_gamma, ln_beta, dense_w, dense_b):
        import jax, jax.numpy as jnp
        import numpy as np
        D_MODEL = 256
        HEADS = 16
        DEPTH = D_MODEL // HEADS
        B, S = (4, 1024)
        EPS_K = 1e-06
        EPS_LN = 1e-06

        def _layernorm(x, g, b):
            m = jnp.mean(x, axis=-1, keepdims=True)
            var = jnp.var(x, axis=-1, keepdims=True)
            return (x - m) * jax.lax.rsqrt(var + EPS_LN) * g + b

        def _split_heads(x):
            bsz, sl, _ = x.shape
            return x.reshape(bsz, sl, HEADS, DEPTH).transpose(0, 2, 1, 3)
        bsz = q.shape[0]
        em = mask[:, None, :, None]
        qh = _split_heads(_layernorm(q @ wq, ln_gamma, ln_beta))
        kh = _split_heads(_layernorm(k @ wk, ln_gamma, ln_beta))
        vh = _split_heads(_layernorm(v @ wv, ln_gamma, ln_beta))
        q_prime = jax.nn.relu(qh) + EPS_K
        k_prime = (jax.nn.relu(kh) + EPS_K) * em
        vh = vh * em
        kv = jnp.einsum('bhnd,bhne->bhde', k_prime, vh)
        z = 1.0 / (jnp.einsum('bhnd,bhd->bhn', q_prime, k_prime.sum(axis=-2)) + EPS_K)
        att = jnp.einsum('bhnd,bhde,bhn->bhne', q_prime, kv, z)
        att = att.reshape(bsz, -1, D_MODEL)
        out = att @ dense_w + dense_b
        return _layernorm(out, ln_gamma, ln_beta)

    def _L1_ffn_ref(x, gate_w, experts):
        import jax, jax.numpy as jnp
        import numpy as np
        SINKHORN_ITERS = 8
        TEMPERATURE = 1.0
        EPS = 1e-06

        def sinkhorn(t):
            t = jnp.log(jnp.clip(t, EPS)) / TEMPERATURE
            for _ in range(SINKHORN_ITERS):
                t = t - jax.nn.logsumexp(t, axis=-2, keepdims=True)
                t = t - jax.nn.logsumexp(t, axis=-1, keepdims=True)
            return jnp.exp(t)
        B, N, D = x.shape
        E = gate_w.shape[-1]
        M = N // E
        gate_logits = jnp.einsum('bnd,de->bne', x, gate_w)
        competitive_gates = sinkhorn(gate_logits)
        vals, idx = jax.lax.top_k(jnp.swapaxes(competitive_gates, -1, -2), M)
        gate_values = jnp.swapaxes(vals, -1, -2)
        routed_indices = jnp.swapaxes(idx, -1, -2)
        b_idx = jnp.arange(B)[:, None, None]
        routed = x[b_idx, routed_indices]
        routed = jnp.transpose(routed, (2, 0, 1, 3))
        outputs = jnp.einsum('ebmd,edf->ebmf', routed, experts)
        outputs = outputs * jnp.transpose(gate_values, (2, 0, 1))[..., None]
        vals_bmed = jnp.transpose(outputs, (1, 2, 0, 3))
        routed_back = jnp.zeros_like(x).at[b_idx, routed_indices].set(vals_bmed)
        return routed_back
    x = x + jnp.tanh(g_xattn[0]) * _L0_xattn_ref(ctx_1024, _layernorm(x, axis=-1), mask_BxS2_bk0, L0_xattn_ln_x_w, L0_xattn_ln_x_b, L0_xattn_ln_l_w, L0_xattn_ln_l_b, L0_xattn_Wq, L0_xattn_Wkv, L0_xattn_q_scale, L0_xattn_k_scale, L0_xattn_Wo, L0_xattn_ln_o_w, L0_xattn_ln_o_b)
    x = x + jnp.tanh(g_ffn[0]) * _L0_ffn_ref(_layernorm(x, axis=-1), L0_ffn_Wq, L0_ffn_bq, L0_ffn_Wk, L0_ffn_bk, L0_ffn_Wv, L0_ffn_bv, L0_ffn_Wr, L0_ffn_br, L0_ffn_Wo, L0_ffn_bo)
    x = x + jnp.tanh(g_xattn[1]) * _L1_xattn_ref(_layernorm(x, axis=-1), ctx_1024, ctx_1024, mask_BxS2_ff1, L1_xattn_wq, L1_xattn_wk, L1_xattn_wv, L1_xattn_ln_gamma, L1_xattn_ln_beta, L1_xattn_dense_w, L1_xattn_dense_b)
    x = x + jnp.tanh(g_ffn[1]) * _L1_ffn_ref(_layernorm(x, axis=-1), L1_ffn_gate_w, L1_ffn_experts)
    return x

_drawn_inputs = setup_inputs


def setup_inputs(seed=0):
    import zlib

    import numpy as np

    out = dict(_drawn_inputs(seed))
    spreads = {'g_ffn': (-1.0, 0.596),
     'L0_xattn_ln_x_w': (1.0, 0.2),
     'L0_xattn_ln_x_b': (0.0, 0.1),
     'L0_xattn_ln_l_w': (1.0, 0.2),
     'L0_xattn_ln_l_b': (0.0, 0.1),
     'L0_xattn_q_scale': (1.0, 0.2),
     'L0_xattn_k_scale': (1.0, 0.2),
     'L0_xattn_ln_o_w': (1.0, 0.2),
     'L0_xattn_ln_o_b': (0.0, 0.1),
     'L0_ffn_bq': (0.0, 0.296),
     'L0_ffn_bk': (0.0, 0.8),
     'L0_ffn_bv': (0.0, 0.1),
     'L0_ffn_br': (0.0, 0.1),
     'L0_ffn_bo': (0.0, 0.1),
     'L1_xattn_ln_gamma': (1.0, 0.2),
     'L1_xattn_ln_beta': (0.0, 0.1),
     'L1_xattn_dense_b': (0.0, 0.1)}
    factors = {}
    for name, (base, spread) in spreads.items():
        noise = np.random.default_rng([zlib.crc32(name.encode()), seed]).standard_normal(out[name].shape)
        drawn = base * np.exp(spread * noise) if base else spread * noise
        out[name] = jnp.asarray(drawn.astype(out[name].dtype))
    for name, factor in factors.items():
        out[name] = (out[name] * factor).astype(out[name].dtype)
    return out
```

```python
from contextlib import ExitStack

import concourse.bass as bass
from concourse import mybir

F32 = mybir.dt.float32
F16 = mybir.dt.float16
I32 = mybir.dt.int32
U32 = mybir.dt.uint32
U8 = mybir.dt.uint8
ALU = mybir.AluOpType
ACT = mybir.ActivationFunctionType
AX = mybir.AxisListType.X

P = 128
B, S, D = 8, 256, 256
NT = S // P
ND = D // P
HA, DH = 8, 64
INNER = HA * DH
KV = 2 * S
KT = KV // P
UNITS = HA * NT
OFF = 1e30

NH_B, NA_B = 16, 4
ROW_B = 7 * DH + 2
BIAS_B = 11 * DH
HC, DC = 16, 16
HP_C = P // DC
E, M = 8, 32
SINKHORN = 8


class Chain:

    def __init__(self, eng, sem):
        self.eng, self.sem, self.base, self.n = eng, sem, 0, 0

    def step(self, ins):
        self.n += 1
        return ins.then_inc(self.sem, 1)

    def wait(self):
        if isinstance(self.base, int) and self.base + self.n <= 0:
            return
        self.eng.wait_ge(self.sem, self.base + self.n)

    def mark(self):
        self.per, self.n = self.n, 0
        return self.per

    def leave(self, base):
        self.base, self.n = 0, base


def need(eng, sem, value):
    if isinstance(value, int) and value <= 0:
        return
    eng.wait_ge(sem, value)


def build(nc, io, stages=4):
    with ExitStack() as ctx:
        def sb(name, shape, dt=F32):
            return ctx.enter_context(nc.sbuf_tensor(name, shape, dt))

        def sem(name):
            return ctx.enter_context(nc.semaphore(name))

        pe_, dve_, act_, pool_ = nc.tensor, nc.vector, nc.scalar, nc.gpsimd
        banks = [ctx.enter_context(nc.psum_tensor(f"bank{i}", [P, 512], F32)) for i in range(8)]

        def bank16(i):
            return banks[i][:, :].bitcast(F16)

        def heads(ap):
            return ap.rearrange("p (h d) -> p h d", d=DH)

        def across(ap, n):
            return ap.unsqueeze(2).broadcast_to([P, ap.shape[1], n])

        arena = sb("arena", [P, 4 * B * NT * S])
        h_all = sb("h_all", [P, B * NT, D])
        h_flat = h_all[:, :, :].rearrange("p a b -> p (a b)")
        taken = [0]
        taken_h = [0]

        def carve(shape, dt=F32, arena=arena, taken=taken):
            elems = 1
            for n in shape[1:]:
                elems *= n
            words = elems if dt == F32 else elems // 2
            at, taken[0] = taken[0], taken[0] + words
            assert taken[0] <= arena.shape[1]
            flat = arena[:, at:at + words]
            flat = flat if dt == F32 else flat.bitcast(dt)
            names = "abcd"[:len(shape) - 1]
            sizes = {n: k for n, k in zip(names[1:], shape[2:])}
            return flat.rearrange(f"p ({' '.join(names)}) -> p {' '.join(names)}", **sizes)

        x_all = sb("x_all", [P, B * NT, D])
        c_all = sb("c_all", [P, B * NT, D])
        ident = sb("ident", [P, P])
        ident16 = sb("ident16", [P, P], F16)
        eps5 = sb("eps5", [P, 16])
        half = sb("half", [P, 16])
        mask8 = sb("mask8", [P, B, S], U8)
        gates = sb("gates", [P, 4])

        wq_a = carve([P, ND, INNER], F32, h_flat, taken_h)
        wkv_a = carve([P, ND, 2 * INNER])
        wo_a = carve([P, INNER // P, D], F32, h_flat, taken_h)
        ln_cols = sb("ln_cols", [P, 4, ND])
        qk_scale = sb("qk_scale", [P, 2, DH])
        ln_o = carve([P, 2, D], F32, h_flat, taken_h)
        stat_a = sb("stat_a", [P, KT, 6])
        mv_a = sb("mv_a", [P, KT, 2])
        rstd_a = sb("rstd_a", [P, KT])
        tiny_a = sb("tiny_a", [P, 2, KT])
        xn_a = carve([P, KT, D])
        xT_a = carve([P, ND, KV])
        v_a = carve([P, KT, INNER])
        square = carve([P, 2, INNER])
        normed = carve([P, 2, INNER])
        sumsq = sb("sumsq", [P, KT + NT, HA])
        rnorm = sb("rnorm", [P, KT + NT, HA])
        kk16 = carve([P, KT, HA, 2 * DH], F16)
        qq16 = carve([P, NT, HA, 3 * DH], F16)
        kT16 = carve([P, HA, KV], F16)
        qT16 = carve([P, 2, HA, S], F16)
        mask_row = sb("mask_row", [P, KV])
        scores = sb("scores", [P, 2, KV])
        probs = sb("probs", [P, 2, KV])
        probsT = sb("probsT", [P, 2, KV])
        negmax = sb("negmax", [P, UNITS])
        rowsum = sb("rowsum", [P, UNITS])
        recip_a = sb("recip_a", [P, HA])
        o_a = carve([P, INNER], F32, h_flat, taken_h)
        oT_a = carve([P, INNER // P, P], F32, h_flat, taken_h)
        stat_o = sb("stat_o", [P, 6])
        mv_o = sb("mv_o", [P, 2])
        rstd_o = sb("rstd_o", [P, 2])
        y_a = carve([P, D], F32, h_flat, taken_h)


        stat_n = sb("stat_n", [P, B * NT, 6])
        mv_n = sb("mv_n", [P, B * NT, 2])
        rstd_n = sb("rstd_n", [P, 2, B * NT])
        hT_all = sb("hT_all", [P, B, ND, S])
        hT = sb("hT", [P, 2, ND, S])

        h_sum = sb("h_sum", [P, ND, B])
        w_router = sb("w_router", [P, ND, NH_B])
        b_router = sb("b_router", [B, NH_B])
        logits = sb("logits", [B, NH_B])
        top = sb("top", [B, 8])
        top_at = sb("top_at", [B, 8], U32)
        neg_at = sb("neg_at", [B, 8])
        sorted_at = sb("sorted_at", [B, 8])
        chosen8 = sb("chosen8", [B, NA_B], I32)
        chosen = sb("chosen", [1, B * NA_B], I32)
        head_tab = sb("head_tab", [P, NH_B, ROW_B])
        taken[0] = 0
        head_w = carve([P, 2, NA_B, BIAS_B + 2])
        wo_b = sb("wo_b", [P, NA_B * DH // P, D])
        bo_b = sb("bo_b", [P, D])
        q_high = carve([P, NA_B, S], F16)
        q_low = carve([P, NA_B, S], F16)
        k_both = carve([P, NA_B, S], F16)
        v_b = carve([P, NT, NA_B * DH])
        negmax_b = sb("negmax_b", [P, NA_B, NT])
        rowsum_b = sb("rowsum_b", [P, NT, NA_B])
        recip_b = sb("recip_b", [P, NT * NA_B])
        o_b = carve([P, NT, NA_B * DH])
        oT_b = carve([P, ND, S])

        w_c = sb("w_c", [P, 3, ND, D])
        dense_c = sb("dense_c", [P, ND, D])
        norm_rows = sb("norm_rows", [P, 3, D])
        gated_rows = sb("gated_rows", [P, 2, D])
        norm_cols = sb("norm_cols", [P, 2, ND])
        em = sb("em", [P, B * NT])
        eps6 = sb("eps6", [P, 16])
        minus1 = sb("minus1", [P, 16])
        taken[0] = 0
        ctx_b = carve([P, 2, NT, D])
        ctxT = carve([P, ND, S])
        stat_c = sb("stat_c", [P, 6, 6])
        mv_c = sb("mv_c", [P, 6, 2])
        rstd_c = sb("rstd_c", [P, 2, 6])
        qn_c = carve([P, NT, D])
        kv_c = carve([P, NT, 2, D])
        kp_c = carve([P, NT, D])
        v_ones = sb("v_ones", [P, NT, ND, P + 1])
        qpT_c = carve([P, ND, S])
        head_block = sb("head_block", [P, P])
        head_cols = sb("head_cols", [P, HP_C])
        kv_own = carve([P, ND, P])
        kv_block = sb("kv_block", [P, ND, DC + 1])
        q_own = carve([P, ND, DC, HP_C, DC])
        den_c = sb("den_c", [P, ND, DC])
        att_c = carve([P, NT, D])
        attT_c = carve([P, ND, S])
        y_c = carve([P, NT, D])
        stat_y = sb("stat_y", [P, NT, 6])
        mv_y = sb("mv_y", [P, NT, 2])
        rstd_y = sb("rstd_y", [P, 2, NT])

        w_gate = sb("w_gate", [P, ND, E])
        w_exp = head_tab[:, :, :].rearrange("p h r -> p (h r)")[:, 0:E * ND * D]\
            .rearrange("p (e t n) -> p e t n", e=E, t=ND)
        ones = sb("ones", [P, P])
        ones16 = sb("ones16", [B * E, P], F16)
        gate_e = sb("gate_e", [P, NT, B, E])
        recip_col = sb("recip_col", [P, B, E])
        sum_row = sb("sum_row", [P, 2, B * NT])
        gateT = sb("gateT", [B * E, S])
        picked = sb("picked", [B * E, M])
        picked_at = sb("picked_at", [B * E, M], U32)
        pick_rows = sb("pick_rows", [B * E, 2, M])
        spread16 = scores[0:B * E, :, :].rearrange("p a b -> p (a b)").bitcast(F16)\
            .rearrange("p (r m) -> p r m", m=M)
        slot_cols = sb("slot_cols", [P, 2, B * E * M // P])
        token_col = sb("token_col", [P, NT])
        token_row = sb("token_row", [P, S])
        slot_key = sb("slot_key", [P, E, M])
        keyed = sb("keyed", [P, 2, S])
        winner = sb("winner", [P, 2])
        taken[0] = 0
        take = carve([P, B, NT, S])
        put = carve([P, B, 2, S])
        xgT = carve([P, ND, E, B, M])
        yT = carve([P, ND, B, E, M])
        y_e = probs[:, :, :].rearrange("p s (a n) -> p s a n", n=D)
        x_in = [sem(f"x_in{i}") for i in range(4)]
        c_in = [sem(f"c_in{i}") for i in range(4)]
        w_in = sem("w_in"); w2_in = sem("w2_in"); small_in = sem("small_in")
        out_done = sem("out_done")
        ident_ready = sem("ident_ready"); pool_steps = sem("pool_steps"); dve_steps = sem("dve_steps")
        gates_ready = sem("gates_ready"); scaled = sem("scaled"); held = sem("held"); held_pool = sem("held_pool")
        a_var = sem("a_var"); a_rstd = sem("a_rstd"); a_xn = sem("a_xn"); a_xT_ps = sem("a_xT_ps"); a_xT = sem("a_xT")
        a_kq_ps = sem("a_kq_ps"); a_sq = sem("a_sq"); a_ss = sem("a_ss"); a_rn = sem("a_rn"); a_kn = sem("a_kn")
        a_hi = sem("a_hi"); a_lo = sem("a_lo"); a_kqT_ps = sem("a_kqT_ps"); a_kqT = sem("a_kqT")
        a_v_ps = sem("a_v_ps"); a_v = sem("a_v")
        a_s_ps = sem("a_s_ps"); a_max = sem("a_max"); a_ex = sem("a_ex"); a_pT_ps = sem("a_pT_ps")
        a_pT = [sem("a_pT_dve"), sem("a_pT_act")]; a_pv = sem("a_pv")
        a_on = sem("a_on"); a_oT_ps = sem("a_oT_ps"); a_oT = sem("a_oT"); a_wo_ps = sem("a_wo_ps")
        a_ovar = sem("a_ovar"); a_orstd = sem("a_orstd"); a_y = sem("a_y"); a_x = sem("a_x")

        b_in = sem("b_in"); c_w_in = sem("c_w_in"); e_in = sem("e_in")
        n_var = sem("n_var"); n_rstd = sem("n_rstd"); n_h = sem("n_h"); n_ps = sem("n_ps"); n_hT = sem("n_hT")
        r_ps = sem("r_ps"); r_chosen = sem("r_chosen"); r_sent = sem("r_sent")
        b_scaled = sem("b_scaled"); b_bias = sem("b_bias"); b_sel = sem("b_sel"); b_qk_ps = sem("b_qk_ps")
        b_v_ps = sem("b_v_ps"); b_hi = sem("b_hi"); b_lo = sem("b_lo"); b_v = sem("b_v"); b_s_ps = sem("b_s_ps")
        b_max = sem("b_max"); b_ex = sem("b_ex"); b_pT_ps = sem("b_pT_ps"); b_pv = sem("b_pv")
        b_pT = [sem("b_pT_dve"), sem("b_pT_act")]
        b_on = sem("b_on"); b_oT_ps = sem("b_oT_ps"); b_oT = sem("b_oT"); b_wo_ps = sem("b_wo_ps"); b_x = sem("b_x")
        c_cur = sem("c_cur"); c_cT_ps = sem("c_cT_ps"); c_cT = sem("c_cT"); c_q_ps = sem("c_q_ps")
        c_kv_ps = sem("c_kv_ps"); c_var = sem("c_var"); c_rstd = sem("c_rstd"); c_qn = sem("c_qn")
        c_kvn = sem("c_kvn"); c_kvg = sem("c_kvg"); c_kvb = sem("c_kvb"); c_kp = sem("c_kp"); c_qT_ps = sem("c_qT_ps")
        c_relu = sem("c_relu"); c_qp = sem("c_qp"); c_qown = sem("c_qown"); c_qown_act = sem("c_qown_act"); c_sum_ps = sem("c_sum_ps"); c_kvm = sem("c_kvm")
        c_num_ps = sem("c_num_ps"); c_att = sem("c_att"); c_aT_ps = sem("c_aT_ps"); c_aT = sem("c_aT")
        c_y_ps = sem("c_y_ps"); c_yvar = sem("c_yvar"); c_yrstd = sem("c_yrstd"); c_yg = sem("c_yg"); c_x = sem("c_x")
        e_logit_ps = sem("e_logit_ps"); e_gate = sem("e_gate"); e_col_ps = sem("e_col_ps"); e_gT_ps = sem("e_gT_ps")
        e_picks = sem("e_picks"); e_rows_ps = sem("e_rows_ps"); e_cols_ps = sem("e_cols_ps"); e_take = sem("e_take")
        e_put = sem("e_put"); e_xg_ps = sem("e_xg_ps"); e_xg = sem("e_xg"); e_yT_ps = sem("e_yT_ps")
        e_yT = [sem("e_yT_dve"), sem("e_yT_act")]
        e_y_ps = sem("e_y_ps"); e_y = sem("e_y"); e_o_ps = sem("e_o_ps"); e_x = sem("e_x")
        consts = sem("consts")

        N16 = B * NT

        def pool_late(pool, ch):
            def token_rstd(n, wait_for):
                pool.wait_ge(n_var, n + 1)
                ch.step(pool_.tensor_tensor(rstd_n[:, 0, :], mv_n[:, :, 1], eps5[:, :], ALU.add))
                ch.wait()
                pool_.tensor_tensor(rstd_n[:, 1, :], rstd_n[:, 0, :], half[:, :], ALU.pow).then_inc(n_rstd, 1)

            token_rstd(0, a_x)
            pool.wait_ge(b_in, 16 * 7)
            pool.wait_ge(gates_ready, 1)
            ch.step(pool_.tensor_scalar(bo_b[:, :], bo_b[:, :], gates[:, 2:3], 1.0, ALU.mult, ALU.mult))
            ch.wait()
            pool.wait_ge(n_h, N16)
            with pool.Fori(0, N16) as i:
                xt = x_all[:, i, :]
                pool_.tensor_tensor(xt, xt, bo_b[:, :], ALU.add).then_inc(b_bias, 1)

            pool.wait_ge(r_sent, 16)
            pool.wait_ge(b_scaled, 1)
            pool.wait_ge(n_hT, N16)

            def choose(b, par):
                need(pool, b_v_ps, b - 1)
                need(pool, b_qk_ps, NA_B * (b - 1))
                need(pool, b_on, b - 1)
                for j in range(NA_B):
                    at = pool.value_load(chosen[0:1, bass.ds(NA_B * b + j, 1)], min_val=0, max_val=NH_B - 1)
                    twice = head_w[:, par, j, 0:8 * DH].rearrange("p (g r d) -> p g r d", r=2, d=DH)
                    row = head_tab[:, bass.ds(at, 1), :]
                    once = row[:, 0, 0:4 * DH].rearrange("p (g d) -> p g d", d=DH)
                    for r in range(2):
                        pool_.tensor_copy(twice[:, :, r, :], once)
                    pool_.tensor_copy(head_w[:, par, j, 8 * DH:].unsqueeze(1), row[:, :, 4 * DH:])
                pool_.tensor_copy(hT[:, par, :, :].unsqueeze(1), hT_all[:, bass.ds(b, 1), :, :]).then_inc(b_sel, 1)

            for b in range(2):
                choose(b, b)
            with pool.Fori(1, B // 2) as i:
                for par in range(2):
                    choose(2 * i + par, par)
            if stages < 3:
                return

            token_rstd(1, b_x)
            pool.wait_ge(gates_ready, 1)
            pool.wait_ge(c_w_in, 16 * 9)
            for r in range(2):
                ch.step(pool_.tensor_scalar(gated_rows[:, r, :], norm_rows[:, r, :], gates[:, 1:2], 1.0, ALU.mult,
                                            ALU.mult))
            ch.wait()
            pool.wait_ge(n_hT, 2 * N16)
            start = ch.n

            def linear(b, par):
                need(pool, c_q_ps, b - 1)
                need(pool, c_cT_ps, b - 1)
                pool_.tensor_copy(hT[:, par, :, :].unsqueeze(1), hT_all[:, bass.ds(b, 1), :, :])
                pool_.tensor_copy(ctx_b[:, par, :, :], c_all[:, bass.ds(NT * b, NT), :]).then_inc(c_cur, 1)
                need(pool, c_var, b + 1)
                ch.step(pool_.tensor_tensor(rstd_c[:, 1, :], mv_c[:, :, 1], eps6[:, 0:6], ALU.add))
                ch.wait()
                ch.step(pool_.tensor_tensor(rstd_c[:, 0, :], rstd_c[:, 1, :], half[:, 0:6], ALU.pow))
                ch.wait()
                ch.step(pool_.tensor_tensor(rstd_c[:, 1, :], rstd_c[:, 0, :], mv_c[:, :, 0], ALU.mult))
                ch.wait()
                pool_.tensor_tensor(rstd_c[:, 1, :], rstd_c[:, 1, :], minus1[:, 0:6], ALU.mult).then_inc(c_rstd, 1)
                need(pool, c_kvg, b + 1)
                rows4 = norm_rows[:, 1:2, :].broadcast_to([P, 2 * NT, D])
                kv4 = kv_c[:, :, :, :].rearrange("p t w d -> p (t w) d")
                pool_.tensor_tensor(kv4, kv4, rows4, ALU.add).then_inc(c_kvb, 1)
                need(pool, c_yvar, b + 1)
                ch.step(pool_.tensor_tensor(rstd_y[:, 0, :], mv_y[:, :, 1], eps6[:, 0:NT], ALU.add))
                ch.wait()
                pool_.tensor_tensor(rstd_y[:, 1, :], rstd_y[:, 0, :], half[:, 0:NT], ALU.pow).then_inc(c_yrstd, 1)
                need(pool, c_yg, b + 1)
                ch.step(pool_.tensor_tensor(y_c[:, :, :], y_c[:, :, :],
                                            gated_rows[:, 1:2, :].broadcast_to([P, NT, D]), ALU.add))
                ch.wait()
                pool.sem_inc(held_pool, 1)
                xt = x_all[:, bass.ds(NT * b, NT), :]
                pool_.tensor_tensor(xt, xt, y_c[:, :, :], ALU.add).then_inc(c_x, 1)

            for b in range(2):
                linear(b, b)
            per = (ch.n - start) // 2
            with pool.Fori(1, B // 2) as i:
                for par in range(2):
                    ch.base, ch.n = start + per * (2 * i + par), 0
                    linear(2 * i + par, par)
            ch.leave(start + per * B)
            if stages < 4:
                return
            token_rstd(2, c_x)

        def dve_late(dve, ch):
            def hold(semaphore, value):
                dve.wait_ge(semaphore, value)
                if not isinstance(value, int):
                    dve.sem_inc(held, 1)

            def norm_tokens(n, last_x):
                dve.wait_ge(*last_x)
                start = ch.n
                with dve.Fori(0, N16) as i:
                    dve_.bn_stats(stat_n[:, i, :], x_all[:, i, :]).then_inc(dve_steps, 1)
                ch.n = start + N16
                ch.wait()
                for i in range(N16):
                    last = dve_.bn_aggr(mv_n[:, i, :], stat_n[:, i, :])
                last.then_inc(n_var, 1)
                dve.wait_ge(n_rstd, n + 1)
                with dve.Fori(0, N16) as i:
                    dve_.tensor_scalar(h_all[:, i, :], x_all[:, i, :], mv_n[:, i, 0:1], rstd_n[:, 1, bass.ds(i, 1)],
                                       ALU.subtract, ALU.mult).then_inc(n_h, 1)


            norm_tokens(0, (a_x, N16))
            dve.wait_ge(b_in, 16 * 7)
            ch.step(dve_.tensor_scalar(head_tab[:, :, 0:2 * DH], head_tab[:, :, 0:2 * DH], DH ** -0.5, None, ALU.mult))
            dve_.tensor_scalar(head_tab[:, :, 7 * DH:7 * DH + 1], head_tab[:, :, 7 * DH:7 * DH + 1], DH ** -0.5, None,
                               ALU.mult).then_inc(b_scaled, 1)
            ch.step(dve_.memset(neg_at[:, :], -1e6))
            dve.wait_ge(r_ps, 1)
            ch.step(dve_.scalar_tensor_tensor(logits[:, :], banks[0][0:B, 0:NH_B], 1.0 / S, b_router[:, :], ALU.mult,
                                              ALU.add))
            ch.wait()
            ch.step(dve_.max(top[:, :], logits[:, :]))
            ch.wait()
            ch.step(dve_.max_index(top_at[:, :], top[:, :], logits[:, :]))
            ch.wait()
            ch.step(dve_.tensor_scalar(neg_at[:, 0:NA_B], top_at[:, 0:NA_B], -1.0, None, ALU.mult))
            ch.wait()
            ch.step(dve_.max(sorted_at[:, :], neg_at[:, :]))
            ch.wait()
            dve_.tensor_scalar(chosen8[:, :], sorted_at[:, 0:NA_B], -1.0, None, ALU.mult).then_inc(r_chosen, 1)

            dve.wait_ge(b_bias, N16)
            start = ch.n

            def attend(b, par):
                def low(j):
                    need(dve, b_hi, NA_B * b + j + 1)
                    w, bank = head_w[:, par, j, :], banks[j % 2]
                    dve_.scalar_tensor_tensor(q_low[:, j, :], bank[:, 0:S], w[:, BIAS_B:BIAS_B + 1], q_high[:, j, :],
                                              ALU.add, ALU.subtract)
                    kl = k_both[DH:P, j, :]
                    dve_.scalar_tensor_tensor(kl, bank[DH:P, S:2 * S], w[DH:P, BIAS_B + 1:BIAS_B + 2], kl,
                                              ALU.add, ALU.subtract).then_inc(b_lo, 1)

                def maximum(j):
                    need(dve, b_s_ps, NA_B * b + j + 1)
                    dve_.tensor_reduce(negmax_b[:, j, :], banks[2 + j % 2][:, :].rearrange("p (t n) -> p t n", n=S),
                                       AX, ALU.max, negate=True).then_inc(b_max, 1)

                def copy_pT(j):
                    need(dve, b_pT_ps, NA_B * b + j + 1)
                    need(dve, b_pv, NA_B * b + j - 1)
                    dve_.tensor_copy(probsT[:, j % 2, :], banks[4 + j % 2][:, :]).then_inc(b_pT[0], 1)

                low(0)
                low(1)
                maximum(0)
                low(2)
                maximum(1)
                low(3)
                copy_pT(0)
                maximum(2)
                maximum(3)
                copy_pT(2)
                need(dve, b_pv, NA_B * b + NA_B)
                ch.step(dve_.reciprocal(recip_b[:, :], rowsum_b[:, :, :].rearrange("p t h -> p (t h)")))
                ch.wait()
                need(dve, b_oT_ps, b)
                ch.step(dve_.tensor_tensor(heads(o_b[:, :, :].rearrange("p t n -> p (t n)")), heads(banks[7][:, :]),
                                           across(recip_b[:, :], DH), ALU.mult))
                ch.wait()
                for t in range(NT):
                    o = heads(o_b[:, t, :])
                    last = dve_.tensor_tensor(o, o, head_w[:, par, :, 10 * DH:11 * DH], ALU.add)
                last.then_inc(b_on, 1)
                need(dve, b_wo_ps, b + 1)
                xt = x_all[:, bass.ds(NT * b, NT), :]
                dve_.scalar_tensor_tensor(xt, banks[7][:, :].rearrange("p (t n) -> p t n", n=D), gates[:, 2:3], xt,
                                          ALU.mult, ALU.add).then_inc(b_x, 1)

            for b in range(2):
                attend(b, b)
            per = (ch.n - start) // 2
            with dve.Fori(1, B // 2) as i:
                for par in range(2):
                    ch.base, ch.n = start + per * (2 * i + par), 0
                    attend(2 * i + par, par)
            ch.leave(start + per * B)
            if stages < 3:
                return

            norm_tokens(1, (b_x, B))
            dve.wait_ge(consts, 1)
            dve.wait_ge(c_w_in, 16 * 9)
            start = ch.n

            def linear(b):
                need(dve, c_q_ps, b + 1)
                for t in range(NT):
                    ch.step(dve_.bn_stats(stat_c[:, t, :], banks[1][:, D * t:D * t + D]))
                need(dve, c_kv_ps, b + 1)
                for t in range(NT):
                    for w in range(2):
                        ch.step(dve_.bn_stats(stat_c[:, 2 + 2 * t + w, :], banks[2 + t][:, D * w:D * w + D]))
                hold(dve_steps, ch.base + ch.n)
                if not isinstance(b, int) or b:
                    hold(c_kvn, b)
                for i in range(6):
                    last = dve_.bn_aggr(mv_c[:, i, :], stat_c[:, i, :])
                last.then_inc(c_var, 1)
                need(dve, c_rstd, b + 1)
                need(dve, c_qT_ps, b)
                for t in range(NT):
                    last = dve_.tensor_scalar(qn_c[:, t, :], banks[1][:, D * t:D * t + D], mv_c[:, t, 0:1],
                                              rstd_c[:, 0, t:t + 1], ALU.subtract, ALU.mult)
                last.then_inc(c_qn, 1)
                need(dve, c_kvn, b + 1)
                kv4 = kv_c[:, :, :, :].rearrange("p t w d -> p (t w) d")
                dve_.tensor_tensor(kv4, kv4, norm_rows[:, 0:1, :].broadcast_to([P, 2 * NT, D]), ALU.mult)\
                    .then_inc(c_kvg, 1)
                need(dve, c_relu, b + 1)
                dve_.tensor_scalar(qpT_c[:, :, :], qpT_c[:, :, :], 1e-6, None, ALU.add).then_inc(c_qp, 1)
                need(dve, c_qp, b + 1)
                need(dve, c_num_ps, b)
                dve_.tensor_tensor(q_own[:, 0, :, :, :],
                                   qpT_c[:, 0, :].rearrange("p (r n) -> p n r", n=DC).unsqueeze(2)
                                   .broadcast_to([P, DC, HP_C, DC]),
                                   head_cols[:, :].unsqueeze(1).unsqueeze(3).broadcast_to([P, DC, HP_C, DC]),
                                   ALU.mult).then_inc(c_qown, 1)
                need(dve, c_kvb, b + 1)
                need(dve, c_sum_ps, b)
                ch.step(dve_.tensor_scalar(kp_c[:, :, :], kv_c[:, :, 0, :], 0.0, 1e-6, ALU.max, ALU.add))
                ch.wait()
                for t in range(NT):
                    mt = em[:, bass.ds(NT * b + t, 1)]
                    dve_.tensor_scalar(kp_c[:, t, :], kp_c[:, t, :], mt, None, ALU.mult)
                    last = dve_.tensor_scalar(v_ones[:, t, :, 0:P],
                                              kv_c[:, t, 1, :].rearrange("p (a n) -> p a n", n=P), mt, None, ALU.mult)
                last.then_inc(c_kp, 1)
                need(dve, c_sum_ps, b + 1)
                need(dve, c_num_ps, b)
                for dt in range(ND):
                    ch.step(dve_.tensor_tensor(kv_own[:, dt, :], banks[5][:, S * dt:S * dt + P], head_block[:, :],
                                               ALU.mult))
                ch.wait()
                for dt in range(ND):
                    dve_.tensor_reduce(kv_block[:, dt, 0:DC], kv_own[:, dt, :].rearrange("p (h e) -> p e h", e=DC), AX,
                                       ALU.add)
                    last = dve_.tensor_copy(kv_block[:, dt, DC:DC + 1], banks[5][:, S * dt + P:S * dt + P + 1])
                last.then_inc(c_kvm, 1)
                need(dve, c_num_ps, b + 1)
                for dt in range(ND):
                    num = banks[6 + dt][:, 0:DC * (DC + 1)].rearrange("p (n e) -> p n e", e=DC + 1)
                    ch.step(dve_.tensor_scalar(den_c[:, dt, :], num[:, :, DC], 1e-6, None, ALU.add))
                ch.wait()
                ch.step(dve_.reciprocal(den_c[:, :, :], den_c[:, :, :]))
                ch.wait()
                need(dve, c_aT_ps, b)
                for dt in range(ND):
                    num = banks[6 + dt][:, 0:DC * (DC + 1)].rearrange("p (n e) -> p n e", e=DC + 1)
                    last = dve_.tensor_tensor(att_c[:, dt, :].rearrange("p (n e) -> p n e", e=DC), num[:, :, 0:DC],
                                              across(den_c[:, dt, :], DC), ALU.mult)
                last.then_inc(c_att, 1)
                need(dve, c_y_ps, b + 1)
                need(dve, c_x, b)
                ch.step(dve_.tensor_tensor(y_c[:, :, :], banks[5][:, :].rearrange("p (t n) -> p t n", n=D),
                                           norm_rows[:, 2:3, :].broadcast_to([P, NT, D]), ALU.add))
                ch.wait()
                for t in range(NT):
                    ch.step(dve_.bn_stats(stat_y[:, t, :], y_c[:, t, :]))
                hold(dve_steps, ch.base + ch.n)
                for t in range(NT):
                    last = dve_.bn_aggr(mv_y[:, t, :], stat_y[:, t, :])
                last.then_inc(c_yvar, 1)
                need(dve, c_yrstd, b + 1)
                for t in range(NT):
                    ch.step(dve_.tensor_scalar(y_c[:, t, :], y_c[:, t, :], mv_y[:, t, 0:1], rstd_y[:, 1, t:t + 1],
                                               ALU.subtract, ALU.mult))
                ch.wait()
                dve_.tensor_tensor(y_c[:, :, :], y_c[:, :, :], gated_rows[:, 0:1, :].broadcast_to([P, NT, D]),
                                   ALU.mult).then_inc(c_yg, 1)

            linear(0)
            per = ch.n - start
            with dve.Fori(1, B) as b:
                ch.base, ch.n = start + per * b, 0
                linear(b)
            ch.leave(start + per * B)
            if stages < 4:
                return

            norm_tokens(2, (c_x, B))
            dve.wait_ge(e_logit_ps, 1)
            flat = gate_e[:, :, :, :].rearrange("p t b e -> p (t b) e")
            dve_.tensor_scalar(gate_e[:, :, :, :].rearrange("p t b e -> p (t b e)"), banks[0][:, 0:N16 * E], 1e-6, None,
                               ALU.max).then_inc(e_gate, 1)
            start = ch.n

            def sinkhorn(i):
                need(dve, e_col_ps, i + 1)
                ch.step(dve_.reciprocal(recip_col[:, :, :], banks[1][:, 0:B * E].rearrange("p (b e) -> p b e", e=E)))
                ch.wait()
                for t in range(NT):
                    ch.step(dve_.tensor_tensor(gate_e[:, t, :, :], gate_e[:, t, :, :], recip_col[:, :, :], ALU.mult))
                ch.wait()
                ch.step(dve_.tensor_reduce(sum_row[:, 0, :], flat, AX, ALU.add))
                ch.wait()
                ch.step(dve_.reciprocal(sum_row[:, 1, :], sum_row[:, 0, :]))
                ch.wait()
                dve_.tensor_tensor(flat, flat, across(sum_row[:, 1, :], E), ALU.mult).then_inc(e_gate, 1)

            sinkhorn(0)
            per = ch.n - start
            with dve.Fori(1, SINKHORN) as i:
                ch.base, ch.n = start + per * i, 0
                sinkhorn(i)
            ch.leave(start + per * SINKHORN)

            dve.wait_ge(e_gT_ps, 1)
            ch.step(dve_.tensor_copy(gateT[:, :], banks[2][0:B * E, 0:S]))
            ch.wait()
            for r in range(M // 8):
                cut = slice(8 * r, 8 * r + 8)
                ch.step(dve_.max(picked[:, cut], gateT[:, :]))
                ch.wait()
                ch.step(dve_.max_index(picked_at[:, cut], picked[:, cut], gateT[:, :]))
                ch.wait()
                if r < M // 8 - 1:
                    ch.step(dve_.match_replace(gateT[:, :], picked[:, cut], gateT[:, :], -1.0))
                    ch.wait()
            ch.step(dve_.tensor_copy(pick_rows[:, 0, :], picked_at[:, :]))
            ch.step(dve_.tensor_copy(pick_rows[:, 1, :], picked[:, :]))
            ch.wait()
            dve_.tensor_tensor(spread16[:, :, :], pick_rows[:, 0:1, :].broadcast_to([B * E, B * E, M]),
                               ident[0:B * E, 0:B * E].unsqueeze(2).broadcast_to([B * E, B * E, M]), ALU.mult)\
                .then_inc(e_picks, 1)
            dve.wait_ge(e_cols_ps, 1)
            turned = banks[3][0:M, 0:2 * B * E].rearrange("m (w g j) -> m w g j", w=2, j=4)
            for j in range(4):
                last = dve_.tensor_copy(slot_cols[M * j:M * j + M, :, :], turned[:, :, :, j])
            ch.step(last)
            dve.wait_ge(e_rows_ps, 1)
            for b in range(B):
                for t in range(NT):
                    slots = banks[4 + b // 2][:, S * (b % 2):S * (b % 2) + S]
                    kd, win = keyed[:, t, :], winner[:, t:t + 1]
                    ch.step(dve_.scalar_tensor_tensor(kd, slots, token_col[:, t:t + 1],
                                                      slot_key[:, :, :].rearrange("p e m -> p (e m)"), ALU.is_equal,
                                                      ALU.mult))
                    ch.wait()
                    ch.step(dve_.tensor_reduce(win, kd, AX, ALU.max))
                    ch.wait()
                    ch.step(dve_.tensor_scalar(win, win, 0.5, None, ALU.max))
                    ch.wait()
                    dve_.tensor_scalar(take[:, b, t, :], kd, win, None, ALU.is_equal).then_inc(e_take, 1)
                for half_e in range(2):
                    g = 2 * b + half_e
                    dve_.tensor_scalar(put[:, b, half_e, :], token_row[:, :], slot_cols[:, 0, g:g + 1], None,
                                       ALU.is_equal).then_inc(e_put, 1)
            for e in range(0, E, 2):
                dve.wait_ge(e_yT_ps, e + 1)
                dve_.tensor_copy(yT[:, :, :, e, :], banks[4 + e % 4][:, :].rearrange("p (a b m) -> p a b m", a=ND, m=M))\
                    .then_inc(e_yT[0], 1)
            for b in range(B):
                dve.wait_ge(e_o_ps, b + 1)
                xt = x_all[:, NT * b:NT * b + NT, :]
                dve_.scalar_tensor_tensor(xt, banks[2 + b % 2][:, :].rearrange("p (t n) -> p t n", n=D), gates[:, 3:4],
                                          xt, ALU.mult, ALU.add).then_inc(e_x, 1)

        def act_late(act):
            def copy_hT(n, sums):
                for b in range(B):
                    act.wait_ge(n_ps, B * n + b + 1)
                    for dt in range(ND):
                        extra = dict(accum_out=h_sum[:, dt, b:b + 1]) if sums else {}
                        act_.activation(hT_all[:, b, dt, :], banks[b][:, S * dt:S * dt + S], ACT.Copy, **extra)\
                            .then_inc(n_hT, 1)

            copy_hT(0, True)

            def attend(b, par):
                def high(j):
                    need(act, b_qk_ps, NA_B * b + j + 1)
                    w, bank = head_w[:, par, j, :], banks[j % 2]
                    act_.activation(q_high[:, j, :], bank[:, 0:S], ACT.Identity, bias=w[:, BIAS_B:BIAS_B + 1])
                    act_.activation(k_both[:, j, :], bank[:, S:2 * S], ACT.Identity,
                                    bias=w[:, BIAS_B + 1:BIAS_B + 2]).then_inc(b_hi, 1)

                def exps(j):
                    need(act, b_max, NA_B * b + j + 1)
                    need(act, b_pT_ps, NA_B * b + j - 1)
                    for t in range(NT):
                        last = act_.activation(probs[:, j % 2, S * t:S * t + S], banks[2 + j % 2][:, S * t:S * t + S],
                                               ACT.Exp, bias=negmax_b[:, j, t:t + 1], scale=1.0,
                                               accum_out=rowsum_b[:, t, j:j + 1])
                    last.then_inc(b_ex, 1)

                def copy_pT(j):
                    need(act, b_pT_ps, NA_B * b + j + 1)
                    need(act, b_pv, NA_B * b + j - 1)
                    act_.activation(probsT[:, j % 2, :], banks[4 + j % 2][:, :], ACT.Copy).then_inc(b_pT[1], 1)

                high(0)
                high(1)
                need(act, b_v_ps, b + 1)
                act_.activation(v_b[:, :, :], banks[6][:, :].rearrange("p (t n) -> p t n", t=NT), ACT.Copy)\
                    .then_inc(b_v, 1)
                high(2)
                exps(0)
                high(3)
                exps(1)
                exps(2)
                copy_pT(1)
                exps(3)
                copy_pT(3)
                need(act, b_oT_ps, b + 1)
                act_.activation(oT_b[:, :, :], banks[6][:, :].rearrange("p (k n) -> p k n", n=S), ACT.Copy)\
                    .then_inc(b_oT, 1)

            for b in range(2):
                attend(b, b)
            with act.Fori(1, B // 2) as i:
                for par in range(2):
                    attend(2 * i + par, par)
            if stages < 3:
                return

            copy_hT(1, False)

            def linear(b):
                need(act, c_cT_ps, b + 1)
                act_.activation(ctxT[:, :, :], banks[0][:, :].rearrange("p (k n) -> p k n", n=S), ACT.Copy)\
                    .then_inc(c_cT, 1)
                need(act, c_rstd, b + 1)
                need(act, c_kp, b)
                for t in range(NT):
                    for w in range(2):
                        i = 2 + 2 * t + w
                        last = act_.activation(kv_c[:, t, w, :], banks[2 + t][:, D * w:D * w + D], ACT.Identity,
                                               bias=rstd_c[:, 1, i:i + 1], scale=rstd_c[:, 0, i:i + 1])
                last.then_inc(c_kvn, 1)
                need(act, c_qT_ps, b + 1)
                need(act, c_num_ps, b)
                for dt in range(ND):
                    last = act_.activation(qpT_c[:, dt, :], banks[4][:, S * dt:S * dt + S], ACT.Relu,
                                           bias=norm_cols[:, 1, dt:dt + 1], scale=norm_cols[:, 0, dt:dt + 1])
                last.then_inc(c_relu, 1)
                need(act, c_qp, b + 1)
                for h in range(HP_C):
                    last = act_.activation(q_own[:, 1, :, h, :], qpT_c[:, 1, :].rearrange("p (r n) -> p n r", n=DC),
                                           ACT.Copy, scale=head_cols[:, h:h + 1])
                last.then_inc(c_qown_act, 1)
                need(act, c_aT_ps, b + 1)
                act_.activation(attT_c[:, :, :], banks[4][:, :].rearrange("p (k n) -> p k n", n=S), ACT.Copy)\
                    .then_inc(c_aT, 1)

            act.wait_ge(c_w_in, 16 * 9)
            linear(0)
            with act.Fori(1, B) as b:
                linear(b)
            if stages < 4:
                return

            copy_hT(2, False)
            for b in range(B):
                act.wait_ge(e_xg_ps, b + 1)
                act_.activation(xgT[:, :, :, b, :], banks[b % 2][:, :].rearrange("p (a e m) -> p a e m", a=ND, m=M),
                                ACT.Copy).then_inc(e_xg, 1)
            for e in range(1, E, 2):
                act.wait_ge(e_yT_ps, e + 1)
                act_.activation(yT[:, :, :, e, :], banks[4 + e % 4][:, :].rearrange("p (a b m) -> p a b m", a=ND, m=M),
                                ACT.Copy).then_inc(e_yT[1], 1)
            for b in range(B):
                act.wait_ge(e_y_ps, b + 1)
                if b >= 2:
                    act.wait_ge(e_o_ps, b - 1)
                for half_e in range(2):
                    g = 2 * b + half_e
                    last = act_.activation(y_e[:, b % 2, half_e, :], banks[b % 2][:, D * half_e:D * half_e + D],
                                           ACT.Copy, scale=slot_cols[:, 1, g:g + 1])
                last.then_inc(e_y, 1)

        def pe_late(pe):
            def transposes_h(n, waits):
                for semaphore, value in waits:
                    pe.wait_ge(semaphore, value)
                for b in range(B):
                    pe.wait_ge(n_h, N16 * n + NT * b + NT)
                    for dt in range(ND):
                        for t in range(NT):
                            last = pe_.transpose(banks[b][:, S * dt + P * t:S * dt + P * t + P],
                                                 h_all[:, NT * b + t, P * dt:P * dt + P], ident[:, :])
                    last.then_inc(n_ps, 1)

            transposes_h(0, [])
            pe.wait_ge(n_hT, N16)
            pe.wait_ge(b_in, 16 * 7)
            for k in range(ND):
                last = pe_.matmul(banks[0][0:B, 0:NH_B], h_sum[:, k, :], w_router[:, k, :], start=k == 0,
                                  stop=k == ND - 1)
            last.then_inc(r_ps, 1)
            pe.wait_ge(r_chosen, 1)

            def attend(b, par):
                hb = hT[:, par, :, :]

                def project_qk(j):
                    if j == 0:
                        need(pe, b_sel, b + 1)
                    need(pe, b_lo, NA_B * b + j - 1)
                    for w in range(2):
                        for k in range(ND):
                            at = P * (ND * w + k)
                            twice = head_w[:, par, j, at:at + P]
                            last = pe_.matmul(banks[j % 2][:, S * w:S * w + S], twice, hb[:, k, :], start=k == 0,
                                              stop=k == ND - 1)
                    last.then_inc(b_qk_ps, 1)

                def scores_of(j):
                    need(pe, b_lo, NA_B * b + j + 1)
                    need(pe, b_ex, NA_B * b + j - 1)
                    for t in range(NT):
                        for v, q in enumerate((q_high, q_low)):
                            last = pe_.matmul(banks[2 + j % 2][:, S * t:S * t + S], q[:, j, P * t:P * t + P],
                                              k_both[:, j, :], start=v == 0, stop=v == 1)
                    last.then_inc(b_s_ps, 1)

                def transposes_p(j):
                    need(pe, b_ex, NA_B * b + j + 1)
                    need(pe, b_pT[j % 2], NA_B // 2 * b + j // 2)
                    for t in range(NT):
                        for k in range(NT):
                            last = pe_.transpose(banks[4 + j % 2][:, S * k + P * t:S * k + P * t + P],
                                                 probs[:, j % 2, S * t + P * k:S * t + P * k + P], ident[:, :])
                    last.then_inc(b_pT_ps, 1)

                def values(j):
                    need(pe, b_pT[j % 2], NA_B // 2 * b + j // 2 + 1)
                    if j == 0:
                        need(pe, b_v, b + 1)
                        need(pe, b_x, b)
                    for t in range(NT):
                        for k in range(NT):
                            at = D * t + DH * j
                            last = pe_.matmul(banks[7][:, at:at + DH],
                                              probsT[:, j % 2, S * k + P * t:S * k + P * t + P],
                                              v_b[:, k, DH * j:DH * j + DH], start=k == 0, stop=k == NT - 1)
                    last.then_inc(b_pv, 1)

                project_qk(0)
                project_qk(1)
                need(pe, b_oT, b)
                for t in range(NT):
                    for k in range(ND):
                        at = DH * (8 + k)
                        last = pe_.matmul(banks[6][:, D * t:D * t + D], hb[:, k, P * t:P * t + P],
                                          head_w[:, par, :, at:at + DH], start=k == 0, stop=k == ND - 1)
                last.then_inc(b_v_ps, 1)
                scores_of(0)
                project_qk(2)
                scores_of(1)
                project_qk(3)
                transposes_p(0)
                scores_of(2)
                transposes_p(1)
                values(0)
                scores_of(3)
                transposes_p(2)
                values(1)
                transposes_p(3)
                values(2)
                values(3)
                need(pe, b_on, b + 1)
                for k in range(ND):
                    for t in range(NT):
                        last = pe_.transpose(banks[6][:, S * k + P * t:S * k + P * t + P],
                                             o_b[:, t, P * k:P * k + P], ident[:, :])
                last.then_inc(b_oT_ps, 1)
                need(pe, b_oT, b + 1)
                for t in range(NT):
                    for k in range(ND):
                        last = pe_.matmul(banks[7][:, D * t:D * t + D], oT_b[:, k, P * t:P * t + P], wo_b[:, k, :],
                                          start=k == 0, stop=k == ND - 1)
                last.then_inc(b_wo_ps, 1)

            for b in range(2):
                attend(b, b)
            with pe.Fori(1, B // 2) as i:
                for par in range(2):
                    attend(2 * i + par, par)
            if stages < 3:
                return

            transposes_h(1, [])
            pe.wait_ge(n_hT, 2 * N16)
            pe.wait_ge(c_w_in, 16 * 9)
            pe.wait_ge(consts, 1)

            def linear(b, par):
                need(pe, c_cur, b + 1)
                for k in range(ND):
                    for t in range(NT):
                        last = pe_.transpose(banks[0][:, S * k + P * t:S * k + P * t + P],
                                             ctx_b[:, par, t, P * k:P * k + P], ident[:, :])
                last.then_inc(c_cT_ps, 1)
                for t in range(NT):
                    for k in range(ND):
                        last = pe_.matmul(banks[1][:, D * t:D * t + D], hT[:, par, k, P * t:P * t + P],
                                          w_c[:, 0, k, :], start=k == 0, stop=k == ND - 1)
                last.then_inc(c_q_ps, 1)
                need(pe, c_cT, b + 1)
                for t in range(NT):
                    for k in range(ND):
                        last = pe_.matmul(banks[2 + t][:, :], ctxT[:, k, P * t:P * t + P], w_c[:, 1:3, k, :],
                                          start=k == 0, stop=k == ND - 1)
                last.then_inc(c_kv_ps, 1)
                need(pe, c_qn, b + 1)
                for k in range(ND):
                    for t in range(NT):
                        last = pe_.transpose(banks[4][:, S * k + P * t:S * k + P * t + P],
                                             qn_c[:, t, P * k:P * k + P], ident[:, :])
                last.then_inc(c_qT_ps, 1)
                need(pe, c_kp, b + 1)
                need(pe, c_yvar, b)
                for dt in range(ND):
                    for t in range(NT):
                        last = pe_.matmul(banks[5][:, S * dt:S * dt + P + 1], kp_c[:, t, P * dt:P * dt + P],
                                          v_ones[:, t, dt, :], start=t == 0, stop=t == NT - 1)
                last.then_inc(c_sum_ps, 1)
                need(pe, c_qown, b + 1)
                need(pe, c_qown_act, b + 1)
                need(pe, c_kvm, b + 1)
                for dt in range(ND):
                    for n in range(DC):
                        at = (DC + 1) * n
                        last = pe_.matmul(banks[6 + dt][:, at:at + DC + 1], q_own[:, dt, n, :, :],
                                          kv_block[:, dt, :], start=True, stop=True)
                last.then_inc(c_num_ps, 1)
                need(pe, c_att, b + 1)
                for k in range(ND):
                    for t in range(NT):
                        last = pe_.transpose(banks[4][:, S * k + P * t:S * k + P * t + P],
                                             att_c[:, t, P * k:P * k + P], ident[:, :])
                last.then_inc(c_aT_ps, 1)
                need(pe, c_aT, b + 1)
                for t in range(NT):
                    for k in range(ND):
                        last = pe_.matmul(banks[5][:, D * t:D * t + D], attT_c[:, k, P * t:P * t + P],
                                          dense_c[:, k, :], start=k == 0, stop=k == ND - 1)
                last.then_inc(c_y_ps, 1)

            for b in range(2):
                linear(b, b)
            with pe.Fori(1, B // 2) as i:
                for par in range(2):
                    linear(2 * i + par, par)
            if stages < 4:
                return

            transposes_h(2, [])
            pe.wait_ge(n_hT, 3 * N16)
            pe.wait_ge(e_in, 32)
            for b in range(B):
                for t in range(NT):
                    for k in range(ND):
                        at = E * (B * t + b)
                        last = pe_.matmul(banks[0][:, at:at + E], hT_all[:, b, k, P * t:P * t + P], w_gate[:, k, :],
                                          start=k == 0, stop=k == ND - 1)
            last.then_inc(e_logit_ps, 1)

            def column_sums(i):
                need(pe, e_gate, i + 1)
                for t in range(NT):
                    last = pe_.matmul(banks[1][:, 0:B * E], ones[:, :], gate_e[:, t, :, :], start=t == 0,
                                      stop=t == NT - 1)
                last.then_inc(e_col_ps, 1)

            column_sums(0)
            with pe.Fori(1, SINKHORN) as i:
                column_sums(i)
            pe.wait_ge(e_gate, SINKHORN + 1)
            for t in range(NT):
                last = pe_.transpose(banks[2][0:B * E, P * t:P * t + P], gate_e[:, t, :, :], ident[:, :])
            last.then_inc(e_gT_ps, 1)
            pe.wait_ge(e_picks, 1)
            for w in range(2):
                last = pe_.transpose(banks[3][0:M, B * E * w:B * E * w + B * E], pick_rows[:, w, :],
                                     ident[0:B * E, 0:B * E])
            last.then_inc(e_cols_ps, 1)
            for g in range(4):
                n = B * E // 4
                last = pe_.matmul(banks[4 + g][:, :], ones16[:, :], spread16[:, n * g:n * g + n, :], start=True,
                                  stop=True)
            last.then_inc(e_rows_ps, 1)
            for b in range(B):
                pe.wait_ge(e_take, NT * b + NT)
                if b >= 2:
                    pe.wait_ge(e_xg, b - 1)
                for k in range(ND):
                    for t in range(NT):
                        last = pe_.matmul(banks[b % 2][:, S * k:S * k + S], h_all[:, NT * b + t, P * k:P * k + P],
                                          take[:, b, t, :], start=t == 0, stop=t == NT - 1)
                last.then_inc(e_xg_ps, 1)
            pe.wait_ge(e_xg, B)
            for e in range(E):
                if e >= 4:
                    pe.wait_ge(e_yT[e % 2], (e - 4) // 2 + 1)
                for f in range(ND):
                    for k in range(ND):
                        last = pe_.matmul(banks[4 + e % 4][:, S * f:S * f + S], w_exp[:, e, k, P * f:P * f + P],
                                          xgT[:, k, e, :, :], start=k == 0, stop=k == ND - 1)
                last.then_inc(e_yT_ps, 1)
            pe.wait_ge(e_yT[0], E // 2)
            pe.wait_ge(e_yT[1], E // 2)
            pe.wait_ge(e_put, 2 * B)

            def slots_by_row(b):
                if b >= 2:
                    pe.wait_ge(e_y, b - 1)
                for half_e in range(2):
                    for f in range(ND):
                        last = pe_.transpose(banks[b % 2][:, D * half_e + P * f:D * half_e + P * f + P],
                                             yT[:, f, b, 4 * half_e:4 * half_e + 4, :], ident[:, :])
                last.then_inc(e_y_ps, 1)

            slots_by_row(0)
            for b in range(B):
                if b + 1 < B:
                    slots_by_row(b + 1)
                pe.wait_ge(e_y, b + 1)
                if b >= 2:
                    pe.wait_ge(e_x, b - 1)
                for t in range(NT):
                    for half_e in range(2):
                        last = pe_.matmul(banks[2 + b % 2][:, D * t:D * t + D], put[:, b, half_e, P * t:P * t + P],
                                          y_e[:, b % 2, half_e, :], start=half_e == 0, stop=half_e == 1)
                last.then_inc(e_o_ps, 1)

        block = ctx.enter_context(nc.Block())
        tok = "b (t p) d -> p (b t) d"
        rows = "(t p) n -> p t n"

        @block.sync
        def _(sp):
            x_v, c_v = io["x"].rearrange(tok, p=P), io["ctx_1024"].rearrange(tok, p=P)
            for i in range(4):
                sp.dma_start(c_all[:, 4 * i:4 * i + 4, :], c_v[:, 4 * i:4 * i + 4, :]).then_inc(c_in[i], 16)
                sp.dma_start(x_all[:, 4 * i:4 * i + 4, :], x_v[:, 4 * i:4 * i + 4, :]).then_inc(x_in[i], 16)
                if i == 0:
                    sp.dma_start(wkv_a[:, :, :], io["L0_xattn_Wkv"].rearrange(rows, p=P)).then_inc(w_in, 16)
                    sp.dma_start(wq_a[:, :, :], io["L0_xattn_Wq"].rearrange(rows, p=P)).then_inc(w_in, 16)
                if i == 1:
                    sp.dma_start(wo_a[:, :, :], io["L0_xattn_Wo"].rearrange(rows, p=P)).then_inc(w2_in, 16)
            sp.dma_start(head_tab[:, :, 0:6 * DH], io["head_weights"]).then_inc(b_in, 16)
            sp.dma_start(head_tab[:, :, 6 * DH:7 * DH],
                         io["L0_ffn_bv"].rearrange("(h d) -> h d", d=DH).unsqueeze(0).broadcast_to([P, NH_B, DH]))\
                .then_inc(b_in, 16)
            sp.dma_start(head_tab[:, :, 7 * DH:ROW_B], io["head_biases"]).then_inc(b_in, 16)
            sp.dma_start(w_router[:, :, :], io["L0_ffn_Wr"].rearrange(rows, p=P)).then_inc(b_in, 16)
            sp.dma_start(b_router[:, :], io["L0_ffn_br"].unsqueeze(0).broadcast_to([B, NH_B])).then_inc(b_in, 16)
            sp.dma_start(wo_b[:, :, :], io["L0_ffn_Wo"].rearrange(rows, p=P)).then_inc(b_in, 16)
            sp.dma_start(bo_b[:, :], io["L0_ffn_bo"].unsqueeze(0).broadcast_to([P, D])).then_inc(b_in, 16)
            for i, w in enumerate(("wq", "wk", "wv")):
                sp.dma_start(w_c[:, i, :, :], io[f"L1_xattn_{w}"].rearrange(rows, p=P)).then_inc(c_w_in, 16)
            sp.dma_start(dense_c[:, :, :], io["L1_xattn_dense_w"].rearrange(rows, p=P)).then_inc(c_w_in, 16)
            for i, w in enumerate(("ln_gamma", "ln_beta", "dense_b")):
                sp.dma_start(norm_rows[:, i, :], io[f"L1_xattn_{w}"].unsqueeze(0).broadcast_to([P, D]))\
                    .then_inc(c_w_in, 16)
            sp.dma_start(norm_cols[:, :, :], io["norm_cols"]).then_inc(c_w_in, 16)
            sp.dma_start(em[:, :], io["em"]).then_inc(c_w_in, 16)
            sp.dma_start(w_gate[:, :, :], io["L1_ffn_gate_w"].rearrange(rows, p=P)).then_inc(e_in, 16)
            sp.wait_ge(r_chosen, 1)
            sp.dma_start(chosen[0:1, :], chosen8[:, :]).then_inc(r_sent, 16)
            if stages > 3:
                sp.wait_ge(b_sel, B)
                sp.dma_start(w_exp[:, :, :, :], io["L1_ffn_experts"].rearrange("e (t p) n -> p e t n", p=P))\
                    .then_inc(e_in, 16)
            out_v = io["out"].rearrange(tok, p=P)
            if stages < 4:
                sp.wait_ge(*{1: (a_x, NT * B), 2: (b_x, B), 3: (c_x, B)}[stages])
                sp.dma_start(out_v, x_all[:, :, :]).then_inc(out_done, 16)
                sp.wait_ge(out_done, 16)
            else:
                for b in range(B):
                    sp.wait_ge(e_x, b + 1)
                    sp.dma_start(out_v[:, NT * b:NT * b + NT, :], x_all[:, NT * b:NT * b + NT, :]).then_inc(out_done, 16)
                sp.wait_ge(out_done, 16 * B)

        @block.gpsimd
        def _(pool):
            ch = Chain(pool, pool_steps)
            ch.step(pool_.memset(ident[:, :], 0.0))
            ch.step(pool_.memset(half[:, :], -0.5))
            ch.step(pool_.memset(eps5[:, :], 1e-5))
            ch.step(pool_.memset(eps6[:, :], 1e-6))
            ch.step(pool_.memset(minus1[:, :], -1.0))
            ch.step(pool_.memset(ones[:, :], 1.0))
            ch.step(pool_.memset(ones16[:, :], 1.0))
            ch.step(pool_.memset(v_ones[:, :, :, :], 1.0))
            ch.step(pool_.memset(head_block[:, :], 1.0))
            ch.step(pool_.memset(head_cols[:, :], 1.0))
            ch.step(pool_.iota(token_row[:, :], [[1, S]], base=0, channel_multiplier=0,
                               allow_small_or_imprecise_dtypes=True))
            ch.step(pool_.iota(token_col[:, :], [[P, NT]], base=0, channel_multiplier=1,
                               allow_small_or_imprecise_dtypes=True))
            ch.step(pool_.iota(slot_key[:, :, :], [[1, E], [E, M]], base=1, channel_multiplier=0,
                               allow_small_or_imprecise_dtypes=True))
            ch.wait()
            blocks = head_block[:, :].rearrange("p (h c) -> p h c", c=DC)
            for view, inner in ((blocks, [[0, DC]]), (head_cols[:, :], [])):
                for base, sign in ((0, 1), (DC - 1, -1)):
                    ch.step(pool_.affine_select(out=view, in_=view, compare_op=ALU.is_ge, fill=0.0, base=base,
                                                pattern=[[-sign * DC, HP_C]] + inner, channel_multiplier=sign))
                    ch.wait()
            pool_.memset(keyed[:, :, :], 0.0).then_inc(consts, 1)
            ch.wait()
            ch.step(pool_.affine_select(out=ident[:, :], in_=ident[:, :], compare_op=ALU.not_equal, fill=1.0, base=0,
                                        pattern=[[-1, P]], channel_multiplier=1))
            ch.wait()
            pool_.tensor_copy(ident16[:, :], ident[:, :]).then_inc(ident_ready, 1)
            pool.wait_ge(small_in, SMALL * 16)
            pool.wait_ge(gates_ready, 1)
            ch.step(pool_.tensor_scalar(ln_o[:, :, :], ln_o[:, :, :], gates[:, 0:1], 1.0, ALU.mult, ALU.mult))
            start = ch.n

            def rstd(b):
                need(pool, a_var, b + 1)
                need(pool, a_xn, b)
                ch.step(pool_.tensor_tensor(tiny_a[:, 0, :], mv_a[:, :, 1], eps5[:, 0:KT], ALU.add))
                ch.wait()
                ch.step(pool_.tensor_tensor(rstd_a[:, :], tiny_a[:, 0, :], half[:, 0:KT], ALU.pow))
                ch.wait()
                lat, t = rstd_a[:, NT:KT], tiny_a[:, 1, NT:KT]
                ch.step(pool_.tensor_tensor(t, lat, lat, ALU.mult))
                ch.wait()
                ch.step(pool_.tensor_tensor(t, t, mv_a[:, NT:KT, 1], ALU.mult))
                ch.wait()
                ch.step(pool_.tensor_tensor(t, t, eps5[:, 0:NT], ALU.add))
                ch.wait()
                ch.step(pool_.tensor_tensor(t, t, half[:, 0:NT], ALU.pow))
                ch.wait()
                pool_.tensor_tensor(lat, lat, t, ALU.mult).then_inc(a_rstd, 1)

            def norms(b, i):
                need(pool, a_ss, 6 * b + i + 1)
                pool_.tensor_tensor(rnorm[:, i, :], sumsq[:, i, :], half[:, 0:HA], ALU.pow).then_inc(a_rn, 1)

            def low(b, i):
                need(pool, a_hi, 6 * b + i + 1)
                dst = kk16[:, i, :, :] if i < KT else qq16[:, i - KT, :, :]
                pool_.tensor_tensor(dst[:, :, DH:2 * DH], heads(normed[:, i % 2, :]), dst[:, :, 0:DH],
                                    ALU.subtract).then_inc(a_lo, 1)

            def out_rstd(b, qt):
                need(pool, a_ovar, NT * b + qt + 1)
                ch.step(pool_.tensor_tensor(rstd_o[:, 0:1], mv_o[:, 1:2], eps5[:, 0:1], ALU.add))
                ch.wait()
                pool_.tensor_tensor(rstd_o[:, 1:2], rstd_o[:, 0:1], half[:, 0:1], ALU.pow).then_inc(a_orstd, 1)

            def residual(b, qt):
                need(pool, a_y, NT * b + qt + 1)
                ch.step(pool_.tensor_tensor(y_a[:, :], y_a[:, :], ln_o[:, 0, :], ALU.mult))
                ch.wait()
                ch.step(pool_.tensor_tensor(y_a[:, :], y_a[:, :], ln_o[:, 1, :], ALU.add))
                ch.wait()
                pool.sem_inc(held_pool, 1)
                xt = x_all[:, NT * b + qt, :]
                pool_.tensor_tensor(xt, xt, y_a[:, :], ALU.add).then_inc(a_x, 1)

            def batch(b):
                rstd(b)
                for i in range(KT + NT + 1):
                    if i < KT + NT:
                        norms(b, i)
                    if i:
                        low(b, i - 1)
                for qt in range(NT):
                    out_rstd(b, qt)
                    residual(b, qt)

            ch.n = start
            batch(0)
            per = ch.n - start
            with pool.Fori(1, B) as b:
                ch.base, ch.n = start + per * b, 0
                batch(b)
            ch.leave(start + per * B)
            if stages > 1:
                pool_late(pool, ch)

        @block.vector
        def _(dve):
            ch = Chain(dve, dve_steps)
            ch.step(dve_.memset(mask_row[:, :], 0.0))
            dve.wait_ge(small_in, SMALL * 16)
            ch.step(dve_.tensor_tensor(qk_scale[:, 0, :], qk_scale[:, 0, :], qk_scale[:, 1, :], ALU.mult))
            start = ch.n

            def hold(semaphore, value):
                if isinstance(value, int) and value <= 0:
                    return
                dve.wait_ge(semaphore, value)
                if not isinstance(value, int):
                    dve.sem_inc(held, 1)

            def token_tile(b, t):
                return c_all[:, NT * b + t, :] if t < NT else x_all[:, NT * b + t - NT, :]

            def stats(b):
                for t in range(KT):
                    ch.step(dve_.bn_stats(stat_a[:, t, :], token_tile(b, t)))
                hold(dve_steps, ch.base + ch.n)
                hold(a_xn, b)
                for t in range(KT):
                    last = dve_.bn_aggr(mv_a[:, t, :], stat_a[:, t, :])
                last.then_inc(a_var, 1)

            def norm(b):
                need(dve, a_rstd, b + 1)
                need(dve, a_xT_ps, ND * b)
                for t in range(KT):
                    last = dve_.tensor_scalar(xn_a[:, t, :], token_tile(b, t), mv_a[:, t, 0:1], rstd_a[:, t:t + 1],
                                              ALU.subtract, ALU.mult)
                last.then_inc(a_xn, 1)

            def head_sums(b, i):
                need(dve, a_sq, 6 * b + i + 1)
                ch.step(dve_.tensor_reduce(sumsq[:, i, :], heads(square[:, i % 2, :]), AX, ALU.add))
                ch.wait()
                dve_.tensor_scalar(sumsq[:, i, :], sumsq[:, i, :], 1e-24, None, ALU.max).then_inc(a_ss, 1)

            def unit_norm(b, i):
                need(dve, a_rn, 6 * b + i + 1)
                need(dve, a_lo, 6 * b + i - 1)
                n = heads(normed[:, i % 2, :])
                ins = dve_.tensor_tensor(n, heads(banks[i][:, :]), across(rnorm[:, i, :], DH), ALU.mult)
                if i >= KT:
                    ch.step(ins)
                    ch.wait()
                    ins = dve_.tensor_tensor(n, n, qk_scale[:, 0:1, :].broadcast_to([P, HA, DH]), ALU.mult)
                ins.then_inc(a_kn, 1)

            def transposed(b, j):
                need(dve, a_kqT_ps, 8 * b + j + 1)
                if j < KT:
                    dst, src = kT16[:, :, P * j:P * j + P], j
                else:
                    qt, v = divmod(j - KT, 2)
                    dst, src = qT16[:, v, :, P * qt:P * qt + P], (4 + v if qt == 0 else v)
                dve_.tensor_copy(dst, bank16(src).rearrange("p (h n) -> p h n", h=HA)).then_inc(a_kqT, 1)

            def maximum(b, u):
                need(dve, a_ex, UNITS * b + u - 1)
                hold(a_s_ps, UNITS * b + u + 1)
                dve_.tensor_tensor_reduce(out=scores[:, u % 2, :], in0=banks[2 + u % 2][:, :], in1=mask_row[:, :],
                                          scale=-8.0, scalar=3e38, op0=ALU.add, op1=ALU.min,
                                          accum_out=negmax[:, u:u + 1]).then_inc(a_max, 1)

            def copy_pT(b, u):
                need(dve, a_pT_ps, UNITS * b + u + 1)
                need(dve, a_pv, UNITS * b + u - 1)
                dve_.tensor_copy(probsT[:, u % 2, :], banks[4 + u % 2][:, :]).then_inc(a_pT[0], 1)

            def divide(b, qt):
                need(dve, a_pv, UNITS * b + HA * (qt + 1))
                ch.step(dve_.reciprocal(recip_a[:, :], rowsum[:, HA * qt:HA * qt + HA]))
                ch.wait()
                need(dve, a_oT_ps, NT * b + qt)
                dve_.tensor_tensor(heads(o_a[:, :]), heads(banks[6 + qt][:, :]), across(recip_a[:, :], DH),
                                   ALU.mult).then_inc(a_on, 1)

            def out_stats(b, qt):
                need(dve, a_wo_ps, NT * b + qt + 1)
                ch.step(dve_.bn_stats(stat_o[:, :], banks[1][:, 0:D]))
                hold(dve_steps, ch.base + ch.n)
                dve_.bn_aggr(mv_o[:, :], stat_o[:, :]).then_inc(a_ovar, 1)

            def out_norm(b, qt):
                need(dve, a_orstd, NT * b + qt + 1)
                need(dve, a_x, NT * b + qt)
                dve_.tensor_scalar(y_a[:, :], banks[1][:, 0:D], mv_o[:, 0:1], rstd_o[:, 1:2], ALU.subtract,
                                   ALU.mult).then_inc(a_y, 1)

            def batch(b):
                stats(b)
                norm(b)
                ch.step(dve_.tensor_scalar(mask_row[:, 0:S], mask8[:, b, :], OFF, -OFF, ALU.mult, ALU.add))
                n = KT + NT
                for i in range(n + 1):
                    if i < n:
                        head_sums(b, i)
                    if i:
                        unit_norm(b, i - 1)
                    if i > 2:
                        transposed(b, i - 3)
                for j in range(n - 2, 8):
                    transposed(b, j)
                hold(dve_steps, ch.base + ch.n)
                maximum(b, 0)
                maximum(b, 1)
                for u in range(UNITS):
                    if u + 2 < UNITS:
                        maximum(b, u + 2)
                    if u % 2 == 0:
                        copy_pT(b, u)
                    if u == HA:
                        divide(b, 0)
                    if u == HA + 4:
                        out_stats(b, 0)
                    if u == HA + 5:
                        out_norm(b, 0)
                divide(b, 1)
                out_stats(b, 1)
                out_norm(b, 1)

            for i in range(4):
                dve.wait_ge(c_in[i], 16)
                dve.wait_ge(x_in[i], 16)
            batch(0)
            per = ch.n - start
            with dve.Fori(1, B) as b:
                ch.base, ch.n = start + per * b, 0
                batch(b)
            ch.leave(start + per * B)
            if stages > 1:
                dve_late(dve, ch)

        @block.scalar
        def _(act):
            def row(ap):
                return ap.unsqueeze(0).broadcast_to([P, ap.shape[0]])

            pre = "L0_xattn_"
            small = [(ln_cols[:, :, :], io["ln_cols"]),
                     (gates[:, 0:2], row(io["g_xattn"])), (gates[:, 2:4], row(io["g_ffn"])),
                     (qk_scale[:, 0, :], row(io[pre + "q_scale"])), (qk_scale[:, 1, :], row(io[pre + "k_scale"])),
                     (ln_o[:, 0, :], row(io[pre + "ln_o_w"])), (ln_o[:, 1, :], row(io[pre + "ln_o_b"])),
                     (mask8[:, :, :], io["mask_BxS2_bk0"].unsqueeze(0).broadcast_to([P, B, S]))]
            assert len(small) == SMALL
            for dst, src in small:
                act.dma_start(dst, src).then_inc(small_in, 16)
            act.wait_ge(small_in, SMALL * 16)
            act_.activation(gates[:, :], gates[:, :], ACT.Tanh).then_inc(gates_ready, 1)

            def copy_xT(b):
                for dt in range(ND):
                    need(act, a_xT_ps, ND * b + dt + 1)
                    for part in range(2):
                        w, c = ln_cols[:, 2 * part, dt:dt + 1], ln_cols[:, 2 * part + 1, dt:dt + 1]
                        cut = slice(S * part, S * part + S)
                        last = act_.activation(xT_a[:, dt, cut], banks[6 + dt][:, cut], ACT.Identity, bias=c, scale=w)
                    last.then_inc(a_xT, 1)

            def squares(b, i):
                need(act, a_kq_ps, 6 * b + i + 1)
                need(act, a_ss, 6 * b + i - 1)
                act_.activation(square[:, i % 2, :], banks[i][:, :], ACT.Square).then_inc(a_sq, 1)

            def high(b, i):
                need(act, a_kn, 6 * b + i + 1)
                n = heads(normed[:, i % 2, :])
                if i < KT:
                    act_.activation(kk16[:, i, :, 0:DH], n, ACT.Copy).then_inc(a_hi, 1)
                else:
                    q = qq16[:, i - KT, :, :]
                    act_.activation(q[:, :, 0:DH], n, ACT.Copy)
                    act_.activation(q[:, :, 2 * DH:3 * DH], n, ACT.Copy).then_inc(a_hi, 1)

            def copy_v(b, t):
                need(act, a_v_ps, KT * b + t + 1)
                act_.activation(v_a[:, t, :], banks[6 + t % 2][:, :], ACT.Copy).then_inc(a_v, 1)

            def exps(b, u):
                need(act, a_max, UNITS * b + u + 1)
                need(act, a_pT_ps, UNITS * b + u - 1)
                act_.activation(probs[:, u % 2, :], scores[:, u % 2, :], ACT.Exp, bias=negmax[:, u:u + 1], scale=-1.0,
                                accum_out=rowsum[:, u:u + 1]).then_inc(a_ex, 1)

            def copy_pT(b, u):
                need(act, a_pT_ps, UNITS * b + u + 1)
                need(act, a_pv, UNITS * b + u - 1)
                act_.activation(probsT[:, u % 2, :], banks[4 + u % 2][:, :], ACT.Copy).then_inc(a_pT[1], 1)

            def copy_oT(b, qt):
                need(act, a_oT_ps, NT * b + qt + 1)
                need(act, a_wo_ps, NT * b + qt)
                act_.activation(oT_a[:, :, :], banks[0][:, :].rearrange("p (k n) -> p k n", n=P), ACT.Copy)\
                    .then_inc(a_oT, 1)

            def batch(b):
                copy_xT(b)
                n = KT + NT
                for i in range(n + 2):
                    if i < n:
                        squares(b, i)
                    if i > 1:
                        high(b, i - 2)
                for t in range(KT):
                    copy_v(b, t)
                exps(b, 0)
                for u in range(UNITS):
                    if u + 1 < UNITS:
                        exps(b, u + 1)
                    if u % 2:
                        copy_pT(b, u)
                    if u == HA + 2:
                        copy_oT(b, 0)
                copy_oT(b, 1)

            batch(0)
            with act.Fori(1, B) as b:
                batch(b)
            if stages > 1:
                act_late(act)

        @block.tensor
        def _(pe):
            def transposes_x(b):
                need(pe, a_xn, b + 1)
                need(pe, a_on, NT * b)
                for dt in range(ND):
                    for t in range(KT):
                        last = pe_.transpose(banks[6 + dt][:, P * t:P * t + P], xn_a[:, t, P * dt:P * dt + P],
                                             ident[:, :])
                    last.then_inc(a_xT_ps, 1)

            def project(bank, t, w, done):
                for k in range(ND):
                    last = pe_.matmul(banks[bank][:, :], xT_a[:, k, P * t:P * t + P], w[:, k, :], start=k == 0,
                                      stop=k == ND - 1)
                last.then_inc(done, 1)

            def project_kq(b, i):
                if i == 0:
                    need(pe, a_xT, ND * b + ND)
                    need(pe, a_oT, NT * b)
                    need(pe, a_y, NT * b)
                if i == 2:
                    need(pe, a_max, UNITS * b)
                if i == 4:
                    need(pe, a_pT[0], UNITS // 2 * b)
                    need(pe, a_pT[1], UNITS // 2 * b)
                if i < KT:
                    project(i, i, wkv_a[:, :, 0:INNER], a_kq_ps)
                else:
                    project(i, i - KT + NT, wq_a, a_kq_ps)

            def project_v(b, t):
                need(pe, a_v, KT * b + t - 1)
                project(6 + t % 2, t, wkv_a[:, :, INNER:], a_v_ps)

            def transposes_kq(b, j):
                if j < KT:
                    need(pe, a_lo, 6 * b + j + 1)
                    dst, src = bank16(j), kk16[:, j, :, :]
                else:
                    qt, v = divmod(j - KT, 2)
                    need(pe, a_lo, 6 * b + KT + qt + 1)
                    if j == KT + 1:
                        need(pe, a_kn, 6 * b + KT + NT)
                    if qt == 1:
                        need(pe, a_kqT, 8 * b + v + 1)
                    dst, src = bank16(4 + v if qt == 0 else v), qq16[:, qt, :, DH * v:DH * v + 2 * DH]
                for h in range(HA):
                    last = pe_.transpose(dst[:, P * h:P * h + P], src[:, h, :], ident16[:, :])
                last.then_inc(a_kqT_ps, 1)

            def scores_of(b, u):
                qt, h = divmod(u, HA)
                if u == 0:
                    need(pe, a_kqT, 8 * b + KT + 2)
                if u == HA:
                    need(pe, a_kqT, 8 * b + 8)
                if u >= 2:
                    need(pe, a_max, UNITS * b + u - 1)
                for v in range(2):
                    last = pe_.matmul(banks[2 + u % 2][:, :], qT16[:, v, h, P * qt:P * qt + P], kT16[:, h, :],
                                      start=v == 0, stop=v == 1)
                last.then_inc(a_s_ps, 1)

            def transposes_p(b, u):
                need(pe, a_ex, UNITS * b + u + 1)
                if u >= 2:
                    need(pe, a_pT[u % 2], UNITS // 2 * b + u // 2)
                for kt in range(KT):
                    last = pe_.transpose(banks[4 + u % 2][:, P * kt:P * kt + P], probs[:, u % 2, P * kt:P * kt + P],
                                         ident[:, :])
                last.then_inc(a_pT_ps, 1)

            def values(b, u):
                qt, h = divmod(u, HA)
                need(pe, a_pT[u % 2], UNITS // 2 * b + u // 2 + 1)
                if u == 0:
                    need(pe, a_v, KT * b + KT)
                for kt in range(KT):
                    last = pe_.matmul(banks[6 + qt][:, DH * h:DH * h + DH], probsT[:, u % 2, P * kt:P * kt + P],
                                      v_a[:, kt, DH * h:DH * h + DH], start=kt == 0, stop=kt == KT - 1)
                last.then_inc(a_pv, 1)

            def transposes_o(b, qt):
                need(pe, a_on, NT * b + qt + 1)
                for k in range(INNER // P):
                    last = pe_.transpose(banks[0][:, P * k:P * k + P], o_a[:, P * k:P * k + P], ident[:, :])
                last.then_inc(a_oT_ps, 1)

            def out_project(b, qt):
                need(pe, a_oT, NT * b + qt + 1)
                need(pe, a_y, NT * b + qt)
                for k in range(INNER // P):
                    last = pe_.matmul(banks[1][:, 0:D], oT_a[:, k, :], wo_a[:, k, :], start=k == 0,
                                      stop=k == INNER // P - 1)
                last.then_inc(a_wo_ps, 1)

            def batch(b):
                transposes_x(b)
                for i in range(KT + NT):
                    project_kq(b, i)
                project_v(b, 0)
                project_v(b, 1)
                for j in range(KT):
                    transposes_kq(b, j)
                project_v(b, 2)
                project_v(b, 3)
                for j in range(KT, 8):
                    transposes_kq(b, j)
                scores_of(b, 0)
                scores_of(b, 1)
                for u in range(UNITS):
                    if u + 2 < UNITS:
                        scores_of(b, u + 2)
                    transposes_p(b, u)
                    if u:
                        values(b, u - 1)
                    if u == HA + 1:
                        transposes_o(b, 0)
                    if u == HA + 3:
                        out_project(b, 0)
                values(b, UNITS - 1)
                transposes_o(b, 1)
                out_project(b, 1)

            pe.wait_ge(ident_ready, 1)
            pe.wait_ge(w_in, 32)
            pe.wait_ge(w2_in, 16)
            batch(0)
            with pe.Fori(1, B) as b:
                batch(b)
            if stages > 1:
                pe_late(pe)


SMALL = 8


def kernel(**inputs):
    import numpy as np
    import concourse.bacc as bacc
    from concourse.bass_utils import run_bass_kernel_spmd as run

    nc = bacc.Bacc("TRN2", target_bir_lowering=False, num_devices=1)
    arrays, io = {}, {}
    laid = {name: np.asarray(value) for name, value in inputs.items()}
    by_width = [laid.pop("L0_xattn_" + n).reshape(ND, P).T for n in ("ln_x_w", "ln_x_b", "ln_l_w", "ln_l_b")]
    laid["ln_cols"] = np.stack(by_width, axis=1)
    by_head = [laid.pop("L0_ffn_W" + n).reshape(ND, P, NH_B, DH).transpose(1, 2, 0, 3) for n in "qkv"]
    laid["head_weights"] = np.stack(by_head, axis=2).reshape(P, NH_B, 6 * DH)
    biases = np.stack([laid.pop("L0_ffn_b" + n).reshape(NH_B, DH).T for n in "qk"], axis=2)
    laid["head_biases"] = np.concatenate([biases, biases], axis=0)
    laid["norm_cols"] = np.stack([laid["L1_xattn_ln_" + n].reshape(ND, P).T for n in ("gamma", "beta")], axis=1)
    laid["em"] = laid.pop("mask_BxS2_ff1").reshape(B * NT, P).T
    for name, value in laid.items():
        a = np.ascontiguousarray(value)
        arrays[f"in_{name}"] = a
        io[name] = nc.dram_tensor(f"in_{name}", a.shape, mybir.dt.from_np(a.dtype), kind="ExternalInput").ap()
    io["out"] = nc.dram_tensor("out_0", (B, S, D), F32, kind="ExternalOutput").ap()
    build(nc, io)
    return run(nc, [arrays], core_ids=[0]).results[0]["out_0"]
```

```python
from contextlib import ExitStack

import concourse.bass as bass
from concourse import mybir

F32 = mybir.dt.float32
F16 = mybir.dt.float16
I32 = mybir.dt.int32
U32 = mybir.dt.uint32
U8 = mybir.dt.uint8
ALU = mybir.AluOpType
ACT = mybir.ActivationFunctionType
AX = mybir.AxisListType.X

P = 128
B, S, D = 8, 256, 256
NT = S // P
ND = D // P
HA, DH = 8, 64
INNER = HA * DH
KV = 2 * S
KT = KV // P
UNITS = HA * NT
OFF = 1e30

NH_B, NA_B = 16, 4
ROW_B = 7 * DH + 2
BIAS_B = 11 * DH
HC, DC = 16, 16
HP_C = P // DC
E, M = 8, 32
SINKHORN = 8


class Chain:

    def __init__(self, eng, sem):
        self.eng, self.sem, self.base, self.n = eng, sem, 0, 0

    def step(self, ins):
        self.n += 1
        return ins.then_inc(self.sem, 1)

    def wait(self):
        if isinstance(self.base, int) and self.base + self.n <= 0:
            return
        self.eng.wait_ge(self.sem, self.base + self.n)

    def mark(self):
        self.per, self.n = self.n, 0
        return self.per

    def leave(self, base):
        self.base, self.n = 0, base


def need(eng, sem, value):
    if isinstance(value, int) and value <= 0:
        return
    eng.wait_ge(sem, value)


def build(nc, io, stages=4):
    with ExitStack() as ctx:
        def sb(name, shape, dt=F32):
            return ctx.enter_context(nc.sbuf_tensor(name, shape, dt))

        def sem(name):
            return ctx.enter_context(nc.semaphore(name))

        pe_, dve_, act_, pool_ = nc.tensor, nc.vector, nc.scalar, nc.gpsimd
        banks = [ctx.enter_context(nc.psum_tensor(f"bank{i}", [P, 512], F32)) for i in range(8)]

        def bank16(i):
            return banks[i][:, :].bitcast(F16)

        def heads(ap):
            return ap.rearrange("p (h d) -> p h d", d=DH)

        def across(ap, n):
            return ap.unsqueeze(2).broadcast_to([P, ap.shape[1], n])

        arena = sb("arena", [P, 4 * B * NT * S])
        h_all = sb("h_all", [P, B * NT, D])
        h_flat = h_all[:, :, :].rearrange("p a b -> p (a b)")
        taken = [0]
        taken_h = [0]

        def carve(shape, dt=F32, arena=arena, taken=taken):
            elems = 1
            for n in shape[1:]:
                elems *= n
            words = elems if dt == F32 else elems // 2
            at, taken[0] = taken[0], taken[0] + words
            assert taken[0] <= arena.shape[1]
            flat = arena[:, at:at + words]
            flat = flat if dt == F32 else flat.bitcast(dt)
            names = "abcd"[:len(shape) - 1]
            sizes = {n: k for n, k in zip(names[1:], shape[2:])}
            return flat.rearrange(f"p ({' '.join(names)}) -> p {' '.join(names)}", **sizes)

        x_all = sb("x_all", [P, B * NT, D])
        c_all = sb("c_all", [P, B * NT, D])
        ident = sb("ident", [P, P])
        ident16 = sb("ident16", [P, P], F16)
        eps5 = sb("eps5", [P, 16])
        half = sb("half", [P, 16])
        mask8 = sb("mask8", [P, B, S], U8)
        gates = sb("gates", [P, 4])

        wq_a = carve([P, ND, INNER], F32, h_flat, taken_h)
        wkv_a = carve([P, ND, 2 * INNER])
        wo_a = carve([P, INNER // P, D], F32, h_flat, taken_h)
        ln_cols = sb("ln_cols", [P, 4, ND])
        qk_scale = sb("qk_scale", [P, 2, DH])
        ln_o = carve([P, 2, D], F32, h_flat, taken_h)
        stat_a = sb("stat_a", [P, KT, 6])
        mv_a = sb("mv_a", [P, KT, 2])
        rstd_a = sb("rstd_a", [P, KT])
        tiny_a = sb("tiny_a", [P, 2, KT])
        xn_a = carve([P, KT, D])
        xT_a = carve([P, ND, KV])
        v_a = carve([P, KT, INNER])
        square = carve([P, 2, INNER])
        normed = carve([P, 2, INNER])
        sumsq = sb("sumsq", [P, KT + NT, HA])
        rnorm = sb("rnorm", [P, KT + NT, HA])
        kk16 = carve([P, KT, HA, 2 * DH], F16)
        qq16 = carve([P, NT, HA, 3 * DH], F16)
        kT16 = carve([P, HA, KV], F16)
        qT16 = carve([P, 2, HA, S], F16)
        mask_row = sb("mask_row", [P, KV])
        scores = sb("scores", [P, 2, KV])
        probs = sb("probs", [P, 2, KV])
        probsT = sb("probsT", [P, 2, KV])
        negmax = sb("negmax", [P, UNITS])
        rowsum = sb("rowsum", [P, UNITS])
        recip_a = sb("recip_a", [P, HA])
        o_a = carve([P, INNER], F32, h_flat, taken_h)
        oT_a = carve([P, INNER // P, P], F32, h_flat, taken_h)
        stat_o = sb("stat_o", [P, 6])
        mv_o = sb("mv_o", [P, 2])
        rstd_o = sb("rstd_o", [P, 2])
        y_a = carve([P, D], F32, h_flat, taken_h)


        stat_n = sb("stat_n", [P, B * NT, 6])
        mv_n = sb("mv_n", [P, B * NT, 2])
        rstd_n = sb("rstd_n", [P, 2, B * NT])
        hT_all = sb("hT_all", [P, B, ND, S])
        hT = sb("hT", [P, 2, ND, S])

        h_sum = sb("h_sum", [P, ND, B])
        w_router = sb("w_router", [P, ND, NH_B])
        b_router = sb("b_router", [B, NH_B])
        logits = sb("logits", [B, NH_B])
        top = sb("top", [B, 8])
        top_at = sb("top_at", [B, 8], U32)
        neg_at = sb("neg_at", [B, 8])
        sorted_at = sb("sorted_at", [B, 8])
        chosen8 = sb("chosen8", [B, NA_B], I32)
        chosen = sb("chosen", [1, B * NA_B], I32)
        head_tab = sb("head_tab", [P, NH_B, ROW_B])
        taken[0] = 0
        head_w = carve([P, 2, NA_B, BIAS_B + 2])
        wo_b = sb("wo_b", [P, NA_B * DH // P, D])
        bo_b = sb("bo_b", [P, D])
        q_high = carve([P, NA_B, S], F16)
        q_low = carve([P, NA_B, S], F16)
        k_both = carve([P, NA_B, S], F16)
        v_b = carve([P, NT, NA_B * DH])
        negmax_b = sb("negmax_b", [P, NA_B, NT])
        rowsum_b = sb("rowsum_b", [P, NT, NA_B])
        recip_b = sb("recip_b", [P, NT * NA_B])
        o_b = carve([P, NT, NA_B * DH])
        oT_b = carve([P, ND, S])

        w_c = sb("w_c", [P, 3, ND, D])
        dense_c = sb("dense_c", [P, ND, D])
        norm_rows = sb("norm_rows", [P, 3, D])
        gated_rows = sb("gated_rows", [P, 2, D])
        norm_cols = sb("norm_cols", [P, 2, ND])
        em = sb("em", [P, B * NT])
        eps6 = sb("eps6", [P, 16])
        minus1 = sb("minus1", [P, 16])
        taken[0] = 0
        ctx_b = carve([P, 2, NT, D])
        ctxT = carve([P, ND, S])
        stat_c = sb("stat_c", [P, 6, 6])
        mv_c = sb("mv_c", [P, 6, 2])
        rstd_c = sb("rstd_c", [P, 2, 6])
        qn_c = carve([P, NT, D])
        kv_c = carve([P, NT, 2, D])
        kp_c = carve([P, NT, D])
        v_ones = sb("v_ones", [P, NT, ND, P + 1])
        qpT_c = carve([P, ND, S])
        head_block = sb("head_block", [P, P])
        head_cols = sb("head_cols", [P, HP_C])
        parity = sb("parity", [P, 2])
        kv_own = carve([P, ND, P])
        k_own = carve([P, ND, P])
        turned_c = carve([P, 2, ND * DC, 2 * DC])
        den_c = carve([P, 2, ND * DC])
        att_c = carve([P, NT, D])
        attT_c = carve([P, ND, S])
        y_c = carve([P, NT, D])
        stat_y = sb("stat_y", [P, NT, 6])
        mv_y = sb("mv_y", [P, NT, 2])
        rstd_y = sb("rstd_y", [P, 2, NT])

        w_gate = sb("w_gate", [P, ND, E])
        w_exp = head_tab[:, :, :].rearrange("p h r -> p (h r)")[:, 0:E * ND * D]\
            .rearrange("p (e t n) -> p e t n", e=E, t=ND)
        ones = sb("ones", [P, P])
        ones16 = sb("ones16", [B * E, P], F16)
        gate_e = sb("gate_e", [P, NT, B, E])
        recip_col = sb("recip_col", [P, B, E])
        sum_row = sb("sum_row", [P, 2, B * NT])
        gateT = sb("gateT", [B * E, S])
        picked = sb("picked", [B * E, M])
        picked_at = sb("picked_at", [B * E, M], U32)
        pick_rows = sb("pick_rows", [B * E, 2, M])
        spread16 = scores[0:B * E, :, :].rearrange("p a b -> p (a b)").bitcast(F16)\
            .rearrange("p (r m) -> p r m", m=M)
        slot_cols = sb("slot_cols", [P, 2, B * E * M // P])
        token_col = sb("token_col", [P, NT])
        token_row = sb("token_row", [P, S])
        slot_key = sb("slot_key", [P, E, M])
        keyed = sb("keyed", [P, 2, S])
        winner = sb("winner", [P, 2])
        taken[0] = 0
        take = carve([P, B, NT, S])
        put = carve([P, B, 2, S])
        xgT = carve([P, ND, E, B, M])
        yT = carve([P, ND, B, E, M])
        y_e = probs[:, :, :].rearrange("p s (a n) -> p s a n", n=D)
        x_in = [sem(f"x_in{i}") for i in range(4)]
        c_in = [sem(f"c_in{i}") for i in range(4)]
        w_in = sem("w_in"); w2_in = sem("w2_in"); small_in = sem("small_in")
        out_done = sem("out_done")
        ident_ready = sem("ident_ready"); pool_steps = sem("pool_steps"); dve_steps = sem("dve_steps")
        gates_ready = sem("gates_ready"); scaled = sem("scaled"); held = sem("held"); held_pool = sem("held_pool")
        a_var = sem("a_var"); a_rstd = sem("a_rstd"); a_xn = sem("a_xn"); a_xT_ps = sem("a_xT_ps"); a_xT = sem("a_xT")
        a_kq_ps = sem("a_kq_ps"); a_sq = sem("a_sq"); a_ss = sem("a_ss"); a_rn = sem("a_rn"); a_kn = sem("a_kn")
        a_hi = sem("a_hi"); a_lo = sem("a_lo"); a_kqT_ps = sem("a_kqT_ps"); a_kqT = sem("a_kqT")
        a_v_ps = sem("a_v_ps"); a_v = sem("a_v")
        a_s_ps = sem("a_s_ps"); a_max = sem("a_max"); a_ex = sem("a_ex"); a_pT_ps = sem("a_pT_ps")
        a_pT = [sem("a_pT_dve"), sem("a_pT_act")]; a_pv = sem("a_pv")
        a_on = sem("a_on"); a_oT_ps = sem("a_oT_ps"); a_oT = sem("a_oT"); a_wo_ps = sem("a_wo_ps")
        a_ovar = sem("a_ovar"); a_orstd = sem("a_orstd"); a_y = sem("a_y"); a_x = sem("a_x")

        b_in = sem("b_in"); c_w_in = sem("c_w_in"); e_in = sem("e_in")
        n_var = sem("n_var"); n_rstd = sem("n_rstd"); n_h = sem("n_h"); n_ps = sem("n_ps"); n_hT = sem("n_hT")
        r_ps = sem("r_ps"); r_chosen = sem("r_chosen"); r_sent = sem("r_sent")
        b_scaled = sem("b_scaled"); b_bias = sem("b_bias"); b_sel = sem("b_sel"); b_qk_ps = sem("b_qk_ps")
        b_v_ps = sem("b_v_ps"); b_hi = sem("b_hi"); b_lo = sem("b_lo"); b_v = sem("b_v"); b_s_ps = sem("b_s_ps")
        b_max = sem("b_max"); b_ex = sem("b_ex"); b_pT_ps = sem("b_pT_ps"); b_pv = sem("b_pv")
        b_pT = [sem("b_pT_dve"), sem("b_pT_act")]
        b_on = sem("b_on"); b_oT_ps = sem("b_oT_ps"); b_oT = sem("b_oT"); b_wo_ps = sem("b_wo_ps"); b_x = sem("b_x")
        c_cur = sem("c_cur"); c_cT_ps = sem("c_cT_ps"); c_cT = sem("c_cT"); c_q_ps = sem("c_q_ps")
        c_kv_ps = sem("c_kv_ps"); c_var = sem("c_var"); c_rstd = sem("c_rstd"); c_qn = sem("c_qn")
        c_kvn = sem("c_kvn"); c_kvg = sem("c_kvg"); c_kvb = sem("c_kvb"); c_kp = sem("c_kp"); c_qT_ps = sem("c_qT_ps")
        c_relu = sem("c_relu"); c_qp = sem("c_qp"); c_sum_ps = sem("c_sum_ps"); c_kvm = sem("c_kvm")
        c_num_ps = sem("c_num_ps"); c_att = sem("c_att"); c_aT_ps = sem("c_aT_ps"); c_aT = sem("c_aT")
        c_y_ps = sem("c_y_ps"); c_yvar = sem("c_yvar"); c_yrstd = sem("c_yrstd"); c_yg = sem("c_yg"); c_x = sem("c_x")
        e_logit_ps = sem("e_logit_ps"); e_gate = sem("e_gate"); e_col_ps = sem("e_col_ps"); e_gT_ps = sem("e_gT_ps")
        e_picks = sem("e_picks"); e_rows_ps = sem("e_rows_ps"); e_cols_ps = sem("e_cols_ps"); e_take = sem("e_take")
        e_put = sem("e_put"); e_xg_ps = sem("e_xg_ps"); e_xg = sem("e_xg"); e_yT_ps = sem("e_yT_ps")
        e_yT = [sem("e_yT_dve"), sem("e_yT_act")]
        e_y_ps = sem("e_y_ps"); e_y = sem("e_y"); e_o_ps = sem("e_o_ps"); e_x = sem("e_x")
        consts = sem("consts")

        N16 = B * NT

        def pool_late(pool, ch):
            def token_rstd(n, wait_for):
                pool.wait_ge(n_var, n + 1)
                ch.step(pool_.tensor_tensor(rstd_n[:, 0, :], mv_n[:, :, 1], eps5[:, :], ALU.add))
                ch.wait()
                pool_.tensor_tensor(rstd_n[:, 1, :], rstd_n[:, 0, :], half[:, :], ALU.pow).then_inc(n_rstd, 1)

            token_rstd(0, a_x)
            pool.wait_ge(b_in, 16 * 7)
            pool.wait_ge(gates_ready, 1)
            ch.step(pool_.tensor_scalar(bo_b[:, :], bo_b[:, :], gates[:, 2:3], 1.0, ALU.mult, ALU.mult))
            ch.wait()
            pool.wait_ge(n_h, N16)
            with pool.Fori(0, N16) as i:
                xt = x_all[:, i, :]
                pool_.tensor_tensor(xt, xt, bo_b[:, :], ALU.add).then_inc(b_bias, 1)

            pool.wait_ge(r_sent, 16)
            pool.wait_ge(b_scaled, 1)
            pool.wait_ge(n_hT, N16)

            def choose(b, par):
                need(pool, b_v_ps, b - 1)
                need(pool, b_qk_ps, NA_B * (b - 1))
                need(pool, b_on, b - 1)
                for j in range(NA_B):
                    at = pool.value_load(chosen[0:1, bass.ds(NA_B * b + j, 1)], min_val=0, max_val=NH_B - 1)
                    twice = head_w[:, par, j, 0:8 * DH].rearrange("p (g r d) -> p g r d", r=2, d=DH)
                    row = head_tab[:, bass.ds(at, 1), :]
                    once = row[:, 0, 0:4 * DH].rearrange("p (g d) -> p g d", d=DH)
                    for r in range(2):
                        pool_.tensor_copy(twice[:, :, r, :], once)
                    pool_.tensor_copy(head_w[:, par, j, 8 * DH:].unsqueeze(1), row[:, :, 4 * DH:])
                pool_.tensor_copy(hT[:, par, :, :].unsqueeze(1), hT_all[:, bass.ds(b, 1), :, :]).then_inc(b_sel, 1)

            for b in range(2):
                choose(b, b)
            with pool.Fori(1, B // 2) as i:
                for par in range(2):
                    choose(2 * i + par, par)
            if stages < 3:
                return

            token_rstd(1, b_x)
            pool.wait_ge(gates_ready, 1)
            pool.wait_ge(c_w_in, 16 * 9)
            for r in range(2):
                ch.step(pool_.tensor_scalar(gated_rows[:, r, :], norm_rows[:, r, :], gates[:, 1:2], 1.0, ALU.mult,
                                            ALU.mult))
            ch.wait()
            pool.wait_ge(n_hT, 2 * N16)

            def current(b, par):
                need(pool, c_q_ps, b - 1)
                need(pool, c_cT_ps, b - 1)
                pool_.tensor_copy(hT[:, par, :, :].unsqueeze(1), hT_all[:, bass.ds(b, 1), :, :])
                pool_.tensor_copy(ctx_b[:, par, :, :], c_all[:, bass.ds(NT * b, NT), :]).then_inc(c_cur, 1)

            def rstd(b):
                need(pool, c_var, b + 1)
                ch.step(pool_.tensor_tensor(rstd_c[:, 1, :], mv_c[:, :, 1], eps6[:, 0:6], ALU.add))
                ch.wait()
                ch.step(pool_.tensor_tensor(rstd_c[:, 0, :], rstd_c[:, 1, :], half[:, 0:6], ALU.pow))
                ch.wait()
                ch.step(pool_.tensor_tensor(rstd_c[:, 1, :], rstd_c[:, 0, :], mv_c[:, :, 0], ALU.mult))
                ch.wait()
                pool_.tensor_tensor(rstd_c[:, 1, :], rstd_c[:, 1, :], minus1[:, 0:6], ALU.mult).then_inc(c_rstd, 1)

            def add_beta(b):
                need(pool, c_kvg, b + 1)
                rows4 = norm_rows[:, 1:2, :].broadcast_to([P, 2 * NT, D])
                kv4 = kv_c[:, :, :, :].rearrange("p t w d -> p (t w) d")
                pool_.tensor_tensor(kv4, kv4, rows4, ALU.add).then_inc(c_kvb, 1)

            def out_rstd(b):
                need(pool, c_yvar, b + 1)
                ch.step(pool_.tensor_tensor(rstd_y[:, 0, :], mv_y[:, :, 1], eps6[:, 0:NT], ALU.add))
                ch.wait()
                pool_.tensor_tensor(rstd_y[:, 1, :], rstd_y[:, 0, :], half[:, 0:NT], ALU.pow).then_inc(c_yrstd, 1)

            def residual(b):
                need(pool, c_yg, b + 1)
                ch.step(pool_.tensor_tensor(y_c[:, :, :], y_c[:, :, :],
                                            gated_rows[:, 1:2, :].broadcast_to([P, NT, D]), ALU.add))
                ch.wait()
                pool.sem_inc(held_pool, 1)
                xt = x_all[:, bass.ds(NT * b, NT), :]
                pool_.tensor_tensor(xt, xt, y_c[:, :, :], ALU.add).then_inc(c_x, 1)

            def turn(i, par, first=True, second=True, third=True):
                if first:
                    current(i + 2, par)
                if second:
                    add_beta(i + 1)
                if first:
                    rstd(i + 2)
                if third:
                    out_rstd(i)
                    residual(i)

            turn(-2, 0, second=False, third=False)
            turn(-1, 1, third=False)
            turn(0, 0)
            turn(1, 1)
            fore, per = ch.n, 5
            with pool.Fori(1, B // 2 - 1) as i:
                for par in range(2):
                    ch.base, ch.n = fore + per * (2 * i + par - 2), 0
                    turn(2 * i + par, par)
                    assert ch.n == per
            ch.leave(fore + per * (B - 4))
            turn(B - 2, 0, first=False)
            turn(B - 1, 1, first=False, second=False)
            if stages < 4:
                return
            token_rstd(2, c_x)

        def dve_late(dve, ch):
            def hold(semaphore, value):
                dve.wait_ge(semaphore, value)
                if not isinstance(value, int):
                    dve.sem_inc(held, 1)

            def norm_tokens(n, last_x):
                dve.wait_ge(*last_x)
                start = ch.n
                with dve.Fori(0, N16) as i:
                    dve_.bn_stats(stat_n[:, i, :], x_all[:, i, :]).then_inc(dve_steps, 1)
                ch.n = start + N16
                ch.wait()
                for i in range(N16):
                    last = dve_.bn_aggr(mv_n[:, i, :], stat_n[:, i, :])
                last.then_inc(n_var, 1)
                dve.wait_ge(n_rstd, n + 1)
                with dve.Fori(0, N16) as i:
                    dve_.tensor_scalar(h_all[:, i, :], x_all[:, i, :], mv_n[:, i, 0:1], rstd_n[:, 1, bass.ds(i, 1)],
                                       ALU.subtract, ALU.mult).then_inc(n_h, 1)


            norm_tokens(0, (a_x, N16))
            dve.wait_ge(b_in, 16 * 7)
            ch.step(dve_.tensor_scalar(head_tab[:, :, 0:2 * DH], head_tab[:, :, 0:2 * DH], DH ** -0.5, None, ALU.mult))
            dve_.tensor_scalar(head_tab[:, :, 7 * DH:7 * DH + 1], head_tab[:, :, 7 * DH:7 * DH + 1], DH ** -0.5, None,
                               ALU.mult).then_inc(b_scaled, 1)
            ch.step(dve_.memset(neg_at[:, :], -1e6))
            dve.wait_ge(r_ps, 1)
            ch.step(dve_.scalar_tensor_tensor(logits[:, :], banks[0][0:B, 0:NH_B], 1.0 / S, b_router[:, :], ALU.mult,
                                              ALU.add))
            ch.wait()
            ch.step(dve_.max(top[:, :], logits[:, :]))
            ch.wait()
            ch.step(dve_.max_index(top_at[:, :], top[:, :], logits[:, :]))
            ch.wait()
            ch.step(dve_.tensor_scalar(neg_at[:, 0:NA_B], top_at[:, 0:NA_B], -1.0, None, ALU.mult))
            ch.wait()
            ch.step(dve_.max(sorted_at[:, :], neg_at[:, :]))
            ch.wait()
            dve_.tensor_scalar(chosen8[:, :], sorted_at[:, 0:NA_B], -1.0, None, ALU.mult).then_inc(r_chosen, 1)

            dve.wait_ge(b_bias, N16)
            start = ch.n

            def attend(b, par):
                def low(j):
                    need(dve, b_hi, NA_B * b + j + 1)
                    w, bank = head_w[:, par, j, :], banks[j % 2]
                    dve_.scalar_tensor_tensor(q_low[:, j, :], bank[:, 0:S], w[:, BIAS_B:BIAS_B + 1], q_high[:, j, :],
                                              ALU.add, ALU.subtract)
                    kl = k_both[DH:P, j, :]
                    dve_.scalar_tensor_tensor(kl, bank[DH:P, S:2 * S], w[DH:P, BIAS_B + 1:BIAS_B + 2], kl,
                                              ALU.add, ALU.subtract).then_inc(b_lo, 1)

                def maximum(j):
                    need(dve, b_s_ps, NA_B * b + j + 1)
                    dve_.tensor_reduce(negmax_b[:, j, :], banks[2 + j % 2][:, :].rearrange("p (t n) -> p t n", n=S),
                                       AX, ALU.max, negate=True).then_inc(b_max, 1)

                def copy_pT(j):
                    need(dve, b_pT_ps, NA_B * b + j + 1)
                    need(dve, b_pv, NA_B * b + j - 1)
                    dve_.tensor_copy(probsT[:, j % 2, :], banks[4 + j % 2][:, :]).then_inc(b_pT[0], 1)

                low(0)
                low(1)
                maximum(0)
                low(2)
                maximum(1)
                low(3)
                copy_pT(0)
                maximum(2)
                maximum(3)
                copy_pT(2)
                need(dve, b_pv, NA_B * b + NA_B)
                ch.step(dve_.reciprocal(recip_b[:, :], rowsum_b[:, :, :].rearrange("p t h -> p (t h)")))
                ch.wait()
                need(dve, b_oT_ps, b)
                ch.step(dve_.tensor_tensor(heads(o_b[:, :, :].rearrange("p t n -> p (t n)")), heads(banks[7][:, :]),
                                           across(recip_b[:, :], DH), ALU.mult))
                ch.wait()
                for t in range(NT):
                    o = heads(o_b[:, t, :])
                    last = dve_.tensor_tensor(o, o, head_w[:, par, :, 10 * DH:11 * DH], ALU.add)
                last.then_inc(b_on, 1)
                need(dve, b_wo_ps, b + 1)
                xt = x_all[:, bass.ds(NT * b, NT), :]
                dve_.scalar_tensor_tensor(xt, banks[7][:, :].rearrange("p (t n) -> p t n", n=D), gates[:, 2:3], xt,
                                          ALU.mult, ALU.add).then_inc(b_x, 1)

            for b in range(2):
                attend(b, b)
            per = (ch.n - start) // 2
            with dve.Fori(1, B // 2) as i:
                for par in range(2):
                    ch.base, ch.n = start + per * (2 * i + par), 0
                    attend(2 * i + par, par)
            ch.leave(start + per * B)
            if stages < 3:
                return

            norm_tokens(1, (b_x, B))
            dve.wait_ge(consts, 1)
            ch.step(dve_.tensor_reduce(parity[:, :], head_cols[:, :].rearrange("p (h a) -> p a h", a=2), AX, ALU.add))
            dve.wait_ge(c_w_in, 16 * 9)

            def stats(b):
                need(dve, c_q_ps, b + 1)
                for t in range(NT):
                    ch.step(dve_.bn_stats(stat_c[:, t, :], banks[1][:, D * t:D * t + D]))
                need(dve, c_kv_ps, b + 1)
                for t in range(NT):
                    for w in range(2):
                        ch.step(dve_.bn_stats(stat_c[:, 2 + 2 * t + w, :], banks[2 + t][:, D * w:D * w + D]))
                hold(dve_steps, ch.base + ch.n)
                if not isinstance(b, int) or b:
                    hold(c_kvn, b)
                for i in range(6):
                    last = dve_.bn_aggr(mv_c[:, i, :], stat_c[:, i, :])
                last.then_inc(c_var, 1)

            def norm_q(b):
                need(dve, c_rstd, b + 1)
                need(dve, c_qT_ps, b)
                for t in range(NT):
                    last = dve_.tensor_scalar(qn_c[:, t, :], banks[1][:, D * t:D * t + D], mv_c[:, t, 0:1],
                                              rstd_c[:, 0, t:t + 1], ALU.subtract, ALU.mult)
                last.then_inc(c_qn, 1)

            def times_gamma(b):
                need(dve, c_kvn, b + 1)
                kv4 = kv_c[:, :, :, :].rearrange("p t w d -> p (t w) d")
                dve_.tensor_tensor(kv4, kv4, norm_rows[:, 0:1, :].broadcast_to([P, 2 * NT, D]), ALU.mult)\
                    .then_inc(c_kvg, 1)

            def queries(b):
                need(dve, c_relu, b + 1)
                dve_.tensor_scalar(qpT_c[:, :, :], qpT_c[:, :, :], 1e-6, None, ALU.add).then_inc(c_qp, 1)

            def keys_values(b):
                need(dve, c_kvb, b + 1)
                need(dve, c_sum_ps, b)
                ch.step(dve_.tensor_scalar(kp_c[:, :, :], kv_c[:, :, 0, :], 0.0, 1e-6, ALU.max, ALU.add))
                ch.wait()
                for t in range(NT):
                    mt = em[:, bass.ds(NT * b + t, 1)]
                    dve_.tensor_scalar(kp_c[:, t, :], kp_c[:, t, :], mt, None, ALU.mult)
                    last = dve_.tensor_scalar(v_ones[:, t, :, 0:P],
                                              kv_c[:, t, 1, :].rearrange("p (a n) -> p a n", n=P), mt, None, ALU.mult)
                last.then_inc(c_kp, 1)

            def own_sums(b):
                need(dve, c_sum_ps, b + 1)
                need(dve, c_num_ps, b)
                for dt in range(ND):
                    at = S * dt + P
                    dve_.tensor_tensor(kv_own[:, dt, :], banks[5][:, S * dt:at], head_block[:, :], ALU.mult)
                    last = dve_.tensor_tensor(k_own[:, dt, :], banks[5][:, at:at + 1].broadcast_to([P, P]),
                                              head_block[:, :], ALU.mult)
                last.then_inc(c_kvm, 1)

            def divide(b):
                need(dve, c_num_ps, b + 1)
                for i, bank in enumerate((7, 6)):
                    for dt in range(ND):
                        runs = banks[bank][:, S * dt:S * dt + S].rearrange("p (r n) -> p n r", n=DC).unsqueeze(2)
                        to = turned_c[:, i, DC * dt:DC * dt + DC, :].rearrange("p n (a r) -> p n a r", a=2)
                        ch.step(dve_.transpose(to, runs.broadcast_to([P, DC, 2, DC])))
                        if i and dt == 0:
                            ch.step(dve_.tensor_scalar(den_c[:, 0, :], turned_c[:, 0, :, 0], parity[:, 0:1], 1e-6,
                                                       ALU.mult, ALU.add))
                    ch.wait()
                ch.step(dve_.scalar_tensor_tensor(den_c[:, 0, :], turned_c[:, 0, :, DC], parity[:, 1:2],
                                                  den_c[:, 0, :], ALU.mult, ALU.add))
                need(dve, c_aT_ps, b)
                att = att_c[:, :, :].rearrange("p k (n e) -> p (k n) e", e=DC)
                turned = turned_c[:, 1, :, :]
                ch.step(dve_.tensor_scalar(att, turned[:, :, 0:DC], parity[:, 0:1], None, ALU.mult))
                ch.wait()
                ch.step(dve_.reciprocal(den_c[:, 1, :], den_c[:, 0, :]))
                ch.step(dve_.scalar_tensor_tensor(att, turned[:, :, DC:], parity[:, 1:2], att, ALU.mult, ALU.add))
                ch.wait()
                dve_.tensor_tensor(att, att, across(den_c[:, 1, :], DC), ALU.mult).then_inc(c_att, 1)

            def out_stats(b):
                need(dve, c_y_ps, b + 1)
                need(dve, c_x, b)
                ch.step(dve_.tensor_tensor(y_c[:, :, :], banks[5][:, :].rearrange("p (t n) -> p t n", n=D),
                                           norm_rows[:, 2:3, :].broadcast_to([P, NT, D]), ALU.add))
                ch.wait()
                for t in range(NT):
                    ch.step(dve_.bn_stats(stat_y[:, t, :], y_c[:, t, :]))
                hold(dve_steps, ch.base + ch.n)
                for t in range(NT):
                    last = dve_.bn_aggr(mv_y[:, t, :], stat_y[:, t, :])
                last.then_inc(c_yvar, 1)

            def out_norm(b):
                need(dve, c_yrstd, b + 1)
                for t in range(NT):
                    ch.step(dve_.tensor_scalar(y_c[:, t, :], y_c[:, t, :], mv_y[:, t, 0:1], rstd_y[:, 1, t:t + 1],
                                               ALU.subtract, ALU.mult))
                ch.wait()
                dve_.tensor_tensor(y_c[:, :, :], y_c[:, :, :], gated_rows[:, 0:1, :].broadcast_to([P, NT, D]),
                                   ALU.mult).then_inc(c_yg, 1)

            def turn(i, first=True, second=True, third=True):
                if second:
                    norm_q(i + 1)
                if second:
                    times_gamma(i + 1)
                if third:
                    divide(i)
                if first:
                    stats(i + 2)
                if second:
                    queries(i + 1)
                if third:
                    out_stats(i)
                if second:
                    keys_values(i + 1)
                if third:
                    out_norm(i)
                if second:
                    own_sums(i + 1)

            turn(-2, second=False, third=False)
            turn(-1, third=False)
            turn(0)
            fore, per = ch.n, 21
            with dve.Fori(1, B - 2) as i:
                ch.base, ch.n = fore + per * (i - 1), 0
                turn(i)
                assert ch.n == per, ch.n
            ch.leave(fore + per * (B - 3))
            turn(B - 2, first=False)
            turn(B - 1, first=False, second=False)
            if stages < 4:
                return

            norm_tokens(2, (c_x, B))
            dve.wait_ge(e_logit_ps, 1)
            flat = gate_e[:, :, :, :].rearrange("p t b e -> p (t b) e")
            dve_.tensor_scalar(gate_e[:, :, :, :].rearrange("p t b e -> p (t b e)"), banks[0][:, 0:N16 * E], 1e-6, None,
                               ALU.max).then_inc(e_gate, 1)
            start = ch.n

            def sinkhorn(i):
                need(dve, e_col_ps, i + 1)
                ch.step(dve_.reciprocal(recip_col[:, :, :], banks[1][:, 0:B * E].rearrange("p (b e) -> p b e", e=E)))
                ch.wait()
                for t in range(NT):
                    ch.step(dve_.tensor_tensor(gate_e[:, t, :, :], gate_e[:, t, :, :], recip_col[:, :, :], ALU.mult))
                ch.wait()
                ch.step(dve_.tensor_reduce(sum_row[:, 0, :], flat, AX, ALU.add))
                ch.wait()
                ch.step(dve_.reciprocal(sum_row[:, 1, :], sum_row[:, 0, :]))
                ch.wait()
                dve_.tensor_tensor(flat, flat, across(sum_row[:, 1, :], E), ALU.mult).then_inc(e_gate, 1)

            sinkhorn(0)
            per = ch.n - start
            with dve.Fori(1, SINKHORN) as i:
                ch.base, ch.n = start + per * i, 0
                sinkhorn(i)
            ch.leave(start + per * SINKHORN)

            dve.wait_ge(e_gT_ps, 1)
            ch.step(dve_.tensor_copy(gateT[:, :], banks[2][0:B * E, 0:S]))
            ch.wait()
            for r in range(M // 8):
                cut = slice(8 * r, 8 * r + 8)
                ch.step(dve_.max(picked[:, cut], gateT[:, :]))
                ch.wait()
                ch.step(dve_.max_index(picked_at[:, cut], picked[:, cut], gateT[:, :]))
                ch.wait()
                if r < M // 8 - 1:
                    ch.step(dve_.match_replace(gateT[:, :], picked[:, cut], gateT[:, :], -1.0))
                    ch.wait()
            ch.step(dve_.tensor_copy(pick_rows[:, 0, :], picked_at[:, :]))
            ch.step(dve_.tensor_copy(pick_rows[:, 1, :], picked[:, :]))
            ch.wait()
            dve_.tensor_tensor(spread16[:, :, :], pick_rows[:, 0:1, :].broadcast_to([B * E, B * E, M]),
                               ident[0:B * E, 0:B * E].unsqueeze(2).broadcast_to([B * E, B * E, M]), ALU.mult)\
                .then_inc(e_picks, 1)
            dve.wait_ge(e_cols_ps, 1)
            turned = banks[3][0:M, 0:2 * B * E].rearrange("m (w g j) -> m w g j", w=2, j=4)
            for j in range(4):
                last = dve_.tensor_copy(slot_cols[M * j:M * j + M, :, :], turned[:, :, :, j])
            ch.step(last)
            dve.wait_ge(e_rows_ps, 1)
            for b in range(B):
                for t in range(NT):
                    slots = banks[4 + b // 2][:, S * (b % 2):S * (b % 2) + S]
                    kd, win = keyed[:, t, :], winner[:, t:t + 1]
                    ch.step(dve_.scalar_tensor_tensor(kd, slots, token_col[:, t:t + 1],
                                                      slot_key[:, :, :].rearrange("p e m -> p (e m)"), ALU.is_equal,
                                                      ALU.mult))
                    ch.wait()
                    ch.step(dve_.tensor_reduce(win, kd, AX, ALU.max))
                    ch.wait()
                    ch.step(dve_.tensor_scalar(win, win, 0.5, None, ALU.max))
                    ch.wait()
                    dve_.tensor_scalar(take[:, b, t, :], kd, win, None, ALU.is_equal).then_inc(e_take, 1)
                for half_e in range(2):
                    g = 2 * b + half_e
                    dve_.tensor_scalar(put[:, b, half_e, :], token_row[:, :], slot_cols[:, 0, g:g + 1], None,
                                       ALU.is_equal).then_inc(e_put, 1)
            for e in range(0, E, 2):
                dve.wait_ge(e_yT_ps, e + 1)
                dve_.tensor_copy(yT[:, :, :, e, :], banks[4 + e % 4][:, :].rearrange("p (a b m) -> p a b m", a=ND, m=M))\
                    .then_inc(e_yT[0], 1)
            for b in range(B):
                dve.wait_ge(e_o_ps, b + 1)
                xt = x_all[:, NT * b:NT * b + NT, :]
                dve_.scalar_tensor_tensor(xt, banks[2 + b % 2][:, :].rearrange("p (t n) -> p t n", n=D), gates[:, 3:4],
                                          xt, ALU.mult, ALU.add).then_inc(e_x, 1)

        def act_late(act):
            def copy_hT(n, sums):
                for b in range(B):
                    act.wait_ge(n_ps, B * n + b + 1)
                    for dt in range(ND):
                        extra = dict(accum_out=h_sum[:, dt, b:b + 1]) if sums else {}
                        act_.activation(hT_all[:, b, dt, :], banks[b][:, S * dt:S * dt + S], ACT.Copy, **extra)\
                            .then_inc(n_hT, 1)

            copy_hT(0, True)

            def attend(b, par):
                def high(j):
                    need(act, b_qk_ps, NA_B * b + j + 1)
                    w, bank = head_w[:, par, j, :], banks[j % 2]
                    act_.activation(q_high[:, j, :], bank[:, 0:S], ACT.Identity, bias=w[:, BIAS_B:BIAS_B + 1])
                    act_.activation(k_both[:, j, :], bank[:, S:2 * S], ACT.Identity,
                                    bias=w[:, BIAS_B + 1:BIAS_B + 2]).then_inc(b_hi, 1)

                def exps(j):
                    need(act, b_max, NA_B * b + j + 1)
                    need(act, b_pT_ps, NA_B * b + j - 1)
                    for t in range(NT):
                        last = act_.activation(probs[:, j % 2, S * t:S * t + S], banks[2 + j % 2][:, S * t:S * t + S],
                                               ACT.Exp, bias=negmax_b[:, j, t:t + 1], scale=1.0,
                                               accum_out=rowsum_b[:, t, j:j + 1])
                    last.then_inc(b_ex, 1)

                def copy_pT(j):
                    need(act, b_pT_ps, NA_B * b + j + 1)
                    need(act, b_pv, NA_B * b + j - 1)
                    act_.activation(probsT[:, j % 2, :], banks[4 + j % 2][:, :], ACT.Copy).then_inc(b_pT[1], 1)

                high(0)
                high(1)
                need(act, b_v_ps, b + 1)
                act_.activation(v_b[:, :, :], banks[6][:, :].rearrange("p (t n) -> p t n", t=NT), ACT.Copy)\
                    .then_inc(b_v, 1)
                high(2)
                exps(0)
                high(3)
                exps(1)
                exps(2)
                copy_pT(1)
                exps(3)
                copy_pT(3)
                need(act, b_oT_ps, b + 1)
                act_.activation(oT_b[:, :, :], banks[6][:, :].rearrange("p (k n) -> p k n", n=S), ACT.Copy)\
                    .then_inc(b_oT, 1)

            for b in range(2):
                attend(b, b)
            with act.Fori(1, B // 2) as i:
                for par in range(2):
                    attend(2 * i + par, par)
            if stages < 3:
                return

            copy_hT(1, False)

            def copy_ctxT(b):
                need(act, c_cT_ps, b + 1)
                act_.activation(ctxT[:, :, :], banks[0][:, :].rearrange("p (k n) -> p k n", n=S), ACT.Copy)\
                    .then_inc(c_cT, 1)

            def norm_kv(b):
                need(act, c_rstd, b + 1)
                need(act, c_kp, b)
                for t in range(NT):
                    for w in range(2):
                        i = 2 + 2 * t + w
                        last = act_.activation(kv_c[:, t, w, :], banks[2 + t][:, D * w:D * w + D], ACT.Identity,
                                               bias=rstd_c[:, 1, i:i + 1], scale=rstd_c[:, 0, i:i + 1])
                last.then_inc(c_kvn, 1)

            def relu(b):
                need(act, c_qT_ps, b + 1)
                need(act, c_num_ps, b)
                for dt in range(ND):
                    last = act_.activation(qpT_c[:, dt, :], banks[4][:, S * dt:S * dt + S], ACT.Relu,
                                           bias=norm_cols[:, 1, dt:dt + 1], scale=norm_cols[:, 0, dt:dt + 1])
                last.then_inc(c_relu, 1)

            def copy_attT(b):
                need(act, c_aT_ps, b + 1)
                act_.activation(attT_c[:, :, :], banks[5][:, :].rearrange("p (k n) -> p k n", n=S), ACT.Copy)\
                    .then_inc(c_aT, 1)

            def turn(i, first=True, second=True, third=True):
                if second:
                    norm_kv(i + 1)
                    relu(i + 1)
                if first:
                    copy_ctxT(i + 2)
                if third:
                    copy_attT(i)

            act.wait_ge(c_w_in, 16 * 9)
            turn(-2, second=False, third=False)
            turn(-1, third=False)
            turn(0)
            with act.Fori(1, B - 2) as i:
                turn(i)
            turn(B - 2, first=False)
            turn(B - 1, first=False, second=False)
            if stages < 4:
                return

            copy_hT(2, False)
            for b in range(B):
                act.wait_ge(e_xg_ps, b + 1)
                act_.activation(xgT[:, :, :, b, :], banks[b % 2][:, :].rearrange("p (a e m) -> p a e m", a=ND, m=M),
                                ACT.Copy).then_inc(e_xg, 1)
            for e in range(1, E, 2):
                act.wait_ge(e_yT_ps, e + 1)
                act_.activation(yT[:, :, :, e, :], banks[4 + e % 4][:, :].rearrange("p (a b m) -> p a b m", a=ND, m=M),
                                ACT.Copy).then_inc(e_yT[1], 1)
            for b in range(B):
                act.wait_ge(e_y_ps, b + 1)
                if b >= 2:
                    act.wait_ge(e_o_ps, b - 1)
                for half_e in range(2):
                    g = 2 * b + half_e
                    last = act_.activation(y_e[:, b % 2, half_e, :], banks[b % 2][:, D * half_e:D * half_e + D],
                                           ACT.Copy, scale=slot_cols[:, 1, g:g + 1])
                last.then_inc(e_y, 1)

        def pe_late(pe):
            def transposes_h(n, waits):
                for semaphore, value in waits:
                    pe.wait_ge(semaphore, value)
                for b in range(B):
                    pe.wait_ge(n_h, N16 * n + NT * b + NT)
                    for dt in range(ND):
                        for t in range(NT):
                            last = pe_.transpose(banks[b][:, S * dt + P * t:S * dt + P * t + P],
                                                 h_all[:, NT * b + t, P * dt:P * dt + P], ident[:, :])
                    last.then_inc(n_ps, 1)

            transposes_h(0, [])
            pe.wait_ge(n_hT, N16)
            pe.wait_ge(b_in, 16 * 7)
            for k in range(ND):
                last = pe_.matmul(banks[0][0:B, 0:NH_B], h_sum[:, k, :], w_router[:, k, :], start=k == 0,
                                  stop=k == ND - 1)
            last.then_inc(r_ps, 1)
            pe.wait_ge(r_chosen, 1)

            def attend(b, par):
                hb = hT[:, par, :, :]

                def project_qk(j):
                    if j == 0:
                        need(pe, b_sel, b + 1)
                    need(pe, b_lo, NA_B * b + j - 1)
                    for w in range(2):
                        for k in range(ND):
                            at = P * (ND * w + k)
                            twice = head_w[:, par, j, at:at + P]
                            last = pe_.matmul(banks[j % 2][:, S * w:S * w + S], twice, hb[:, k, :], start=k == 0,
                                              stop=k == ND - 1)
                    last.then_inc(b_qk_ps, 1)

                def scores_of(j):
                    need(pe, b_lo, NA_B * b + j + 1)
                    need(pe, b_ex, NA_B * b + j - 1)
                    for t in range(NT):
                        for v, q in enumerate((q_high, q_low)):
                            last = pe_.matmul(banks[2 + j % 2][:, S * t:S * t + S], q[:, j, P * t:P * t + P],
                                              k_both[:, j, :], start=v == 0, stop=v == 1)
                    last.then_inc(b_s_ps, 1)

                def transposes_p(j):
                    need(pe, b_ex, NA_B * b + j + 1)
                    need(pe, b_pT[j % 2], NA_B // 2 * b + j // 2)
                    for t in range(NT):
                        for k in range(NT):
                            last = pe_.transpose(banks[4 + j % 2][:, S * k + P * t:S * k + P * t + P],
                                                 probs[:, j % 2, S * t + P * k:S * t + P * k + P], ident[:, :])
                    last.then_inc(b_pT_ps, 1)

                def values(j):
                    need(pe, b_pT[j % 2], NA_B // 2 * b + j // 2 + 1)
                    if j == 0:
                        need(pe, b_v, b + 1)
                        need(pe, b_x, b)
                    for t in range(NT):
                        for k in range(NT):
                            at = D * t + DH * j
                            last = pe_.matmul(banks[7][:, at:at + DH],
                                              probsT[:, j % 2, S * k + P * t:S * k + P * t + P],
                                              v_b[:, k, DH * j:DH * j + DH], start=k == 0, stop=k == NT - 1)
                    last.then_inc(b_pv, 1)

                project_qk(0)
                project_qk(1)
                need(pe, b_oT, b)
                for t in range(NT):
                    for k in range(ND):
                        at = DH * (8 + k)
                        last = pe_.matmul(banks[6][:, D * t:D * t + D], hb[:, k, P * t:P * t + P],
                                          head_w[:, par, :, at:at + DH], start=k == 0, stop=k == ND - 1)
                last.then_inc(b_v_ps, 1)
                scores_of(0)
                project_qk(2)
                scores_of(1)
                project_qk(3)
                transposes_p(0)
                scores_of(2)
                transposes_p(1)
                values(0)
                scores_of(3)
                transposes_p(2)
                values(1)
                transposes_p(3)
                values(2)
                values(3)
                need(pe, b_on, b + 1)
                for k in range(ND):
                    for t in range(NT):
                        last = pe_.transpose(banks[6][:, S * k + P * t:S * k + P * t + P],
                                             o_b[:, t, P * k:P * k + P], ident[:, :])
                last.then_inc(b_oT_ps, 1)
                need(pe, b_oT, b + 1)
                for t in range(NT):
                    for k in range(ND):
                        last = pe_.matmul(banks[7][:, D * t:D * t + D], oT_b[:, k, P * t:P * t + P], wo_b[:, k, :],
                                          start=k == 0, stop=k == ND - 1)
                last.then_inc(b_wo_ps, 1)

            for b in range(2):
                attend(b, b)
            with pe.Fori(1, B // 2) as i:
                for par in range(2):
                    attend(2 * i + par, par)
            if stages < 3:
                return

            transposes_h(1, [])
            pe.wait_ge(n_hT, 2 * N16)
            pe.wait_ge(c_w_in, 16 * 9)
            pe.wait_ge(consts, 1)

            def project(b, par):
                need(pe, c_cur, b + 1)
                for k in range(ND):
                    for t in range(NT):
                        last = pe_.transpose(banks[0][:, S * k + P * t:S * k + P * t + P],
                                             ctx_b[:, par, t, P * k:P * k + P], ident[:, :])
                last.then_inc(c_cT_ps, 1)
                for t in range(NT):
                    for k in range(ND):
                        last = pe_.matmul(banks[1][:, D * t:D * t + D], hT[:, par, k, P * t:P * t + P],
                                          w_c[:, 0, k, :], start=k == 0, stop=k == ND - 1)
                last.then_inc(c_q_ps, 1)
                need(pe, c_cT, b + 1)
                need(pe, c_kvn, b)
                for t in range(NT):
                    for k in range(ND):
                        last = pe_.matmul(banks[2 + t][:, :], ctxT[:, k, P * t:P * t + P], w_c[:, 1:3, k, :],
                                          start=k == 0, stop=k == ND - 1)
                last.then_inc(c_kv_ps, 1)

            def transposes_q(b):
                need(pe, c_qn, b + 1)
                need(pe, c_relu, b)
                for k in range(ND):
                    for t in range(NT):
                        last = pe_.transpose(banks[4][:, S * k + P * t:S * k + P * t + P],
                                             qn_c[:, t, P * k:P * k + P], ident[:, :])
                last.then_inc(c_qT_ps, 1)

            def keys_by_values(b):
                need(pe, c_kp, b + 1)
                need(pe, c_yvar, b)
                for dt in range(ND):
                    for t in range(NT):
                        last = pe_.matmul(banks[5][:, S * dt:S * dt + P + 1], kp_c[:, t, P * dt:P * dt + P],
                                          v_ones[:, t, dt, :], start=t == 0, stop=t == NT - 1)
                last.then_inc(c_sum_ps, 1)

            def numerators(b):
                need(pe, c_qp, b + 1)
                need(pe, c_kvm, b + 1)
                need(pe, c_att, b)
                for bank, own in ((6, kv_own), (7, k_own)):
                    for dt in range(ND):
                        last = pe_.matmul(banks[bank][:, S * dt:S * dt + S], own[:, dt, :], qpT_c[:, dt, :],
                                          start=True, stop=True)
                last.then_inc(c_num_ps, 1)

            def transposes_att(b):
                need(pe, c_att, b + 1)
                for k in range(ND):
                    for t in range(NT):
                        last = pe_.transpose(banks[5][:, S * k + P * t:S * k + P * t + P],
                                             att_c[:, t, P * k:P * k + P], ident[:, :])
                last.then_inc(c_aT_ps, 1)

            def out_project(b):
                need(pe, c_aT, b + 1)
                for t in range(NT):
                    for k in range(ND):
                        last = pe_.matmul(banks[5][:, D * t:D * t + D], attT_c[:, k, P * t:P * t + P],
                                          dense_c[:, k, :], start=k == 0, stop=k == ND - 1)
                last.then_inc(c_y_ps, 1)

            def turn(i, par, first=True, second=True, third=True):
                if third:
                    numerators(i)
                if second:
                    transposes_q(i + 1)
                if first:
                    project(i + 2, par)
                if third:
                    transposes_att(i)
                    out_project(i)
                if second:
                    keys_by_values(i + 1)

            turn(-2, 0, second=False, third=False)
            turn(-1, 1, third=False)
            turn(0, 0)
            turn(1, 1)
            with pe.Fori(1, B // 2 - 1) as i:
                for par in range(2):
                    turn(2 * i + par, par)
            turn(B - 2, 0, first=False)
            turn(B - 1, 1, first=False, second=False)
            if stages < 4:
                return

            transposes_h(2, [])
            pe.wait_ge(n_hT, 3 * N16)
            pe.wait_ge(e_in, 32)
            for b in range(B):
                for t in range(NT):
                    for k in range(ND):
                        at = E * (B * t + b)
                        last = pe_.matmul(banks[0][:, at:at + E], hT_all[:, b, k, P * t:P * t + P], w_gate[:, k, :],
                                          start=k == 0, stop=k == ND - 1)
            last.then_inc(e_logit_ps, 1)

            def column_sums(i):
                need(pe, e_gate, i + 1)
                for t in range(NT):
                    last = pe_.matmul(banks[1][:, 0:B * E], ones[:, :], gate_e[:, t, :, :], start=t == 0,
                                      stop=t == NT - 1)
                last.then_inc(e_col_ps, 1)

            column_sums(0)
            with pe.Fori(1, SINKHORN) as i:
                column_sums(i)
            pe.wait_ge(e_gate, SINKHORN + 1)
            for t in range(NT):
                last = pe_.transpose(banks[2][0:B * E, P * t:P * t + P], gate_e[:, t, :, :], ident[:, :])
            last.then_inc(e_gT_ps, 1)
            pe.wait_ge(e_picks, 1)
            for w in range(2):
                last = pe_.transpose(banks[3][0:M, B * E * w:B * E * w + B * E], pick_rows[:, w, :],
                                     ident[0:B * E, 0:B * E])
            last.then_inc(e_cols_ps, 1)
            for g in range(4):
                n = B * E // 4
                last = pe_.matmul(banks[4 + g][:, :], ones16[:, :], spread16[:, n * g:n * g + n, :], start=True,
                                  stop=True)
            last.then_inc(e_rows_ps, 1)
            for b in range(B):
                pe.wait_ge(e_take, NT * b + NT)
                if b >= 2:
                    pe.wait_ge(e_xg, b - 1)
                for k in range(ND):
                    for t in range(NT):
                        last = pe_.matmul(banks[b % 2][:, S * k:S * k + S], h_all[:, NT * b + t, P * k:P * k + P],
                                          take[:, b, t, :], start=t == 0, stop=t == NT - 1)
                last.then_inc(e_xg_ps, 1)
            pe.wait_ge(e_xg, B)
            for e in range(E):
                if e >= 4:
                    pe.wait_ge(e_yT[e % 2], (e - 4) // 2 + 1)
                for f in range(ND):
                    for k in range(ND):
                        last = pe_.matmul(banks[4 + e % 4][:, S * f:S * f + S], w_exp[:, e, k, P * f:P * f + P],
                                          xgT[:, k, e, :, :], start=k == 0, stop=k == ND - 1)
                last.then_inc(e_yT_ps, 1)
            pe.wait_ge(e_yT[0], E // 2)
            pe.wait_ge(e_yT[1], E // 2)
            pe.wait_ge(e_put, 2 * B)

            def slots_by_row(b):
                if b >= 2:
                    pe.wait_ge(e_y, b - 1)
                for half_e in range(2):
                    for f in range(ND):
                        last = pe_.transpose(banks[b % 2][:, D * half_e + P * f:D * half_e + P * f + P],
                                             yT[:, f, b, 4 * half_e:4 * half_e + 4, :], ident[:, :])
                last.then_inc(e_y_ps, 1)

            slots_by_row(0)
            for b in range(B):
                if b + 1 < B:
                    slots_by_row(b + 1)
                pe.wait_ge(e_y, b + 1)
                if b >= 2:
                    pe.wait_ge(e_x, b - 1)
                for t in range(NT):
                    for half_e in range(2):
                        last = pe_.matmul(banks[2 + b % 2][:, D * t:D * t + D], put[:, b, half_e, P * t:P * t + P],
                                          y_e[:, b % 2, half_e, :], start=half_e == 0, stop=half_e == 1)
                last.then_inc(e_o_ps, 1)

        block = ctx.enter_context(nc.Block())
        tok = "b (t p) d -> p (b t) d"
        rows = "(t p) n -> p t n"

        @block.sync
        def _(sp):
            x_v, c_v = io["x"].rearrange(tok, p=P), io["ctx_1024"].rearrange(tok, p=P)
            for i in range(4):
                sp.dma_start(c_all[:, 4 * i:4 * i + 4, :], c_v[:, 4 * i:4 * i + 4, :]).then_inc(c_in[i], 16)
                sp.dma_start(x_all[:, 4 * i:4 * i + 4, :], x_v[:, 4 * i:4 * i + 4, :]).then_inc(x_in[i], 16)
                if i == 0:
                    wkv = io["L0_xattn_Wkv"].rearrange(rows, p=P)
                    sp.dma_start(wkv_a[:, :, 0:INNER], wkv[:, :, 0:INNER]).then_inc(w_in, 16)
                    sp.dma_start(wq_a[:, :, :], io["L0_xattn_Wq"].rearrange(rows, p=P)).then_inc(w_in, 16)
                    sp.dma_start(wkv_a[:, :, INNER:], wkv[:, :, INNER:]).then_inc(w_in, 16)
                if i == 1:
                    sp.dma_start(wo_a[:, :, :], io["L0_xattn_Wo"].rearrange(rows, p=P)).then_inc(w2_in, 16)
            sp.dma_start(head_tab[:, :, 0:6 * DH], io["head_weights"]).then_inc(b_in, 16)
            sp.dma_start(head_tab[:, :, 6 * DH:7 * DH],
                         io["L0_ffn_bv"].rearrange("(h d) -> h d", d=DH).unsqueeze(0).broadcast_to([P, NH_B, DH]))\
                .then_inc(b_in, 16)
            sp.dma_start(head_tab[:, :, 7 * DH:ROW_B], io["head_biases"]).then_inc(b_in, 16)
            sp.dma_start(w_router[:, :, :], io["L0_ffn_Wr"].rearrange(rows, p=P)).then_inc(b_in, 16)
            sp.dma_start(b_router[:, :], io["L0_ffn_br"].unsqueeze(0).broadcast_to([B, NH_B])).then_inc(b_in, 16)
            sp.dma_start(wo_b[:, :, :], io["L0_ffn_Wo"].rearrange(rows, p=P)).then_inc(b_in, 16)
            sp.dma_start(bo_b[:, :], io["L0_ffn_bo"].unsqueeze(0).broadcast_to([P, D])).then_inc(b_in, 16)
            for i, w in enumerate(("wq", "wk", "wv")):
                sp.dma_start(w_c[:, i, :, :], io[f"L1_xattn_{w}"].rearrange(rows, p=P)).then_inc(c_w_in, 16)
            sp.dma_start(dense_c[:, :, :], io["L1_xattn_dense_w"].rearrange(rows, p=P)).then_inc(c_w_in, 16)
            for i, w in enumerate(("ln_gamma", "ln_beta", "dense_b")):
                sp.dma_start(norm_rows[:, i, :], io[f"L1_xattn_{w}"].unsqueeze(0).broadcast_to([P, D]))\
                    .then_inc(c_w_in, 16)
            sp.dma_start(norm_cols[:, :, :], io["norm_cols"]).then_inc(c_w_in, 16)
            sp.dma_start(em[:, :], io["em"]).then_inc(c_w_in, 16)
            sp.dma_start(w_gate[:, :, :], io["L1_ffn_gate_w"].rearrange(rows, p=P)).then_inc(e_in, 16)
            sp.wait_ge(r_chosen, 1)
            sp.dma_start(chosen[0:1, :], chosen8[:, :]).then_inc(r_sent, 16)
            if stages > 3:
                sp.wait_ge(b_sel, B)
                sp.dma_start(w_exp[:, :, :, :], io["L1_ffn_experts"].rearrange("e (t p) n -> p e t n", p=P))\
                    .then_inc(e_in, 16)
            out_v = io["out"].rearrange(tok, p=P)
            if stages < 4:
                sp.wait_ge(*{1: (a_x, NT * B), 2: (b_x, B), 3: (c_x, B)}[stages])
                sp.dma_start(out_v, x_all[:, :, :]).then_inc(out_done, 16)
                sp.wait_ge(out_done, 16)
            else:
                for b in range(B):
                    sp.wait_ge(e_x, b + 1)
                    sp.dma_start(out_v[:, NT * b:NT * b + NT, :], x_all[:, NT * b:NT * b + NT, :]).then_inc(out_done, 16)
                sp.wait_ge(out_done, 16 * B)

        @block.gpsimd
        def _(pool):
            ch = Chain(pool, pool_steps)
            ch.step(pool_.memset(ident[:, :], 0.0))
            ch.step(pool_.memset(half[:, :], -0.5))
            ch.step(pool_.memset(eps5[:, :], 1e-5))
            ch.step(pool_.memset(eps6[:, :], 1e-6))
            ch.step(pool_.memset(minus1[:, :], -1.0))
            ch.step(pool_.memset(ones[:, :], 1.0))
            ch.step(pool_.memset(ones16[:, :], 1.0))
            ch.step(pool_.memset(v_ones[:, :, :, :], 1.0))
            ch.step(pool_.memset(head_block[:, :], 1.0))
            ch.step(pool_.memset(head_cols[:, :], 1.0))
            ch.step(pool_.iota(token_row[:, :], [[1, S]], base=0, channel_multiplier=0,
                               allow_small_or_imprecise_dtypes=True))
            ch.step(pool_.iota(token_col[:, :], [[P, NT]], base=0, channel_multiplier=1,
                               allow_small_or_imprecise_dtypes=True))
            ch.step(pool_.iota(slot_key[:, :, :], [[1, E], [E, M]], base=1, channel_multiplier=0,
                               allow_small_or_imprecise_dtypes=True))
            ch.wait()
            blocks = head_block[:, :].rearrange("p (h c) -> p h c", c=DC)
            for view, inner in ((blocks, [[0, DC]]), (head_cols[:, :], [])):
                for base, sign in ((0, 1), (DC - 1, -1)):
                    ch.step(pool_.affine_select(out=view, in_=view, compare_op=ALU.is_ge, fill=0.0, base=base,
                                                pattern=[[-sign * DC, HP_C]] + inner, channel_multiplier=sign))
                    ch.wait()
            pool_.memset(keyed[:, :, :], 0.0).then_inc(consts, 1)
            ch.wait()
            ch.step(pool_.affine_select(out=ident[:, :], in_=ident[:, :], compare_op=ALU.not_equal, fill=1.0, base=0,
                                        pattern=[[-1, P]], channel_multiplier=1))
            ch.wait()
            pool_.tensor_copy(ident16[:, :], ident[:, :]).then_inc(ident_ready, 1)
            pool.wait_ge(small_in, SMALL * 16)
            pool.wait_ge(gates_ready, 1)
            ch.step(pool_.tensor_scalar(ln_o[:, :, :], ln_o[:, :, :], gates[:, 0:1], 1.0, ALU.mult, ALU.mult))
            start = ch.n

            def rstd(b):
                need(pool, a_var, b + 1)
                need(pool, a_xn, b)
                ch.step(pool_.tensor_tensor(tiny_a[:, 0, :], mv_a[:, :, 1], eps5[:, 0:KT], ALU.add))
                ch.wait()
                ch.step(pool_.tensor_tensor(rstd_a[:, :], tiny_a[:, 0, :], half[:, 0:KT], ALU.pow))
                ch.wait()
                lat, t = rstd_a[:, NT:KT], tiny_a[:, 1, NT:KT]
                ch.step(pool_.tensor_tensor(t, lat, lat, ALU.mult))
                ch.wait()
                ch.step(pool_.tensor_tensor(t, t, mv_a[:, NT:KT, 1], ALU.mult))
                ch.wait()
                ch.step(pool_.tensor_tensor(t, t, eps5[:, 0:NT], ALU.add))
                ch.wait()
                ch.step(pool_.tensor_tensor(t, t, half[:, 0:NT], ALU.pow))
                ch.wait()
                pool_.tensor_tensor(lat, lat, t, ALU.mult).then_inc(a_rstd, 1)

            def norms(b, i):
                need(pool, a_ss, 6 * b + i + 1)
                pool_.tensor_tensor(rnorm[:, i, :], sumsq[:, i, :], half[:, 0:HA], ALU.pow).then_inc(a_rn, 1)

            def low(b, i):
                need(pool, a_hi, 6 * b + i + 1)
                dst = kk16[:, i, :, :] if i < KT else qq16[:, i - KT, :, :]
                pool_.tensor_tensor(dst[:, :, DH:2 * DH], heads(normed[:, i % 2, :]), dst[:, :, 0:DH],
                                    ALU.subtract).then_inc(a_lo, 1)

            def out_rstd(b, qt):
                need(pool, a_ovar, NT * b + qt + 1)
                ch.step(pool_.tensor_tensor(rstd_o[:, 0:1], mv_o[:, 1:2], eps5[:, 0:1], ALU.add))
                ch.wait()
                pool_.tensor_tensor(rstd_o[:, 1:2], rstd_o[:, 0:1], half[:, 0:1], ALU.pow).then_inc(a_orstd, 1)

            def residual(b, qt):
                need(pool, a_y, NT * b + qt + 1)
                ch.step(pool_.tensor_tensor(y_a[:, :], y_a[:, :], ln_o[:, 0, :], ALU.mult))
                ch.wait()
                ch.step(pool_.tensor_tensor(y_a[:, :], y_a[:, :], ln_o[:, 1, :], ALU.add))
                ch.wait()
                pool.sem_inc(held_pool, 1)
                xt = x_all[:, NT * b + qt, :]
                pool_.tensor_tensor(xt, xt, y_a[:, :], ALU.add).then_inc(a_x, 1)

            def batch(b, first=False, last=False):
                for i in range(KT + NT + 1):
                    if i < KT + NT:
                        norms(b, i)
                    if i:
                        low(b, i - 1)
                    if i == 2 and not first:
                        out_rstd(b - 1, 1)
                if not first:
                    residual(b - 1, 1)
                if not last:
                    rstd(b + 1)
                out_rstd(b, 0)
                residual(b, 0)

            rstd(0)
            batch(0, first=True)
            fore, per = ch.n, 12
            with pool.Fori(1, B - 1) as b:
                ch.base, ch.n = fore + per * (b - 1), 0
                batch(b)
                assert ch.n == per
            ch.leave(fore + per * (B - 2))
            batch(B - 1, last=True)
            out_rstd(B - 1, 1)
            residual(B - 1, 1)
            if stages > 1:
                pool_late(pool, ch)

        @block.vector
        def _(dve):
            ch = Chain(dve, dve_steps)
            ch.step(dve_.memset(mask_row[:, :], 0.0))
            dve.wait_ge(small_in, SMALL * 16)
            ch.step(dve_.tensor_tensor(qk_scale[:, 0, :], qk_scale[:, 0, :], qk_scale[:, 1, :], ALU.mult))
            start = ch.n

            def hold(semaphore, value):
                if isinstance(value, int) and value <= 0:
                    return
                dve.wait_ge(semaphore, value)
                if not isinstance(value, int):
                    dve.sem_inc(held, 1)

            def token_tile(b, t):
                return c_all[:, NT * b + t, :] if t < NT else x_all[:, NT * b + t - NT, :]

            def stats(b):
                for t in range(KT):
                    ch.step(dve_.bn_stats(stat_a[:, t, :], token_tile(b, t)))
                hold(dve_steps, ch.base + ch.n)
                hold(a_xn, b)
                for t in range(KT):
                    last = dve_.bn_aggr(mv_a[:, t, :], stat_a[:, t, :])
                last.then_inc(a_var, 1)

            def norm(b):
                need(dve, a_rstd, b + 1)
                need(dve, a_xT_ps, ND * b)
                for t in range(KT):
                    last = dve_.tensor_scalar(xn_a[:, t, :], token_tile(b, t), mv_a[:, t, 0:1], rstd_a[:, t:t + 1],
                                              ALU.subtract, ALU.mult)
                last.then_inc(a_xn, 1)

            def head_sums(b, i):
                need(dve, a_sq, 6 * b + i + 1)
                ch.step(dve_.tensor_reduce(sumsq[:, i, :], heads(square[:, i % 2, :]), AX, ALU.add))
                ch.wait()
                dve_.tensor_scalar(sumsq[:, i, :], sumsq[:, i, :], 1e-24, None, ALU.max).then_inc(a_ss, 1)

            def unit_norm(b, i):
                need(dve, a_rn, 6 * b + i + 1)
                need(dve, a_lo, 6 * b + i - 1)
                n = heads(normed[:, i % 2, :])
                ins = dve_.tensor_tensor(n, heads(banks[i][:, :]), across(rnorm[:, i, :], DH), ALU.mult)
                if i >= KT:
                    ch.step(ins)
                    ch.wait()
                    ins = dve_.tensor_tensor(n, n, qk_scale[:, 0:1, :].broadcast_to([P, HA, DH]), ALU.mult)
                ins.then_inc(a_kn, 1)

            def transposed(b, j):
                need(dve, a_kqT_ps, 8 * b + j + 1)
                if j < KT:
                    dst, src = kT16[:, :, P * j:P * j + P], j
                else:
                    qt, v = divmod(j - KT, 2)
                    dst, src = qT16[:, v, :, P * qt:P * qt + P], (4 + v if qt == 0 else v)
                dve_.tensor_copy(dst, bank16(src).rearrange("p (h n) -> p h n", h=HA)).then_inc(a_kqT, 1)

            def maximum(b, u):
                need(dve, a_ex, UNITS * b + u - 1)
                hold(a_s_ps, UNITS * b + u + 1)
                dve_.tensor_tensor_reduce(out=scores[:, u % 2, :], in0=banks[2 + u % 2][:, :], in1=mask_row[:, :],
                                          scale=-8.0, scalar=3e38, op0=ALU.add, op1=ALU.min,
                                          accum_out=negmax[:, u:u + 1]).then_inc(a_max, 1)

            def copy_pT(b, u):
                need(dve, a_pT_ps, UNITS * b + u + 1)
                need(dve, a_pv, UNITS * b + u - 1)
                dve_.tensor_copy(probsT[:, u % 2, :], banks[4 + u % 2][:, :]).then_inc(a_pT[0], 1)

            def divide(b, qt):
                need(dve, a_pv, UNITS * b + HA * (qt + 1))
                ch.step(dve_.reciprocal(recip_a[:, :], rowsum[:, HA * qt:HA * qt + HA]))
                ch.wait()
                need(dve, a_oT_ps, NT * b + qt)
                dve_.tensor_tensor(heads(o_a[:, :]), heads(banks[6 + qt][:, :]), across(recip_a[:, :], DH),
                                   ALU.mult).then_inc(a_on, 1)

            def out_stats(b, qt):
                need(dve, a_wo_ps, NT * b + qt + 1)
                ch.step(dve_.bn_stats(stat_o[:, :], banks[1 + 4 * qt][:, 0:D]))
                hold(dve_steps, ch.base + ch.n)
                dve_.bn_aggr(mv_o[:, :], stat_o[:, :]).then_inc(a_ovar, 1)

            def out_norm(b, qt):
                need(dve, a_orstd, NT * b + qt + 1)
                need(dve, a_x, NT * b + qt)
                dve_.tensor_scalar(y_a[:, :], banks[1 + 4 * qt][:, 0:D], mv_o[:, 0:1], rstd_o[:, 1:2], ALU.subtract,
                                   ALU.mult).then_inc(a_y, 1)

            def batch(b, first=False, last=False):
                if not first:
                    divide(b - 1, 1)
                n = KT + NT
                for i in range(n + 1):
                    if i < n:
                        head_sums(b, i)
                    if i:
                        unit_norm(b, i - 1)
                    if i == 2 and not first:
                        out_stats(b - 1, 1)
                    if i == 3 and not first:
                        out_norm(b - 1, 1)
                    if i > n - 2:
                        transposed(b, 2 * (i - n) + 2)
                        transposed(b, 2 * (i - n) + 3)
                ch.step(dve_.tensor_scalar(mask_row[:, 0:S], mask8[:, b, :], OFF, -OFF, ALU.mult, ALU.add))
                transposed(b, KT)
                transposed(b, KT + 1)
                hold(dve_steps, ch.base + ch.n)
                maximum(b, 0)
                maximum(b, 1)
                for u in range(UNITS):
                    if u + 2 < UNITS:
                        maximum(b, u + 2)
                    if u % 2 == 0:
                        copy_pT(b, u)
                    if u == 1:
                        transposed(b, KT + 2)
                        transposed(b, KT + 3)
                    if u == 2 and not last:
                        stats(b + 1)
                    if u == HA - 2 and not last:
                        norm(b + 1)
                    if u == HA:
                        divide(b, 0)
                    if u == HA + 4:
                        out_stats(b, 0)
                    if u == HA + 5:
                        out_norm(b, 0)

            dve.wait_ge(c_in[0], 16)
            dve.wait_ge(x_in[0], 16)
            stats(0)
            norm(0)
            for i in range(1, 4):
                dve.wait_ge(c_in[i], 16)
                dve.wait_ge(x_in[i], 16)
            batch(0, first=True)
            fore, per = ch.n, 17
            with dve.Fori(1, B - 1) as b:
                ch.base, ch.n = fore + per * (b - 1), 0
                batch(b)
                assert ch.n == per, ch.n
            ch.leave(fore + per * (B - 2))
            batch(B - 1, last=True)
            divide(B - 1, 1)
            out_stats(B - 1, 1)
            out_norm(B - 1, 1)
            if stages > 1:
                dve_late(dve, ch)

        @block.scalar
        def _(act):
            def row(ap):
                return ap.unsqueeze(0).broadcast_to([P, ap.shape[0]])

            pre = "L0_xattn_"
            small = [(ln_cols[:, :, :], io["ln_cols"]),
                     (gates[:, 0:2], row(io["g_xattn"])), (gates[:, 2:4], row(io["g_ffn"])),
                     (qk_scale[:, 0, :], row(io[pre + "q_scale"])), (qk_scale[:, 1, :], row(io[pre + "k_scale"])),
                     (ln_o[:, 0, :], row(io[pre + "ln_o_w"])), (ln_o[:, 1, :], row(io[pre + "ln_o_b"])),
                     (mask8[:, :, :], io["mask_BxS2_bk0"].unsqueeze(0).broadcast_to([P, B, S]))]
            assert len(small) == SMALL
            for dst, src in small:
                act.dma_start(dst, src).then_inc(small_in, 16)
            act.wait_ge(small_in, SMALL * 16)
            act_.activation(gates[:, :], gates[:, :], ACT.Tanh).then_inc(gates_ready, 1)

            def copy_xT(b):
                for dt in range(ND):
                    need(act, a_xT_ps, ND * b + dt + 1)
                    for part in range(2):
                        w, c = ln_cols[:, 2 * part, dt:dt + 1], ln_cols[:, 2 * part + 1, dt:dt + 1]
                        cut = slice(S * part, S * part + S)
                        last = act_.activation(xT_a[:, dt, cut], banks[dt][:, cut], ACT.Identity, bias=c, scale=w)
                    last.then_inc(a_xT, 1)

            def squares(b, i):
                need(act, a_kq_ps, 6 * b + i + 1)
                need(act, a_ss, 6 * b + i - 1)
                act_.activation(square[:, i % 2, :], banks[i][:, :], ACT.Square).then_inc(a_sq, 1)

            def high(b, i):
                need(act, a_kn, 6 * b + i + 1)
                n = heads(normed[:, i % 2, :])
                if i < KT:
                    act_.activation(kk16[:, i, :, 0:DH], n, ACT.Copy).then_inc(a_hi, 1)
                else:
                    q = qq16[:, i - KT, :, :]
                    act_.activation(q[:, :, 0:DH], n, ACT.Copy)
                    act_.activation(q[:, :, 2 * DH:3 * DH], n, ACT.Copy).then_inc(a_hi, 1)

            def copy_v(b, t):
                need(act, a_v_ps, KT * b + t + 1)
                act_.activation(v_a[:, t, :], banks[6 + t % 2][:, :], ACT.Copy).then_inc(a_v, 1)

            def exps(b, u):
                need(act, a_max, UNITS * b + u + 1)
                need(act, a_pT_ps, UNITS * b + u - 1)
                act_.activation(probs[:, u % 2, :], scores[:, u % 2, :], ACT.Exp, bias=negmax[:, u:u + 1], scale=-1.0,
                                accum_out=rowsum[:, u:u + 1]).then_inc(a_ex, 1)

            def copy_pT(b, u):
                need(act, a_pT_ps, UNITS * b + u + 1)
                need(act, a_pv, UNITS * b + u - 1)
                act_.activation(probsT[:, u % 2, :], banks[4 + u % 2][:, :], ACT.Copy).then_inc(a_pT[1], 1)

            def copy_oT(b, qt):
                need(act, a_oT_ps, NT * b + qt + 1)
                need(act, a_wo_ps, NT * b + qt)
                act_.activation(oT_a[:, :, :], banks[4 * qt][:, :].rearrange("p (k n) -> p k n", n=P), ACT.Copy)\
                    .then_inc(a_oT, 1)

            def batch(b, first=False, last=False):
                n = KT + NT
                for i in range(n + 2):
                    if i < n:
                        squares(b, i)
                    if i == 1 and not first:
                        copy_oT(b - 1, 1)
                    if i > 1:
                        high(b, i - 2)
                    if i >= n - 1:
                        copy_v(b, i - n + 1)
                copy_v(b, KT - 1)
                exps(b, 0)
                for u in range(UNITS):
                    if u + 1 < UNITS:
                        exps(b, u + 1)
                    if u % 2:
                        copy_pT(b, u)
                    if u == HA + 2:
                        copy_oT(b, 0)
                if not last:
                    copy_xT(b + 1)

            copy_xT(0)
            batch(0, first=True)
            with act.Fori(1, B - 1) as b:
                batch(b)
            batch(B - 1, last=True)
            copy_oT(B - 1, 1)
            if stages > 1:
                act_late(act)

        @block.tensor
        def _(pe):
            def transposes_x(b):
                need(pe, a_xn, b + 1)
                need(pe, a_oT, NT * (b - 1) + 1)
                need(pe, a_y, NT * (b - 1) + 1)
                for dt in range(ND):
                    for t in range(KT):
                        last = pe_.transpose(banks[dt][:, P * t:P * t + P], xn_a[:, t, P * dt:P * dt + P],
                                             ident[:, :])
                    last.then_inc(a_xT_ps, 1)

            def project(bank, t, w, done):
                for k in range(ND):
                    last = pe_.matmul(banks[bank][:, :], xT_a[:, k, P * t:P * t + P], w[:, k, :], start=k == 0,
                                      stop=k == ND - 1)
                last.then_inc(done, 1)

            def project_kq(b, i):
                if i == 0:
                    need(pe, a_xT, ND * b + ND)
                if i == 2:
                    need(pe, a_max, UNITS * b)
                if i == 4:
                    need(pe, a_oT, NT * b)
                if i == 5:
                    need(pe, a_y, NT * b)
                if i < KT:
                    project(i, i, wkv_a[:, :, 0:INNER], a_kq_ps)
                else:
                    project(i, i - KT + NT, wq_a, a_kq_ps)

            def project_v(b, t):
                need(pe, a_v, KT * b + t - 1)
                project(6 + t % 2, t, wkv_a[:, :, INNER:], a_v_ps)

            def transposes_kq(b, j):
                if j < KT:
                    need(pe, a_lo, 6 * b + j + 1)
                    dst, src = bank16(j), kk16[:, j, :, :]
                else:
                    qt, v = divmod(j - KT, 2)
                    need(pe, a_lo, 6 * b + KT + qt + 1)
                    if j == KT + 1:
                        need(pe, a_kn, 6 * b + KT + NT)
                    if qt == 1:
                        need(pe, a_kqT, 8 * b + v + 1)
                    dst, src = bank16(4 + v if qt == 0 else v), qq16[:, qt, :, DH * v:DH * v + 2 * DH]
                for h in range(HA):
                    last = pe_.transpose(dst[:, P * h:P * h + P], src[:, h, :], ident16[:, :])
                last.then_inc(a_kqT_ps, 1)

            def scores_of(b, u):
                qt, h = divmod(u, HA)
                if u == 0:
                    need(pe, a_kqT, 8 * b + KT + 2)
                if u == HA:
                    need(pe, a_kqT, 8 * b + 8)
                if u >= 2:
                    need(pe, a_max, UNITS * b + u - 1)
                for v in range(2):
                    last = pe_.matmul(banks[2 + u % 2][:, :], qT16[:, v, h, P * qt:P * qt + P], kT16[:, h, :],
                                      start=v == 0, stop=v == 1)
                last.then_inc(a_s_ps, 1)

            def transposes_p(b, u):
                need(pe, a_ex, UNITS * b + u + 1)
                if u >= 2:
                    need(pe, a_pT[u % 2], UNITS // 2 * b + u // 2)
                for kt in range(KT):
                    last = pe_.transpose(banks[4 + u % 2][:, P * kt:P * kt + P], probs[:, u % 2, P * kt:P * kt + P],
                                         ident[:, :])
                last.then_inc(a_pT_ps, 1)

            def values(b, u):
                qt, h = divmod(u, HA)
                need(pe, a_pT[u % 2], UNITS // 2 * b + u // 2 + 1)
                if u == 0:
                    need(pe, a_v, KT * b + KT)
                for kt in range(KT):
                    last = pe_.matmul(banks[6 + qt][:, DH * h:DH * h + DH], probsT[:, u % 2, P * kt:P * kt + P],
                                      v_a[:, kt, DH * h:DH * h + DH], start=kt == 0, stop=kt == KT - 1)
                last.then_inc(a_pv, 1)

            def transposes_o(b, qt):
                need(pe, a_on, NT * b + qt + 1)
                for k in range(INNER // P):
                    last = pe_.transpose(banks[4 * qt][:, P * k:P * k + P], o_a[:, P * k:P * k + P], ident[:, :])
                last.then_inc(a_oT_ps, 1)

            def out_project(b, qt):
                need(pe, a_oT, NT * b + qt + 1)
                need(pe, a_y, NT * b + qt)
                for k in range(INNER // P):
                    last = pe_.matmul(banks[1 + 4 * qt][:, 0:D], oT_a[:, k, :], wo_a[:, k, :], start=k == 0,
                                      stop=k == INNER // P - 1)
                last.then_inc(a_wo_ps, 1)

            def batch(b, first=False, last=False):
                for i in range(KT + NT):
                    project_kq(b, i)
                    if i == 0 and not first:
                        transposes_o(b - 1, 1)
                    if i == 1 and not first:
                        out_project(b - 1, 1)
                project_v(b, 0)
                project_v(b, 1)
                transposes_kq(b, 0)
                transposes_kq(b, 1)
                project_v(b, 2)
                transposes_kq(b, 2)
                transposes_kq(b, 3)
                project_v(b, 3)
                transposes_kq(b, KT)
                transposes_kq(b, KT + 1)
                scores_of(b, 0)
                scores_of(b, 1)
                for u in range(UNITS):
                    if u + 2 < UNITS:
                        scores_of(b, u + 2)
                    transposes_p(b, u)
                    if u == 1:
                        transposes_kq(b, KT + 2)
                        transposes_kq(b, KT + 3)
                    if u:
                        values(b, u - 1)
                    if u == HA + 1:
                        transposes_o(b, 0)
                    if u == HA + 3:
                        if first:
                            pe.wait_ge(w2_in, 16)
                        out_project(b, 0)
                    if u == UNITS - 2 and not last:
                        transposes_x(b + 1)
                values(b, UNITS - 1)

            pe.wait_ge(ident_ready, 1)
            transposes_x(0)
            pe.wait_ge(w_in, 16 * 3)
            batch(0, first=True)
            with pe.Fori(1, B - 1) as b:
                batch(b)
            batch(B - 1, last=True)
            transposes_o(B - 1, 1)
            out_project(B - 1, 1)
            if stages > 1:
                pe_late(pe)


SMALL = 8


def kernel(**inputs):
    import numpy as np
    import concourse.bacc as bacc
    from concourse.bass_utils import run_bass_kernel_spmd as run

    nc = bacc.Bacc("TRN2", target_bir_lowering=False, num_devices=1)
    arrays, io = {}, {}
    laid = {name: np.asarray(value) for name, value in inputs.items()}
    by_width = [laid.pop("L0_xattn_" + n).reshape(ND, P).T for n in ("ln_x_w", "ln_x_b", "ln_l_w", "ln_l_b")]
    laid["ln_cols"] = np.stack(by_width, axis=1)
    by_head = [laid.pop("L0_ffn_W" + n).reshape(ND, P, NH_B, DH).transpose(1, 2, 0, 3) for n in "qkv"]
    laid["head_weights"] = np.stack(by_head, axis=2).reshape(P, NH_B, 6 * DH)
    biases = np.stack([laid.pop("L0_ffn_b" + n).reshape(NH_B, DH).T for n in "qk"], axis=2)
    laid["head_biases"] = np.concatenate([biases, biases], axis=0)
    laid["norm_cols"] = np.stack([laid["L1_xattn_ln_" + n].reshape(ND, P).T for n in ("gamma", "beta")], axis=1)
    laid["em"] = laid.pop("mask_BxS2_ff1").reshape(B * NT, P).T
    for name, value in laid.items():
        a = np.ascontiguousarray(value)
        arrays[f"in_{name}"] = a
        io[name] = nc.dram_tensor(f"in_{name}", a.shape, mybir.dt.from_np(a.dtype), kind="ExternalInput").ap()
    io["out"] = nc.dram_tensor("out_0", (B, S, D), F32, kind="ExternalOutput").ap()
    build(nc, io)
    return run(nc, [arrays], core_ids=[0]).results[0]["out_0"]
```

```python
from contextlib import ExitStack

import concourse.bass as bass
from concourse import mybir

F32 = mybir.dt.float32
F16 = mybir.dt.float16
I32 = mybir.dt.int32
U32 = mybir.dt.uint32
U8 = mybir.dt.uint8
ALU = mybir.AluOpType
ACT = mybir.ActivationFunctionType
AX = mybir.AxisListType.X

P = 128
B, S, D = 8, 256, 256
NT = S // P
ND = D // P
HA, DH = 8, 64
INNER = HA * DH
KV = 2 * S
KT = KV // P
UNITS = HA * NT
KQ_BANK = (0, 1, 0, 1, 0, 1)
KQ_UNIT = (1, 3, 5, 7, 9, 11)
OFF = 1e30

NH_B, NA_B = 16, 4
ROW_B = 7 * DH + 2
BIAS_B = 11 * DH
DC = 16
HP_C = P // DC
E, M = 8, 32
SINKHORN = 8
SMALL = 7
B_LOADS, C_LOADS = 7, 9


class Chain:

    def __init__(self, eng, sem):
        self.eng, self.sem, self.base, self.n = eng, sem, 0, 0

    def step(self, ins):
        self.n += 1
        return ins.then_inc(self.sem, 1)

    def wait(self):
        if isinstance(self.base, int) and self.base + self.n <= 0:
            return
        self.eng.wait_ge(self.sem, self.base + self.n)

    def leave(self, base):
        self.base, self.n = 0, base


def need(eng, sem, value):
    if isinstance(value, int) and value <= 0:
        return
    eng.wait_ge(sem, value)


def build(nc, io):
    with ExitStack() as ctx:
        def sb(name, shape, dt=F32):
            return ctx.enter_context(nc.sbuf_tensor(name, shape, dt))

        def sem(name):
            return ctx.enter_context(nc.semaphore(name))

        pe_, dve_, act_, pool_ = nc.tensor, nc.vector, nc.scalar, nc.gpsimd
        banks = [ctx.enter_context(nc.psum_tensor(f"bank{i}", [P, 512], F32)) for i in range(8)]

        def bank16(i):
            return banks[i][:, :].bitcast(F16)

        def heads(ap):
            return ap.rearrange("p (h d) -> p h d", d=DH)

        def across(ap, n):
            return ap.unsqueeze(2).broadcast_to([P, ap.shape[1], n])

        arena = sb("arena", [P, 4 * B * NT * S])
        h_all = sb("h_all", [P, B * NT, D])
        h_flat = h_all[:, :, :].rearrange("p a b -> p (a b)")
        taken = [0]
        taken_h = [0]

        def carve(shape, dt=F32, arena=arena, taken=taken):
            elems = 1
            for n in shape[1:]:
                elems *= n
            words = elems if dt == F32 else elems // 2
            at, taken[0] = taken[0], taken[0] + words
            assert taken[0] <= arena.shape[1]
            flat = arena[:, at:at + words]
            flat = flat if dt == F32 else flat.bitcast(dt)
            names = "abcd"[:len(shape) - 1]
            sizes = {n: k for n, k in zip(names[1:], shape[2:])}
            return flat.rearrange(f"p ({' '.join(names)}) -> p {' '.join(names)}", **sizes)

        x_all = sb("x_all", [P, B * NT, D])
        c_all = sb("c_all", [P, B * NT, D])
        ident = sb("ident", [P, P])
        ident16 = sb("ident16", [P, P], F16)
        eps5 = sb("eps5", [P, 16])
        half = sb("half", [P, 16])
        mask8 = sb("mask8", [P, B, S], U8)
        gates = sb("gates", [P, 4])

        wq_a = carve([P, ND, INNER], F32, h_flat, taken_h)
        wkv_a = carve([P, ND, 2 * INNER])
        wo_a = carve([P, INNER // P, D], F32, h_flat, taken_h)
        ln_cols = sb("ln_cols", [P, 4, ND])
        qk_scale = sb("qk_scale", [P, 2, DH])
        ln_o = carve([P, 2, D], F32, h_flat, taken_h)
        stat_a = sb("stat_a", [P, KT, 6])
        mv_a = sb("mv_a", [P, KT, 2])
        rstd_a = sb("rstd_a", [P, KT])
        tiny_a = sb("tiny_a", [P, 2, KT])
        xn_a = carve([P, KT, D])
        xT_a = carve([P, ND, KV])
        v_a = carve([P, KT, INNER])
        square = carve([P, 2, INNER])
        normed = carve([P, 2, INNER])
        sumsq = sb("sumsq", [P, KT + NT, HA])
        rnorm = sb("rnorm", [P, KT + NT, HA])
        kk16 = carve([P, KT, HA, 2 * DH], F16)
        qq16 = carve([P, NT, HA, 3 * DH], F16)
        kT16 = carve([P, HA, KV], F16)
        qT16 = carve([P, 2, HA, S], F16)
        mask_row = sb("mask_row", [P, KV])
        scores = sb("scores", [P, 2, KV])
        probs = sb("probs", [P, 2, KV])
        probsT = sb("probsT", [P, 2, KV])
        negmax = sb("negmax", [P, UNITS])
        rowsum = sb("rowsum", [P, UNITS])
        recip_a = sb("recip_a", [P, HA])
        o_a = carve([P, INNER], F32, h_flat, taken_h)
        oT_a = carve([P, INNER // P, P], F32, h_flat, taken_h)
        stat_o = sb("stat_o", [P, 6])
        mv_o = sb("mv_o", [P, 2])
        rstd_o = sb("rstd_o", [P, 2])
        y_a = carve([P, D], F32, h_flat, taken_h)

        stat_n = sb("stat_n", [P, NT, 6])
        mv_n = sb("mv_n", [P, NT, 2])
        rstd_n = sb("rstd_n", [P, 2, NT])
        h_cur = sb("h_cur", [P, NT, D])
        hT_all = sb("hT_all", [P, B, ND, S])
        hT = sb("hT", [P, 2, ND, S])

        h_sum = sb("h_sum", [P, ND, B])
        w_router = sb("w_router", [P, ND, NH_B])
        b_router = sb("b_router", [B, NH_B])
        logits = sb("logits", [B, NH_B])
        top = sb("top", [B, 8])
        top_at = sb("top_at", [B, 8], U32)
        neg_at = sb("neg_at", [B, 8])
        sorted_at = sb("sorted_at", [B, 8])
        chosen8 = sb("chosen8", [B, NA_B], I32)
        chosen = sb("chosen", [1, B * NA_B], I32)
        head_tab = sb("head_tab", [P, NH_B, ROW_B])
        taken[0] = 0
        head_w = carve([P, 2, NA_B, BIAS_B + 2])
        wo_b = sb("wo_b", [P, NA_B * DH // P, D])
        bo_b = sb("bo_b", [P, D])
        q_high = carve([P, NA_B, S], F16)
        q_low = carve([P, NA_B, S], F16)
        k_both = carve([P, NA_B, S], F16)
        v_b = carve([P, NT, NA_B * DH])
        negmax_b = sb("negmax_b", [P, NA_B, NT])
        rowsum_b = sb("rowsum_b", [P, NT, NA_B])
        recip_b = sb("recip_b", [P, NT * NA_B])
        o_b = carve([P, NT, NA_B * DH])
        oT_b = carve([P, ND, S])

        w_c = sb("w_c", [P, 3, ND, D])
        dense_c = sb("dense_c", [P, ND, D])
        norm_rows = sb("norm_rows", [P, 3, D])
        gated_rows = sb("gated_rows", [P, 2, D])
        norm_cols = sb("norm_cols", [P, 2, ND])
        em = sb("em", [P, B * NT])
        eps6 = sb("eps6", [P, 16])
        minus1 = sb("minus1", [P, 16])
        taken[0] = 0
        ctx_b = carve([P, 2, NT, D])
        ctxT = carve([P, ND, S])
        stat_c = sb("stat_c", [P, 6, 6])
        mv_c = sb("mv_c", [P, 6, 2])
        rstd_c = sb("rstd_c", [P, 2, 6])
        qn_c = carve([P, NT, D])
        kv_c = carve([P, NT, 2, D])
        kp_c = carve([P, NT, D])
        v_ones = sb("v_ones", [P, NT, ND, P + 1])
        qpT_c = carve([P, ND, S])
        head_block = sb("head_block", [P, P])
        head_cols = sb("head_cols", [P, HP_C])
        parity = sb("parity", [P, 2])
        kv_own = carve([P, ND, P])
        k_own = carve([P, ND, P])
        turned_c = carve([P, 2, ND * DC, 2 * DC])
        den_c = carve([P, 2, ND * DC])
        att_c = carve([P, NT, D])
        attT_c = carve([P, ND, S])
        y_c = carve([P, NT, D])
        stat_y = sb("stat_y", [P, NT, 6])
        mv_y = sb("mv_y", [P, NT, 2])
        rstd_y = sb("rstd_y", [P, 2, NT])

        w_gate = sb("w_gate", [P, ND, E])
        w_exp = head_tab[:, :, :].rearrange("p h r -> p (h r)")[:, 0:E * ND * D]\
            .rearrange("p (e t n) -> p e t n", e=E, t=ND)
        ones = sb("ones", [P, P])
        ones16 = sb("ones16", [B * E, P], F16)
        gate_e = sb("gate_e", [P, NT, B, E])
        recip_col = sb("recip_col", [P, B, E])
        sum_row = sb("sum_row", [P, 2, B * NT])
        gateT = sb("gateT", [B * E, S])
        picked = sb("picked", [B * E, M])
        picked_at = sb("picked_at", [B * E, M], U32)
        pick_rows = sb("pick_rows", [B * E, 2, M])
        spread16 = scores[0:B * E, :, :].rearrange("p a b -> p (a b)").bitcast(F16)\
            .rearrange("p (r m) -> p r m", m=M)
        slot_cols = sb("slot_cols", [P, 2, B * E * M // P])
        token_col = sb("token_col", [P, NT])
        token_row = sb("token_row", [P, S])
        slot_key = sb("slot_key", [P, E, M])
        keyed = w_c[:, :, :, :].rearrange("p w k n -> p (w k n)")[:, 0:2 * NT * (S + 1)]\
            .rearrange("p (b t n) -> p b t n", b=2, t=NT)
        winner = sb("winner", [P, 2, NT])
        taken[0] = 0
        take = carve([P, B, NT, S])
        put = carve([P, B, 2, S])
        xgT = carve([P, ND, E, B, M])
        yT = carve([P, ND, B, E, M])
        y_e = probs[:, :, :].rearrange("p s (a n) -> p s a n", n=D)

        x_in = [sem(f"x_in{i}") for i in range(4)]
        c_in = [sem(f"c_in{i}") for i in range(4)]
        wk_in = sem("wk_in"); wq_in = sem("wq_in"); wv_in = sem("wv_in"); cols_in = sem("cols_in")
        w2_in = sem("w2_in"); small_in = sem("small_in")
        out_done = sem("out_done")
        ident_ready = sem("ident_ready"); pool_steps = sem("pool_steps"); dve_steps = sem("dve_steps")
        gates_ready = sem("gates_ready")
        held = sem("held"); held_pool = sem("held_pool"); held_act = sem("held_act")
        a_var = sem("a_var"); a_rstd = sem("a_rstd"); a_xn = sem("a_xn"); a_xT_ps = sem("a_xT_ps"); a_xT = sem("a_xT")
        a_kq_ps = sem("a_kq_ps"); a_sq = sem("a_sq"); a_ss = sem("a_ss"); a_rn = sem("a_rn"); a_kn = sem("a_kn")
        a_hi = sem("a_hi"); a_lo = sem("a_lo"); a_kqT_ps = sem("a_kqT_ps"); a_kqT = sem("a_kqT")
        a_v_ps = sem("a_v_ps"); a_v = sem("a_v")
        a_s_ps = sem("a_s_ps"); a_max = sem("a_max"); a_ex = sem("a_ex"); a_pT_ps = sem("a_pT_ps")
        a_pT = [sem("a_pT_dve"), sem("a_pT_act")]; a_pv = sem("a_pv")
        a_on = sem("a_on"); a_oT_ps = sem("a_oT_ps"); a_oT = sem("a_oT"); a_wo_ps = sem("a_wo_ps")
        a_ovar = sem("a_ovar"); a_orstd = sem("a_orstd"); a_y = sem("a_y"); a_x = sem("a_x")

        b_in = sem("b_in"); c_w_in = sem("c_w_in"); e_in = sem("e_in")
        n_var = sem("n_var"); n_rstd = sem("n_rstd"); n_h = sem("n_h"); n_ps = sem("n_ps"); n_hT = sem("n_hT")
        r_ps = sem("r_ps"); r_chosen = sem("r_chosen"); r_sent = sem("r_sent")
        b_scaled = sem("b_scaled"); b_bias = sem("b_bias"); b_sel = sem("b_sel"); b_qk_ps = sem("b_qk_ps")
        b_v_ps = sem("b_v_ps"); b_hi = sem("b_hi"); b_lo = sem("b_lo"); b_v = sem("b_v"); b_s_ps = sem("b_s_ps")
        b_max = sem("b_max"); b_ex = sem("b_ex"); b_pT_ps = sem("b_pT_ps"); b_pv = sem("b_pv")
        b_pT = [sem("b_pT_dve"), sem("b_pT_act")]
        b_on = sem("b_on"); b_oT_ps = sem("b_oT_ps"); b_oT = sem("b_oT"); b_wo_ps = sem("b_wo_ps"); b_x = sem("b_x")
        c_cur = sem("c_cur"); c_cT_ps = sem("c_cT_ps"); c_cT = sem("c_cT"); c_q_ps = sem("c_q_ps")
        c_kv_ps = sem("c_kv_ps"); c_var = sem("c_var"); c_rstd = sem("c_rstd"); c_qn = sem("c_qn")
        c_kvn = sem("c_kvn"); c_kvg = sem("c_kvg"); c_kvb = sem("c_kvb"); c_kp = sem("c_kp"); c_vm = sem("c_vm")
        c_qT_ps = sem("c_qT_ps")
        c_relu = sem("c_relu"); c_qp = sem("c_qp"); c_sum_ps = sem("c_sum_ps"); c_kvm = sem("c_kvm")
        c_num_ps = sem("c_num_ps"); c_att = sem("c_att"); c_aT_ps = sem("c_aT_ps"); c_aT = sem("c_aT")
        c_y_ps = sem("c_y_ps"); c_yvar = sem("c_yvar"); c_yrstd = sem("c_yrstd"); c_yg = sem("c_yg"); c_x = sem("c_x")
        e_logit_ps = sem("e_logit_ps"); e_gate = sem("e_gate"); e_col_ps = sem("e_col_ps"); e_gT_ps = sem("e_gT_ps")
        e_picks = sem("e_picks"); e_rows_ps = sem("e_rows_ps"); e_cols_ps = sem("e_cols_ps"); e_take = sem("e_take")
        e_put = sem("e_put"); e_xg_ps = sem("e_xg_ps"); e_xg = sem("e_xg"); e_yT_ps = sem("e_yT_ps")
        e_yT = [sem("e_yT_dve"), sem("e_yT_act")]
        e_y_ps = sem("e_y_ps"); e_y = sem("e_y"); e_o_ps = sem("e_o_ps"); e_x = sem("e_x")
        consts = sem("consts")

        def pool_late(pool, ch, token_rstd):
            token_rstd(B - 1)
            pool.wait_ge(b_in, 16 * B_LOADS)
            pool.wait_ge(gates_ready, 1)
            pool_.tensor_scalar(bo_b[:, :], bo_b[:, :], gates[:, 2:3], 1.0, ALU.mult, ALU.mult).then_inc(b_bias, 1)

            def current(b, par):
                need(pool, b_v_ps, b - 1)
                need(pool, b_qk_ps, NA_B * (b - 1))
                pool_.tensor_copy(hT[:, par, :, :].unsqueeze(1), hT_all[:, bass.ds(b, 1), :, :])

            def choose(b, par):
                need(pool, b_on, b - 1)
                for j in range(NA_B):
                    at = pool.value_load(chosen[0:1, bass.ds(NA_B * b + j, 1)], min_val=0, max_val=NH_B - 1)
                    twice = head_w[:, par, j, 0:8 * DH].rearrange("p (g r d) -> p g r d", r=2, d=DH)
                    row = head_tab[:, bass.ds(at, 1), :]
                    once = row[:, 0, 0:4 * DH].rearrange("p (g d) -> p g d", d=DH)
                    for r in range(2):
                        pool_.tensor_copy(twice[:, :, r, :], once)
                    pool_.tensor_copy(head_w[:, par, j, 8 * DH:].unsqueeze(1), row[:, :, 4 * DH:]).then_inc(b_sel, 1)

            pool.wait_ge(n_hT, 2)
            current(0, 0)
            pool.wait_ge(r_sent, 16)
            pool.wait_ge(b_scaled, 1)
            choose(0, 0)
            current(1, 1)
            choose(1, 1)
            fore, per = ch.n, 1
            with pool.Fori(1, B // 2) as i:
                for par in range(2):
                    ch.base, ch.n = fore + per * (2 * i + par - 2), 0
                    current(2 * i + par, par)
                    choose(2 * i + par, par)
                    token_rstd(B + 2 * i + par - 2)
                    assert ch.n == per
            ch.leave(fore + per * (B - 2))
            token_rstd(2 * B - 2)

            pool.wait_ge(c_w_in, 16 * C_LOADS)
            for r in range(2):
                ch.step(pool_.tensor_scalar(gated_rows[:, r, :], norm_rows[:, r, :], gates[:, 1:2], 1.0, ALU.mult,
                                            ALU.mult))
            ch.wait()
            pool.wait_ge(b_on, B)

            def rstd(b):
                need(pool, c_var, b + 1)
                ch.step(pool_.tensor_tensor(rstd_c[:, 1, :], mv_c[:, :, 1], eps6[:, 0:6], ALU.add))
                ch.wait()
                ch.step(pool_.tensor_tensor(rstd_c[:, 0, :], rstd_c[:, 1, :], half[:, 0:6], ALU.pow))
                ch.wait()
                ch.step(pool_.tensor_tensor(rstd_c[:, 1, :], rstd_c[:, 0, :], mv_c[:, :, 0], ALU.mult))
                ch.wait()
                pool_.tensor_tensor(rstd_c[:, 1, :], rstd_c[:, 1, :], minus1[:, 0:6], ALU.mult).then_inc(c_rstd, 1)

            def add_beta(b):
                need(pool, c_kvg, b + 1)
                rows4 = norm_rows[:, 1:2, :].broadcast_to([P, 2 * NT, D])
                kv4 = kv_c[:, :, :, :].rearrange("p t w d -> p (t w) d")
                pool_.tensor_tensor(kv4, kv4, rows4, ALU.add).then_inc(c_kvb, 1)

            def out_rstd(b):
                need(pool, c_yvar, b + 1)
                ch.step(pool_.tensor_tensor(rstd_y[:, 0, :], mv_y[:, :, 1], eps6[:, 0:NT], ALU.add))
                ch.wait()
                pool_.tensor_tensor(rstd_y[:, 1, :], rstd_y[:, 0, :], half[:, 0:NT], ALU.pow).then_inc(c_yrstd, 1)

            def residual(b):
                need(pool, c_yg, b + 1)
                ch.step(pool_.tensor_tensor(y_c[:, :, :], y_c[:, :, :],
                                            gated_rows[:, 1:2, :].broadcast_to([P, NT, D]), ALU.add))
                ch.wait()
                pool.sem_inc(held_pool, 1)
                xt = x_all[:, bass.ds(NT * b, NT), :]
                pool_.tensor_tensor(xt, xt, y_c[:, :, :], ALU.add).then_inc(c_x, 1)

            def turn(i, first=True, second=True, third=True, past=True):
                if second:
                    add_beta(i + 1)
                if past:
                    token_rstd(2 * B + i - 1)
                if first:
                    rstd(i + 2)
                if third:
                    out_rstd(i)
                    residual(i)

            turn(-2, second=False, third=False, past=False)
            token_rstd(2 * B - 1)
            turn(-1, third=False, past=False)
            turn(0, past=False)
            fore, per = ch.n, 6
            with pool.Fori(1, B - 2) as i:
                ch.base, ch.n = fore + per * (i - 1), 0
                turn(i)
                assert ch.n == per
            ch.leave(fore + per * (B - 3))
            turn(B - 2, first=False)
            turn(B - 1, first=False, second=False)
            token_rstd(3 * B - 1)

        def dve_late(dve, ch, token_stats, token_norm):
            def hold(semaphore, value):
                dve.wait_ge(semaphore, value)
                if not isinstance(value, int):
                    dve.sem_inc(held, 1)

            dve.wait_ge(a_x, B * NT)
            token_stats(B - 1)
            token_norm(B - 1, B - 1)
            dve.wait_ge(b_in, 16 * B_LOADS)
            ch.step(dve_.tensor_scalar(head_tab[:, :, 0:2 * DH], head_tab[:, :, 0:2 * DH], DH ** -0.5, None, ALU.mult))
            dve_.tensor_scalar(head_tab[:, :, 7 * DH:7 * DH + 1], head_tab[:, :, 7 * DH:7 * DH + 1], DH ** -0.5, None,
                               ALU.mult).then_inc(b_scaled, 1)
            ch.step(dve_.memset(neg_at[:, :], -1e6))
            dve.wait_ge(r_ps, 1)
            ch.step(dve_.scalar_tensor_tensor(logits[:, :], banks[0][0:B, 0:NH_B], 1.0 / S, b_router[:, :], ALU.mult,
                                              ALU.add))
            ch.wait()
            ch.step(dve_.max(top[:, :], logits[:, :]))
            ch.wait()
            ch.step(dve_.max_index(top_at[:, :], top[:, :], logits[:, :]))
            ch.wait()
            ch.step(dve_.tensor_scalar(neg_at[:, 0:NA_B], top_at[:, 0:NA_B], -1.0, None, ALU.mult))
            ch.wait()
            ch.step(dve_.max(sorted_at[:, :], neg_at[:, :]))
            ch.wait()
            dve_.tensor_scalar(chosen8[:, :], sorted_at[:, 0:NA_B], -1.0, None, ALU.mult).then_inc(r_chosen, 1)

            dve.wait_ge(b_bias, 1)

            def residual(b):
                need(dve, b_wo_ps, b + 1)
                xt = x_all[:, bass.ds(NT * b, NT), :]
                dve_.scalar_tensor_tensor(xt, banks[7][:, :].rearrange("p (t n) -> p t n", n=D), gates[:, 2:3], xt,
                                          ALU.mult, ALU.add).then_inc(b_x, 1)

            def attend(b, par, first=False):
                def low(j):
                    need(dve, b_hi, NA_B * b + j + 1)
                    w, bank = head_w[:, par, j, :], banks[j % 2]
                    dve_.scalar_tensor_tensor(q_low[:, j, :], bank[:, 0:S], w[:, BIAS_B:BIAS_B + 1], q_high[:, j, :],
                                              ALU.add, ALU.subtract)
                    kl = k_both[DH:P, j, :]
                    dve_.scalar_tensor_tensor(kl, bank[DH:P, S:2 * S], w[DH:P, BIAS_B + 1:BIAS_B + 2], kl,
                                              ALU.add, ALU.subtract).then_inc(b_lo, 1)

                def maximum(j):
                    need(dve, b_s_ps, NA_B * b + j + 1)
                    dve_.tensor_reduce(negmax_b[:, j, :], banks[2 + j % 2][:, :].rearrange("p (t n) -> p t n", n=S),
                                       AX, ALU.max, negate=True).then_inc(b_max, 1)

                def copy_pT(j):
                    need(dve, b_pT_ps, NA_B * b + j + 1)
                    need(dve, b_pv, NA_B * b + j - 1)
                    dve_.tensor_copy(probsT[:, j % 2, :], banks[4 + j % 2][:, :]).then_inc(b_pT[0], 1)

                low(0)
                low(1)
                if not first:
                    residual(b - 1)
                maximum(0)
                low(2)
                maximum(1)
                low(3)
                copy_pT(0)
                maximum(2)
                if not first:
                    if not isinstance(b, int):
                        token_norm(b - 2, B + b - 2)
                    hold(b_x, b)
                    token_stats(b - 1)
                maximum(3)
                copy_pT(2)
                xt = x_all[:, bass.ds(NT * b, NT), :]
                ch.step(dve_.tensor_tensor(xt, xt, bo_b[:, :].unsqueeze(1).broadcast_to([P, NT, D]), ALU.add))
                need(dve, b_pv, NA_B * b + NA_B)
                ch.step(dve_.reciprocal(recip_b[:, :], rowsum_b[:, :, :].rearrange("p t h -> p (t h)")))
                ch.wait()
                need(dve, b_oT_ps, b)
                ch.step(dve_.tensor_tensor(heads(o_b[:, :, :].rearrange("p t n -> p (t n)")), heads(banks[7][:, :]),
                                           across(recip_b[:, :], DH), ALU.mult))
                ch.wait()
                for t in range(NT):
                    o = heads(o_b[:, t, :])
                    last = dve_.tensor_tensor(o, o, head_w[:, par, :, 10 * DH:11 * DH], ALU.add)
                last.then_inc(b_on, 1)
            attend(0, 0, first=True)
            attend(1, 1)
            fore, per = ch.n, 5
            with dve.Fori(1, B // 2) as i:
                for par in range(2):
                    ch.base, ch.n = fore + per * (2 * i + par - 2), 0
                    attend(2 * i + par, par)
                    assert ch.n == per, ch.n
            ch.leave(fore + per * (B - 2))
            residual(B - 1)

            token_norm(B - 2, 2 * B - 2)
            dve.wait_ge(b_x, B)
            token_stats(B - 1)

            dve.wait_ge(consts, 1)
            ch.step(dve_.tensor_reduce(parity[:, :], head_cols[:, :].rearrange("p (h a) -> p a h", a=2), AX, ALU.add))
            dve.wait_ge(c_w_in, 16 * C_LOADS)

            def stats(b):
                need(dve, c_q_ps, b + 1)
                for t in range(NT):
                    ch.step(dve_.bn_stats(stat_c[:, t, :], banks[1][:, D * t:D * t + D]))
                need(dve, c_kv_ps, b + 1)
                for t in range(NT):
                    for w in range(2):
                        ch.step(dve_.bn_stats(stat_c[:, 2 + 2 * t + w, :], banks[2 + t][:, D * w:D * w + D]))
                hold(dve_steps, ch.base + ch.n)
                if not isinstance(b, int) or b:
                    hold(c_kvn, b)
                for i in range(6):
                    last = dve_.bn_aggr(mv_c[:, i, :], stat_c[:, i, :])
                last.then_inc(c_var, 1)

            def times_gamma(b):
                need(dve, c_kvn, b + 1)
                kv4 = kv_c[:, :, :, :].rearrange("p t w d -> p (t w) d")
                dve_.tensor_tensor(kv4, kv4, norm_rows[:, 0:1, :].broadcast_to([P, 2 * NT, D]), ALU.mult)\
                    .then_inc(c_kvg, 1)

            def queries(b):
                need(dve, c_relu, b + 1)
                dve_.tensor_scalar(qpT_c[:, :, :], qpT_c[:, :, :], 1e-6, None, ALU.add).then_inc(c_qp, 1)

            def keys_values(b):
                need(dve, c_kvb, b + 1)
                need(dve, c_sum_ps, b)
                ch.step(dve_.tensor_scalar(kp_c[:, :, :], kv_c[:, :, 0, :], 0.0, 1e-6, ALU.max, ALU.add))
                ch.wait()
                for t in range(NT):
                    last = dve_.tensor_scalar(kp_c[:, t, :], kp_c[:, t, :], em[:, bass.ds(NT * b + t, 1)], None,
                                              ALU.mult)
                last.then_inc(c_kp, 1)

            def own_sums(b):
                need(dve, c_sum_ps, b + 1)
                need(dve, c_num_ps, b)
                for dt in range(ND):
                    at = S * dt + P
                    dve_.tensor_tensor(kv_own[:, dt, :], banks[5][:, S * dt:at], head_block[:, :], ALU.mult)
                    last = dve_.tensor_tensor(k_own[:, dt, :], banks[5][:, at:at + 1].broadcast_to([P, P]),
                                              head_block[:, :], ALU.mult)
                last.then_inc(c_kvm, 1)

            def divide(b):
                need(dve, c_num_ps, b + 1)
                for i, bank in enumerate((7, 6)):
                    for dt in range(ND):
                        runs = banks[bank][:, S * dt:S * dt + S].rearrange("p (r n) -> p n r", n=DC).unsqueeze(2)
                        to = turned_c[:, i, DC * dt:DC * dt + DC, :].rearrange("p n (a r) -> p n a r", a=2)
                        ch.step(dve_.transpose(to, runs.broadcast_to([P, DC, 2, DC])))
                        if i and dt == 0:
                            ch.step(dve_.tensor_scalar(den_c[:, 0, :], turned_c[:, 0, :, 0], parity[:, 0:1], 1e-6,
                                                       ALU.mult, ALU.add))
                    ch.wait()
                ch.step(dve_.scalar_tensor_tensor(den_c[:, 0, :], turned_c[:, 0, :, DC], parity[:, 1:2],
                                                  den_c[:, 0, :], ALU.mult, ALU.add))
                need(dve, c_aT_ps, b)
                att = att_c[:, :, :].rearrange("p k (n e) -> p (k n) e", e=DC)
                turned = turned_c[:, 1, :, :]
                ch.step(dve_.tensor_scalar(att, turned[:, :, 0:DC], parity[:, 0:1], None, ALU.mult))
                ch.wait()
                ch.step(dve_.reciprocal(den_c[:, 1, :], den_c[:, 0, :]))
                ch.step(dve_.scalar_tensor_tensor(att, turned[:, :, DC:], parity[:, 1:2], att, ALU.mult, ALU.add))
                ch.wait()
                dve_.tensor_tensor(att, att, across(den_c[:, 1, :], DC), ALU.mult).then_inc(c_att, 1)

            def out_stats(b):
                need(dve, c_y_ps, b + 1)
                need(dve, c_x, b)
                ch.step(dve_.tensor_tensor(y_c[:, :, :], banks[5][:, :].rearrange("p (t n) -> p t n", n=D),
                                           norm_rows[:, 2:3, :].broadcast_to([P, NT, D]), ALU.add))
                ch.wait()
                for t in range(NT):
                    ch.step(dve_.bn_stats(stat_y[:, t, :], y_c[:, t, :]))
                hold(dve_steps, ch.base + ch.n)
                for t in range(NT):
                    last = dve_.bn_aggr(mv_y[:, t, :], stat_y[:, t, :])
                last.then_inc(c_yvar, 1)

            def out_norm(b):
                need(dve, c_yrstd, b + 1)
                for t in range(NT):
                    ch.step(dve_.tensor_scalar(y_c[:, t, :], y_c[:, t, :], mv_y[:, t, 0:1], rstd_y[:, 1, t:t + 1],
                                               ALU.subtract, ALU.mult))
                ch.wait()
                dve_.tensor_tensor(y_c[:, :, :], y_c[:, :, :], gated_rows[:, 0:1, :].broadcast_to([P, NT, D]),
                                   ALU.mult).then_inc(c_yg, 1)

            def turn(i, first=True, second=True, third=True, past=True):
                if second:
                    times_gamma(i + 1)
                if past:
                    hold(c_x, i)
                    token_stats(i - 1)
                if third:
                    divide(i)
                if first:
                    stats(i + 2)
                if past:
                    token_norm(i - 1, 2 * B + i - 1)
                if second:
                    queries(i + 1)
                if third:
                    out_stats(i)
                if second:
                    keys_values(i + 1)
                if third:
                    out_norm(i)
                if second:
                    own_sums(i + 1)

            turn(-2, second=False, third=False, past=False)
            token_norm(B - 1, 2 * B - 1)
            turn(-1, third=False, past=False)
            turn(0, past=False)
            fore, per = ch.n, 23
            with dve.Fori(1, B - 2) as i:
                ch.base, ch.n = fore + per * (i - 1), 0
                turn(i)
                assert ch.n == per, ch.n
            ch.leave(fore + per * (B - 3))
            turn(B - 2, first=False)
            turn(B - 1, first=False, second=False)

            dve.wait_ge(c_x, B)
            token_stats(B - 1)
            token_norm(B - 1, 3 * B - 1)
            ch.step(dve_.memset(keyed[:, :, :, S:S + 1], 0.5))
            dve.wait_ge(e_logit_ps, 1)
            flat = gate_e[:, :, :, :].rearrange("p t b e -> p (t b) e")
            dve_.tensor_scalar(gate_e[:, :, :, :].rearrange("p t b e -> p (t b e)"),
                               banks[0][:, 0:B * NT * E], 1e-6, None, ALU.max).then_inc(e_gate, 1)
            start = ch.n

            def sinkhorn(i):
                need(dve, e_col_ps, i + 1)
                ch.step(dve_.reciprocal(recip_col[:, :, :], banks[1][:, 0:B * E].rearrange("p (b e) -> p b e", e=E)))
                ch.wait()
                ch.step(dve_.tensor_tensor(gate_e[:, :, :, :], gate_e[:, :, :, :],
                                           recip_col[:, :, :].unsqueeze(1).broadcast_to([P, NT, B, E]), ALU.mult))
                ch.wait()
                ch.step(dve_.tensor_reduce(sum_row[:, 0, :], flat, AX, ALU.add))
                ch.wait()
                ch.step(dve_.reciprocal(sum_row[:, 1, :], sum_row[:, 0, :]))
                ch.wait()
                dve_.tensor_tensor(flat, flat, across(sum_row[:, 1, :], E), ALU.mult).then_inc(e_gate, 1)

            sinkhorn(0)
            per = ch.n - start
            with dve.Fori(1, SINKHORN) as i:
                ch.base, ch.n = start + per * i, 0
                sinkhorn(i)
            ch.leave(start + per * SINKHORN)

            dve.wait_ge(e_gT_ps, 1)
            ch.step(dve_.tensor_copy(gateT[:, :], banks[2][0:B * E, 0:S]))
            ch.wait()
            for r in range(M // 8):
                cut = slice(8 * r, 8 * r + 8)
                ch.step(dve_.max(picked[:, cut], gateT[:, :]))
                ch.wait()
                ch.step(dve_.max_index(picked_at[:, cut], picked[:, cut], gateT[:, :]))
                ch.wait()
                if r < M // 8 - 1:
                    ch.step(dve_.match_replace(gateT[:, :], picked[:, cut], gateT[:, :], -1.0))
                    ch.wait()
            ch.step(dve_.tensor_copy(pick_rows[:, 0, :], picked_at[:, :]))
            ch.step(dve_.tensor_copy(pick_rows[:, 1, :], picked[:, :]))
            ch.wait()
            dve_.tensor_tensor(spread16[:, :, :], pick_rows[:, 0:1, :].broadcast_to([B * E, B * E, M]),
                               ident[0:B * E, 0:B * E].unsqueeze(2).broadcast_to([B * E, B * E, M]), ALU.mult)\
                .then_inc(e_picks, 1)
            dve.wait_ge(e_cols_ps, 1)
            turned = banks[3][0:M, 0:2 * B * E].rearrange("m (w g j) -> m w g j", w=2, j=4)
            for j in range(4):
                last = dve_.tensor_copy(slot_cols[M * j:M * j + M, :, :], turned[:, :, :, j])
            ch.step(last)
            dve.wait_ge(e_rows_ps, 1)
            for b in range(B + 1):
                if b < B:
                    for t in range(NT):
                        slots = banks[4 + b // 2][:, S * (b % 2):S * (b % 2) + S]
                        ch.step(dve_.scalar_tensor_tensor(keyed[:, b % 2, t, 0:S], slots, token_col[:, t:t + 1],
                                                          slot_key[:, :, :].rearrange("p e m -> p (e m)"),
                                                          ALU.is_equal, ALU.mult))
                if b:
                    for t in range(NT):
                        last = dve_.tensor_scalar(take[:, b - 1, t, :], keyed[:, (b - 1) % 2, t, 0:S],
                                                  winner[:, (b - 1) % 2, t:t + 1], None, ALU.is_equal)
                    last.then_inc(e_take, 1)
                if b < B:
                    ch.wait()
                    ch.step(dve_.tensor_reduce(winner[:, b % 2, :], keyed[:, b % 2, :, :], AX, ALU.max))
                    ch.wait()
            for g in range(2 * B):
                dve_.tensor_scalar(put[:, g // 2, g % 2, :], token_row[:, :], slot_cols[:, 0, g:g + 1], None,
                                   ALU.is_equal).then_inc(e_put, 1)
            for e in range(0, E, 2):
                dve.wait_ge(e_yT_ps, e + 1)
                dve_.tensor_copy(yT[:, :, :, e, :],
                                 banks[4 + e % 4][:, :].rearrange("p (a b m) -> p a b m", a=ND, m=M))\
                    .then_inc(e_yT[0], 1)
            for b in range(B):
                dve.wait_ge(e_o_ps, b + 1)
                xt = x_all[:, NT * b:NT * b + NT, :]
                dve_.scalar_tensor_tensor(xt, banks[2 + b % 2][:, :].rearrange("p (t n) -> p t n", n=D), gates[:, 3:4],
                                          xt, ALU.mult, ALU.add).then_inc(e_x, 1)

        def act_late(act, copy_hT):
            copy_hT(B - 1, B - 1, 0, sums=True)

            def copy_oT(b):
                need(act, b_oT_ps, b + 1)
                act_.activation(oT_b[:, :, :], banks[6][:, :].rearrange("p (k n) -> p k n", n=S), ACT.Copy)\
                    .then_inc(b_oT, 1)

            def attend(b, par, first=False):
                def high(j):
                    need(act, b_qk_ps, NA_B * b + j + 1)
                    w, bank = head_w[:, par, j, :], banks[j % 2]
                    act_.activation(q_high[:, j, :], bank[:, 0:S], ACT.Identity, bias=w[:, BIAS_B:BIAS_B + 1])
                    act_.activation(k_both[:, j, :], bank[:, S:2 * S], ACT.Identity,
                                    bias=w[:, BIAS_B + 1:BIAS_B + 2]).then_inc(b_hi, 1)

                def exps(j):
                    need(act, b_max, NA_B * b + j + 1)
                    need(act, b_pT_ps, NA_B * b + j - 1)
                    for t in range(NT):
                        last = act_.activation(probs[:, j % 2, S * t:S * t + S], banks[2 + j % 2][:, S * t:S * t + S],
                                               ACT.Exp, bias=negmax_b[:, j, t:t + 1], scale=1.0,
                                               accum_out=rowsum_b[:, t, j:j + 1])
                    last.then_inc(b_ex, 1)

                def copy_pT(j):
                    need(act, b_pT_ps, NA_B * b + j + 1)
                    need(act, b_pv, NA_B * b + j - 1)
                    act_.activation(probsT[:, j % 2, :], banks[4 + j % 2][:, :], ACT.Copy).then_inc(b_pT[1], 1)

                def copy_v():
                    need(act, b_v_ps, b + 1)
                    act_.activation(v_b[:, :, :], banks[6][:, :].rearrange("p (t n) -> p t n", t=NT), ACT.Copy)\
                        .then_inc(b_v, 1)

                high(0)
                if not first:
                    copy_oT(b - 1)
                high(1)
                if not first:
                    copy_v()
                high(2)
                exps(0)
                high(3)
                exps(1)
                if first:
                    copy_v()
                exps(2)
                copy_pT(1)
                exps(3)
                copy_pT(3)
                if not isinstance(b, int):
                    copy_hT(b - 2, B + b - 2, 0)

            attend(0, 0, first=True)
            attend(1, 1)
            with act.Fori(1, B // 2) as i:
                for par in range(2):
                    attend(2 * i + par, par)
            copy_oT(B - 1)
            copy_hT(B - 2, 2 * B - 2, 4)

            def hold(semaphore, value):
                act.wait_ge(semaphore, value)
                if not isinstance(value, int):
                    act.sem_inc(held_act, 1)

            def current(b, par):
                hold(n_hT, B + b + 1)
                if not isinstance(b, int) or b >= 2:
                    hold(c_q_ps, b - 1)
                act_.activation(hT[:, par, :, :].unsqueeze(1), hT_all[:, bass.ds(b, 1), :, :], ACT.Copy)
                act_.activation(ctx_b[:, par, :, :], c_all[:, bass.ds(NT * b, NT), :], ACT.Copy).then_inc(c_cur, 1)

            def norm_q(b):
                need(act, c_rstd, b + 1)
                need(act, c_qT_ps, b)
                for t in range(NT):
                    last = act_.activation(qn_c[:, t, :], banks[1][:, D * t:D * t + D], ACT.Identity,
                                           bias=rstd_c[:, 1, t:t + 1], scale=rstd_c[:, 0, t:t + 1])
                last.then_inc(c_qn, 1)

            def masked_values(b):
                hold(c_kvb, b + 1)
                if not isinstance(b, int) or b:
                    hold(c_sum_ps, b)
                for t in range(NT):
                    last = act_.activation(v_ones[:, t, :, 0:P], kv_c[:, t, 1, :].rearrange("p (a n) -> p a n", n=P),
                                           ACT.Copy, scale=em[:, bass.ds(NT * b + t, 1)])
                last.then_inc(c_vm, 1)

            def copy_ctxT(b):
                need(act, c_cT_ps, b + 1)
                act_.activation(ctxT[:, :, :], banks[0][:, :].rearrange("p (k n) -> p k n", n=S), ACT.Copy)\
                    .then_inc(c_cT, 1)

            def norm_kv(b):
                need(act, c_rstd, b + 1)
                need(act, c_kp, b)
                need(act, c_vm, b)
                for t in range(NT):
                    for w in range(2):
                        i = 2 + 2 * t + w
                        last = act_.activation(kv_c[:, t, w, :], banks[2 + t][:, D * w:D * w + D], ACT.Identity,
                                               bias=rstd_c[:, 1, i:i + 1], scale=rstd_c[:, 0, i:i + 1])
                last.then_inc(c_kvn, 1)

            def relu(b):
                need(act, c_qT_ps, b + 1)
                need(act, c_num_ps, b)
                for dt in range(ND):
                    last = act_.activation(qpT_c[:, dt, :], banks[4][:, S * dt:S * dt + S], ACT.Relu,
                                           bias=norm_cols[:, 1, dt:dt + 1], scale=norm_cols[:, 0, dt:dt + 1])
                last.then_inc(c_relu, 1)

            def copy_attT(b):
                need(act, c_aT_ps, b + 1)
                act_.activation(attT_c[:, :, :], banks[5][:, :].rearrange("p (k n) -> p k n", n=S), ACT.Copy)\
                    .then_inc(c_aT, 1)

            def turn(i, par, first=True, second=True, third=True, past=True):
                if second:
                    norm_q(i + 1)
                    norm_kv(i + 1)
                if first:
                    current(i + 2, par)
                if second:
                    relu(i + 1)
                if first:
                    copy_ctxT(i + 2)
                if third:
                    copy_attT(i)
                if second:
                    masked_values(i + 1)
                if past:
                    copy_hT(i - 1, 2 * B + i - 1, 6, keep=True)

            act.wait_ge(c_w_in, 16 * C_LOADS)
            act.wait_ge(b_on, B)
            turn(-2, 0, second=False, third=False, past=False)
            copy_hT(B - 1, 2 * B - 1, 5)
            turn(-1, 1, third=False, past=False)
            turn(0, 0, past=False)
            turn(1, 1)
            with act.Fori(1, B // 2 - 1) as i:
                for par in range(2):
                    turn(2 * i + par, par)
            turn(B - 2, 0, first=False)
            turn(B - 1, 1, first=False, second=False)

            copy_hT(B - 1, 3 * B - 1, 4, keep=True)
            for b in range(B):
                act.wait_ge(e_xg_ps, b + 1)
                act_.activation(xgT[:, :, :, b, :], banks[b % 2][:, :].rearrange("p (a e m) -> p a e m", a=ND, m=M),
                                ACT.Copy).then_inc(e_xg, 1)
            for e in range(1, E, 2):
                act.wait_ge(e_yT_ps, e + 1)
                act_.activation(yT[:, :, :, e, :], banks[4 + e % 4][:, :].rearrange("p (a b m) -> p a b m", a=ND, m=M),
                                ACT.Copy).then_inc(e_yT[1], 1)
            for b in range(B):
                act.wait_ge(e_y_ps, b + 1)
                if b >= 2:
                    act.wait_ge(e_o_ps, b - 1)
                for half_e in range(2):
                    g = 2 * b + half_e
                    last = act_.activation(y_e[:, b % 2, half_e, :], banks[b % 2][:, D * half_e:D * half_e + D],
                                           ACT.Copy, scale=slot_cols[:, 1, g:g + 1])
                last.then_inc(e_y, 1)

        def pe_late(pe, transposes_h):
            transposes_h(B - 1, 0)
            pe.wait_ge(n_hT, B)
            pe.wait_ge(b_in, 16 * B_LOADS)
            for k in range(ND):
                last = pe_.matmul(banks[0][0:B, 0:NH_B], h_sum[:, k, :], w_router[:, k, :], start=k == 0,
                                  stop=k == ND - 1)
            last.then_inc(r_ps, 1)
            pe.wait_ge(r_chosen, 1)

            def transposes_o(b):
                need(pe, b_on, b + 1)
                for k in range(ND):
                    for t in range(NT):
                        last = pe_.transpose(banks[6][:, S * k + P * t:S * k + P * t + P],
                                             o_b[:, t, P * k:P * k + P], ident[:, :])
                last.then_inc(b_oT_ps, 1)

            def out_project(b):
                need(pe, b_oT, b + 1)
                for t in range(NT):
                    for k in range(ND):
                        last = pe_.matmul(banks[7][:, D * t:D * t + D], oT_b[:, k, P * t:P * t + P], wo_b[:, k, :],
                                          start=k == 0, stop=k == ND - 1)
                last.then_inc(b_wo_ps, 1)

            def attend(b, par, first=False):
                hb = hT[:, par, :, :]

                def project_qk(j):
                    need(pe, b_sel, NA_B * b + j + 1)
                    need(pe, b_lo, NA_B * b + j - 1)
                    if j == 0 and not isinstance(b, int):
                        need(pe, n_hT, B + b - 2)
                    for w in range(2):
                        for k in range(ND):
                            at = P * (ND * w + k)
                            twice = head_w[:, par, j, at:at + P]
                            last = pe_.matmul(banks[j % 2][:, S * w:S * w + S], twice, hb[:, k, :], start=k == 0,
                                              stop=k == ND - 1)
                    last.then_inc(b_qk_ps, 1)

                def project_v():
                    need(pe, b_sel, NA_B * b + NA_B)
                    for t in range(NT):
                        for k in range(ND):
                            at = DH * (8 + k)
                            last = pe_.matmul(banks[6][:, D * t:D * t + D], hb[:, k, P * t:P * t + P],
                                              head_w[:, par, :, at:at + DH], start=k == 0, stop=k == ND - 1)
                    last.then_inc(b_v_ps, 1)

                def scores_of(j):
                    need(pe, b_lo, NA_B * b + j + 1)
                    need(pe, b_ex, NA_B * b + j - 1)
                    for t in range(NT):
                        for v, q in enumerate((q_high, q_low)):
                            last = pe_.matmul(banks[2 + j % 2][:, S * t:S * t + S], q[:, j, P * t:P * t + P],
                                              k_both[:, j, :], start=v == 0, stop=v == 1)
                    last.then_inc(b_s_ps, 1)

                def transposes_p(j):
                    need(pe, b_ex, NA_B * b + j + 1)
                    need(pe, b_pT[j % 2], NA_B // 2 * b + j // 2)
                    for t in range(NT):
                        for k in range(NT):
                            last = pe_.transpose(banks[4 + j % 2][:, S * k + P * t:S * k + P * t + P],
                                                 probs[:, j % 2, S * t + P * k:S * t + P * k + P], ident[:, :])
                    last.then_inc(b_pT_ps, 1)

                def values(j):
                    need(pe, b_pT[j % 2], NA_B // 2 * b + j // 2 + 1)
                    if j == 0:
                        need(pe, b_v, b + 1)
                        need(pe, b_x, b)
                    for t in range(NT):
                        for k in range(NT):
                            at = D * t + DH * j
                            last = pe_.matmul(banks[7][:, at:at + DH],
                                              probsT[:, j % 2, S * k + P * t:S * k + P * t + P],
                                              v_b[:, k, DH * j:DH * j + DH], start=k == 0, stop=k == NT - 1)
                    last.then_inc(b_pv, 1)

                project_qk(0)
                if not first:
                    transposes_o(b - 1)
                project_qk(1)
                if not first:
                    out_project(b - 1)
                if not first:
                    project_v()
                scores_of(0)
                project_qk(2)
                scores_of(1)
                project_qk(3)
                if first:
                    project_v()
                transposes_p(0)
                scores_of(2)
                transposes_p(1)
                values(0)
                scores_of(3)
                transposes_p(2)
                values(1)
                transposes_p(3)
                if not isinstance(b, int):
                    need(pe, b_lo, NA_B * b + NA_B - 1)
                    transposes_h(B + b - 2, 0)
                values(2)
                values(3)

            attend(0, 0, first=True)
            attend(1, 1)
            with pe.Fori(1, B // 2) as i:
                for par in range(2):
                    attend(2 * i + par, par)
            transposes_o(B - 1)
            out_project(B - 1)
            transposes_h(2 * B - 2, 4)

            pe.wait_ge(c_w_in, 16 * C_LOADS)
            pe.wait_ge(consts, 1)

            def project(b, par):
                need(pe, c_cur, b + 1)
                for k in range(ND):
                    for t in range(NT):
                        last = pe_.transpose(banks[0][:, S * k + P * t:S * k + P * t + P],
                                             ctx_b[:, par, t, P * k:P * k + P], ident[:, :])
                last.then_inc(c_cT_ps, 1)
                for t in range(NT):
                    for k in range(ND):
                        last = pe_.matmul(banks[1][:, D * t:D * t + D], hT[:, par, k, P * t:P * t + P],
                                          w_c[:, 0, k, :], start=k == 0, stop=k == ND - 1)
                last.then_inc(c_q_ps, 1)
                need(pe, c_cT, b + 1)
                need(pe, c_kvn, b)
                for t in range(NT):
                    for k in range(ND):
                        last = pe_.matmul(banks[2 + t][:, :], ctxT[:, k, P * t:P * t + P], w_c[:, 1:3, k, :],
                                          start=k == 0, stop=k == ND - 1)
                last.then_inc(c_kv_ps, 1)

            def transposes_q(b):
                need(pe, c_qn, b + 1)
                need(pe, c_relu, b)
                if isinstance(b, int) and b == 0:
                    pe.wait_ge(n_hT, 2 * B - 1)
                for k in range(ND):
                    for t in range(NT):
                        last = pe_.transpose(banks[4][:, S * k + P * t:S * k + P * t + P],
                                             qn_c[:, t, P * k:P * k + P], ident[:, :])
                last.then_inc(c_qT_ps, 1)

            def keys_by_values(b):
                need(pe, c_kp, b + 1)
                need(pe, c_vm, b + 1)
                need(pe, c_yvar, b)
                for dt in range(ND):
                    for t in range(NT):
                        last = pe_.matmul(banks[5][:, S * dt:S * dt + P + 1], kp_c[:, t, P * dt:P * dt + P],
                                          v_ones[:, t, dt, :], start=t == 0, stop=t == NT - 1)
                last.then_inc(c_sum_ps, 1)

            def numerators(b):
                need(pe, c_qp, b + 1)
                need(pe, c_kvm, b + 1)
                need(pe, c_att, b)
                if not isinstance(b, int) or b >= 2:
                    need(pe, n_hT, 2 * B + b - 1)
                for bank, own in ((6, kv_own), (7, k_own)):
                    for dt in range(ND):
                        last = pe_.matmul(banks[bank][:, S * dt:S * dt + S], own[:, dt, :], qpT_c[:, dt, :],
                                          start=True, stop=True)
                last.then_inc(c_num_ps, 1)

            def transposes_att(b):
                need(pe, c_att, b + 1)
                for k in range(ND):
                    for t in range(NT):
                        last = pe_.transpose(banks[5][:, S * k + P * t:S * k + P * t + P],
                                             att_c[:, t, P * k:P * k + P], ident[:, :])
                last.then_inc(c_aT_ps, 1)

            def out_project(b):
                need(pe, c_aT, b + 1)
                for t in range(NT):
                    for k in range(ND):
                        last = pe_.matmul(banks[5][:, D * t:D * t + D], attT_c[:, k, P * t:P * t + P],
                                          dense_c[:, k, :], start=k == 0, stop=k == ND - 1)
                last.then_inc(c_y_ps, 1)

            def gate_logits(b):
                for t in range(NT):
                    for k in range(ND):
                        at = E * (B * t + b)
                        last = pe_.matmul(banks[0][:, at:at + E], hT_all[:, b, k, P * t:P * t + P], w_gate[:, k, :],
                                          start=k == 0, stop=k == ND - 1)
                return last

            def turn(i, par, first=True, second=True, third=True, past=True, logits=()):
                if second:
                    transposes_q(i + 1)
                if third:
                    numerators(i)
                if first:
                    project(i + 2, par)
                if logits:
                    pe.wait_ge(n_hT, 2 * B + logits[-1] + 1)
                for b in logits:
                    gate_logits(b)
                if third:
                    transposes_att(i)
                    out_project(i)
                if past:
                    transposes_h(2 * B + i - 1, 6)
                if second:
                    keys_by_values(i + 1)

            turn(-2, 0, second=False, third=False, past=False)
            transposes_h(2 * B - 1, 5)
            pe.wait_ge(n_hT, 2 * B)
            turn(-1, 1, third=False, past=False)
            turn(0, 0, past=False)
            turn(1, 1)
            with pe.Fori(1, B // 2 - 1) as i:
                for par in range(2):
                    turn(2 * i + par, par)
            pe.wait_ge(e_in, 32)
            turn(B - 2, 0, first=False, logits=range(3))
            turn(B - 1, 1, first=False, second=False, logits=range(3, B - 2))

            pe.wait_ge(n_hT, 3 * B - 1)
            gate_logits(B - 2)
            transposes_h(3 * B - 1, 4)
            pe.wait_ge(n_hT, 3 * B)
            gate_logits(B - 1).then_inc(e_logit_ps, 1)

            def column_sums(i):
                need(pe, e_gate, i + 1)
                for t in range(NT):
                    last = pe_.matmul(banks[1][:, 0:B * E], ones[:, :], gate_e[:, t, :, :], start=t == 0,
                                      stop=t == NT - 1)
                last.then_inc(e_col_ps, 1)

            column_sums(0)
            with pe.Fori(1, SINKHORN) as i:
                column_sums(i)
            pe.wait_ge(e_gate, SINKHORN + 1)
            for t in range(NT):
                last = pe_.transpose(banks[2][0:B * E, P * t:P * t + P], gate_e[:, t, :, :], ident[:, :])
            last.then_inc(e_gT_ps, 1)
            pe.wait_ge(e_picks, 1)
            for w in range(2):
                last = pe_.transpose(banks[3][0:M, B * E * w:B * E * w + B * E], pick_rows[:, w, :],
                                     ident[0:B * E, 0:B * E])
            last.then_inc(e_cols_ps, 1)
            for g in range(4):
                n = B * E // 4
                last = pe_.matmul(banks[4 + g][:, :], ones16[:, :], spread16[:, n * g:n * g + n, :], start=True,
                                  stop=True)
            last.then_inc(e_rows_ps, 1)
            for b in range(B):
                pe.wait_ge(e_take, b + 1)
                if b >= 2:
                    pe.wait_ge(e_xg, b - 1)
                for k in range(ND):
                    for t in range(NT):
                        last = pe_.matmul(banks[b % 2][:, S * k:S * k + S], h_all[:, NT * b + t, P * k:P * k + P],
                                          take[:, b, t, :], start=t == 0, stop=t == NT - 1)
                last.then_inc(e_xg_ps, 1)
            pe.wait_ge(e_xg, B)
            for e in range(E):
                if e >= 4:
                    pe.wait_ge(e_yT[e % 2], (e - 4) // 2 + 1)
                for f in range(ND):
                    for k in range(ND):
                        last = pe_.matmul(banks[4 + e % 4][:, S * f:S * f + S], w_exp[:, e, k, P * f:P * f + P],
                                          xgT[:, k, e, :, :], start=k == 0, stop=k == ND - 1)
                last.then_inc(e_yT_ps, 1)
            pe.wait_ge(e_yT[0], E // 2)
            pe.wait_ge(e_yT[1], E // 2)
            pe.wait_ge(e_put, 2 * B)

            def slots_by_row(b):
                if b >= 2:
                    pe.wait_ge(e_y, b - 1)
                for half_e in range(2):
                    for f in range(ND):
                        last = pe_.transpose(banks[b % 2][:, D * half_e + P * f:D * half_e + P * f + P],
                                             yT[:, f, b, 4 * half_e:4 * half_e + 4, :], ident[:, :])
                last.then_inc(e_y_ps, 1)

            slots_by_row(0)
            for b in range(B):
                if b + 1 < B:
                    slots_by_row(b + 1)
                pe.wait_ge(e_y, b + 1)
                if b >= 2:
                    pe.wait_ge(e_x, b - 1)
                for t in range(NT):
                    for half_e in range(2):
                        last = pe_.matmul(banks[2 + b % 2][:, D * t:D * t + D], put[:, b, half_e, P * t:P * t + P],
                                          y_e[:, b % 2, half_e, :], start=half_e == 0, stop=half_e == 1)
                last.then_inc(e_o_ps, 1)

        block = ctx.enter_context(nc.Block())
        tok = "b (t p) d -> p (b t) d"
        rows = "(t p) n -> p t n"

        @block.sync
        def _(sp):
            x_v, c_v = io["x"].rearrange(tok, p=P), io["ctx_1024"].rearrange(tok, p=P)
            for i in range(4):
                sp.dma_start(c_all[:, 4 * i:4 * i + 4, :], c_v[:, 4 * i:4 * i + 4, :]).then_inc(c_in[i], 16)
                sp.dma_start(x_all[:, 4 * i:4 * i + 4, :], x_v[:, 4 * i:4 * i + 4, :]).then_inc(x_in[i], 16)
                if i == 0:
                    wkv = io["L0_xattn_Wkv"].rearrange(rows, p=P)
                    sp.dma_start(wkv_a[:, :, 0:INNER], wkv[:, :, 0:INNER]).then_inc(wk_in, 16)
                    sp.dma_start(wq_a[:, :, :], io["L0_xattn_Wq"].rearrange(rows, p=P)).then_inc(wq_in, 16)
                    sp.dma_start(wkv_a[:, :, INNER:], wkv[:, :, INNER:]).then_inc(wv_in, 16)
                if i == 1:
                    sp.dma_start(wo_a[:, :, :], io["L0_xattn_Wo"].rearrange(rows, p=P)).then_inc(w2_in, 16)
            sp.dma_start(head_tab[:, :, 0:6 * DH], io["head_weights"]).then_inc(b_in, 16)
            sp.dma_start(head_tab[:, :, 6 * DH:7 * DH],
                         io["L0_ffn_bv"].rearrange("(h d) -> h d", d=DH).unsqueeze(0).broadcast_to([P, NH_B, DH]))\
                .then_inc(b_in, 16)
            sp.dma_start(head_tab[:, :, 7 * DH:ROW_B], io["head_biases"]).then_inc(b_in, 16)
            sp.dma_start(w_router[:, :, :], io["L0_ffn_Wr"].rearrange(rows, p=P)).then_inc(b_in, 16)
            sp.dma_start(b_router[:, :], io["L0_ffn_br"].unsqueeze(0).broadcast_to([B, NH_B])).then_inc(b_in, 16)
            sp.dma_start(wo_b[:, :, :], io["L0_ffn_Wo"].rearrange(rows, p=P)).then_inc(b_in, 16)
            sp.dma_start(bo_b[:, :], io["L0_ffn_bo"].unsqueeze(0).broadcast_to([P, D])).then_inc(b_in, 16)
            for i, w in enumerate(("wq", "wk", "wv")):
                sp.dma_start(w_c[:, i, :, :], io[f"L1_xattn_{w}"].rearrange(rows, p=P)).then_inc(c_w_in, 16)
            sp.dma_start(dense_c[:, :, :], io["L1_xattn_dense_w"].rearrange(rows, p=P)).then_inc(c_w_in, 16)
            for i, w in enumerate(("ln_gamma", "ln_beta", "dense_b")):
                sp.dma_start(norm_rows[:, i, :], io[f"L1_xattn_{w}"].unsqueeze(0).broadcast_to([P, D]))\
                    .then_inc(c_w_in, 16)
            sp.dma_start(norm_cols[:, :, :], io["norm_cols"]).then_inc(c_w_in, 16)
            sp.dma_start(em[:, :], io["em"]).then_inc(c_w_in, 16)
            sp.dma_start(w_gate[:, :, :], io["L1_ffn_gate_w"].rearrange(rows, p=P)).then_inc(e_in, 16)
            sp.wait_ge(r_chosen, 1)
            sp.dma_start(chosen[0:1, :], chosen8[:, :]).then_inc(r_sent, 16)
            sp.wait_ge(b_sel, NA_B * B)
            sp.dma_start(w_exp[:, :, :, :], io["L1_ffn_experts"].rearrange("e (t p) n -> p e t n", p=P))\
                .then_inc(e_in, 16)
            out_v = io["out"].rearrange(tok, p=P)
            for b in range(B):
                sp.wait_ge(e_x, b + 1)
                sp.dma_start(out_v[:, NT * b:NT * b + NT, :], x_all[:, NT * b:NT * b + NT, :]).then_inc(out_done, 16)
            sp.wait_ge(out_done, 16 * B)

        @block.gpsimd
        def _(pool):
            ch = Chain(pool, pool_steps)
            ch.step(pool_.memset(ident[:, :], 0.0))
            ch.step(pool_.memset(half[:, :], -0.5))
            ch.step(pool_.memset(eps5[:, :], 1e-5))
            ch.step(pool_.memset(eps6[:, :], 1e-6))
            ch.step(pool_.memset(ones[:, :], 1.0))
            ch.step(pool_.memset(ones16[:, :], 1.0))
            ch.step(pool_.memset(v_ones[:, :, :, :], 1.0))
            ch.step(pool_.memset(head_block[:, :], 1.0))
            ch.step(pool_.memset(head_cols[:, :], 1.0))
            ch.step(pool_.iota(token_row[:, :], [[1, S]], base=0, channel_multiplier=0,
                               allow_small_or_imprecise_dtypes=True))
            ch.step(pool_.iota(token_col[:, :], [[P, NT]], base=0, channel_multiplier=1,
                               allow_small_or_imprecise_dtypes=True))
            ch.step(pool_.iota(slot_key[:, :, :], [[1, E], [E, M]], base=1, channel_multiplier=0,
                               allow_small_or_imprecise_dtypes=True))
            ch.wait()
            blocks = head_block[:, :].rearrange("p (h c) -> p h c", c=DC)
            for view, inner in ((blocks, [[0, DC]]), (head_cols[:, :], [])):
                for base, sign in ((0, 1), (DC - 1, -1)):
                    ch.step(pool_.affine_select(out=view, in_=view, compare_op=ALU.is_ge, fill=0.0, base=base,
                                                pattern=[[-sign * DC, HP_C]] + inner, channel_multiplier=sign))
                    ch.wait()
            pool_.memset(minus1[:, :], -1.0).then_inc(consts, 1)
            ch.wait()
            ch.step(pool_.affine_select(out=ident[:, :], in_=ident[:, :], compare_op=ALU.not_equal, fill=1.0, base=0,
                                        pattern=[[-1, P]], channel_multiplier=1))
            ch.wait()
            pool_.tensor_copy(ident16[:, :], ident[:, :]).then_inc(ident_ready, 1)

            def rstd(b):
                need(pool, a_var, b + 1)
                need(pool, a_xn, b)
                ch.step(pool_.tensor_tensor(tiny_a[:, 0, :], mv_a[:, :, 1], eps5[:, 0:KT], ALU.add))
                ch.wait()
                ch.step(pool_.tensor_tensor(rstd_a[:, :], tiny_a[:, 0, :], half[:, 0:KT], ALU.pow))
                ch.wait()
                lat, t = rstd_a[:, NT:KT], tiny_a[:, 1, NT:KT]
                ch.step(pool_.tensor_tensor(t, lat, lat, ALU.mult))
                ch.wait()
                ch.step(pool_.tensor_tensor(t, t, mv_a[:, NT:KT, 1], ALU.mult))
                ch.wait()
                ch.step(pool_.tensor_tensor(t, t, eps5[:, 0:NT], ALU.add))
                ch.wait()
                ch.step(pool_.tensor_tensor(t, t, half[:, 0:NT], ALU.pow))
                ch.wait()
                pool_.tensor_tensor(lat, lat, t, ALU.mult).then_inc(a_rstd, 1)

            def norms(b, i):
                need(pool, a_ss, 6 * b + i + 1)
                pool_.tensor_tensor(rnorm[:, i, :], sumsq[:, i, :], half[:, 0:HA], ALU.pow).then_inc(a_rn, 1)

            def low(b, i):
                need(pool, a_hi, 6 * b + i + 1)
                dst = kk16[:, i, :, :] if i < KT else qq16[:, i - KT, :, :]
                pool_.tensor_tensor(dst[:, :, DH:2 * DH], heads(normed[:, i % 2, :]), dst[:, :, 0:DH],
                                    ALU.subtract).then_inc(a_lo, 1)

            def out_rstd(b, qt):
                need(pool, a_ovar, NT * b + qt + 1)
                ch.step(pool_.tensor_tensor(rstd_o[:, 0:1], mv_o[:, 1:2], eps5[:, 0:1], ALU.add))
                ch.wait()
                pool_.tensor_tensor(rstd_o[:, 1:2], rstd_o[:, 0:1], half[:, 0:1], ALU.pow).then_inc(a_orstd, 1)

            def residual(b, qt):
                need(pool, a_y, NT * b + qt + 1)
                ch.step(pool_.tensor_tensor(y_a[:, :], y_a[:, :], ln_o[:, 0, :], ALU.mult))
                ch.wait()
                ch.step(pool_.tensor_tensor(y_a[:, :], y_a[:, :], ln_o[:, 1, :], ALU.add))
                ch.wait()
                pool.sem_inc(held_pool, 1)
                xt = x_all[:, NT * b + qt, :]
                pool_.tensor_tensor(xt, xt, y_a[:, :], ALU.add).then_inc(a_x, 1)

            def token_rstd(g):
                need(pool, n_var, g + 1)
                ch.step(pool_.tensor_tensor(rstd_n[:, 0, :], mv_n[:, :, 1], eps5[:, 0:NT], ALU.add))
                ch.wait()
                pool_.tensor_tensor(rstd_n[:, 1, :], rstd_n[:, 0, :], half[:, 0:NT], ALU.pow).then_inc(n_rstd, 1)

            def batch(b, first=False, last=False):
                if not first:
                    residual(b - 1, 0)
                if not last:
                    rstd(b + 1)
                if not first:
                    out_rstd(b - 1, 1)
                    residual(b - 1, 1)
                    token_rstd(b - 1)
                if not last:
                    norms(b + 1, 0)
                    for i in range(1, KT + NT):
                        low(b + 1, i - 1)
                        norms(b + 1, i)
                    low(b + 1, KT + NT - 1)
                out_rstd(b, 0)

            rstd(0)
            for i in range(KT + NT + 1):
                if i < KT + NT:
                    norms(0, i)
                if i:
                    low(0, i - 1)
            pool.wait_ge(small_in, SMALL * 16)
            pool.wait_ge(gates_ready, 1)
            ch.step(pool_.tensor_scalar(ln_o[:, :, :], ln_o[:, :, :], gates[:, 0:1], 1.0, ALU.mult, ALU.mult))
            batch(0, first=True)
            fore, per = ch.n, 13
            with pool.Fori(1, B - 1) as b:
                ch.base, ch.n = fore + per * (b - 1), 0
                batch(b)
                assert ch.n == per, ch.n
            ch.leave(fore + per * (B - 2))
            batch(B - 1, last=True)
            residual(B - 1, 0)
            out_rstd(B - 1, 1)
            residual(B - 1, 1)
            pool_late(pool, ch, token_rstd)

        @block.vector
        def _(dve):
            ch = Chain(dve, dve_steps)
            ch.step(dve_.memset(mask_row[:, :], 0.0))

            def hold(semaphore, value):
                if isinstance(value, int) and value <= 0:
                    return
                dve.wait_ge(semaphore, value)
                if not isinstance(value, int):
                    dve.sem_inc(held, 1)

            def token_tile(b, t):
                return c_all[:, NT * b + t, :] if t < NT else x_all[:, NT * b + t - NT, :]

            def token_stats(b):
                for t in range(NT):
                    ch.step(dve_.bn_stats(stat_n[:, t, :], x_all[:, NT * b + t, :]))
                hold(dve_steps, ch.base + ch.n)
                for t in range(NT):
                    last = dve_.bn_aggr(mv_n[:, t, :], stat_n[:, t, :])
                last.then_inc(n_var, 1)

            def token_norm(b, g):
                need(dve, n_rstd, g + 1)
                need(dve, n_hT, g)
                for t in range(NT):
                    last = dve_.tensor_scalar(h_cur[:, t, :], x_all[:, NT * b + t, :], mv_n[:, t, 0:1],
                                              rstd_n[:, 1, t:t + 1], ALU.subtract, ALU.mult)
                last.then_inc(n_h, 1)

            def stats(b):
                for t in range(KT):
                    ch.step(dve_.bn_stats(stat_a[:, t, :], token_tile(b, t)))
                hold(dve_steps, ch.base + ch.n)
                hold(a_xn, b)
                for t in range(KT):
                    last = dve_.bn_aggr(mv_a[:, t, :], stat_a[:, t, :])
                last.then_inc(a_var, 1)

            def norm(b):
                need(dve, a_rstd, b + 1)
                need(dve, a_xT_ps, ND * b)
                for t in range(KT):
                    last = dve_.tensor_scalar(xn_a[:, t, :], token_tile(b, t), mv_a[:, t, 0:1], rstd_a[:, t:t + 1],
                                              ALU.subtract, ALU.mult)
                last.then_inc(a_xn, 1)

            def head_sums(b, i):
                need(dve, a_sq, 6 * b + i + 1)
                ch.step(dve_.tensor_reduce(sumsq[:, i, :], heads(square[:, i % 2, :]), AX, ALU.add))
                ch.wait()
                dve_.tensor_scalar(sumsq[:, i, :], sumsq[:, i, :], 1e-24, None, ALU.max).then_inc(a_ss, 1)

            def unit_norm(b, i):
                need(dve, a_rn, 6 * b + i + 1)
                need(dve, a_lo, 6 * b + i - 1)
                n = heads(normed[:, i % 2, :])
                ins = dve_.tensor_tensor(n, heads(banks[KQ_BANK[i]][:, :]), across(rnorm[:, i, :], DH), ALU.mult)
                if i >= KT:
                    ch.step(ins)
                    ch.wait()
                    ins = dve_.tensor_tensor(n, n, qk_scale[:, 0:1, :].broadcast_to([P, HA, DH]), ALU.mult)
                ins.then_inc(a_kn, 1)

            def transposed(b, j):
                need(dve, a_kqT_ps, 8 * b + j + 1)
                qt, v = divmod(j - KT, 2)
                dst = kT16[:, :, P * j:P * j + P] if j < KT else qT16[:, v, :, P * qt:P * qt + P]
                dve_.tensor_copy(dst, bank16((j + 1) % 4).rearrange("p (h n) -> p h n", h=HA)).then_inc(a_kqT, 1)

            def maximum(b, u):
                need(dve, a_ex, UNITS * b + u - 1)
                hold(a_s_ps, UNITS * b + u + 1)
                dve_.tensor_tensor_reduce(out=scores[:, u % 2, :], in0=banks[2 + u % 2][:, :], in1=mask_row[:, :],
                                          scale=-8.0, scalar=3e38, op0=ALU.add, op1=ALU.min,
                                          accum_out=negmax[:, u:u + 1]).then_inc(a_max, 1)

            def copy_pT(b, u):
                need(dve, a_pT_ps, UNITS * b + u + 1)
                need(dve, a_pv, UNITS * b + u - 1)
                dve_.tensor_copy(probsT[:, u % 2, :], banks[4 + u % 2][:, :]).then_inc(a_pT[0], 1)

            def divide(b, qt):
                need(dve, a_pv, UNITS * b + HA * (qt + 1))
                ch.step(dve_.reciprocal(recip_a[:, :], rowsum[:, HA * qt:HA * qt + HA]))
                ch.wait()
                need(dve, a_oT_ps, NT * b + qt)
                dve_.tensor_tensor(heads(o_a[:, :]), heads(banks[6 + qt][:, :]), across(recip_a[:, :], DH),
                                   ALU.mult).then_inc(a_on, 1)

            def out_stats(b, qt):
                need(dve, a_wo_ps, NT * b + qt + 1)
                ch.step(dve_.bn_stats(stat_o[:, :], banks[5 * qt][:, 0:D]))
                hold(dve_steps, ch.base + ch.n)
                dve_.bn_aggr(mv_o[:, :], stat_o[:, :]).then_inc(a_ovar, 1)

            def out_norm(b, qt):
                need(dve, a_orstd, NT * b + qt + 1)
                need(dve, a_x, NT * b + qt)
                dve_.tensor_scalar(y_a[:, :], banks[5 * qt][:, 0:D], mv_o[:, 0:1], rstd_o[:, 1:2], ALU.subtract,
                                   ALU.mult).then_inc(a_y, 1)

            def batch(b, first=False, last=False):
                if not first:
                    divide(b - 1, 1)
                    out_norm(b - 1, 0)
                if not last:
                    stats(b + 1)
                for j in range(8):
                    transposed(b, j)
                    if j == 3 and not first:
                        out_stats(b - 1, 1)
                    if j == 4 and not first:
                        out_norm(b - 1, 1)
                ch.step(dve_.tensor_scalar(mask_row[:, 0:S], mask8[:, b, :], OFF, -OFF, ALU.mult, ALU.add))
                hold(dve_steps, ch.base + ch.n)
                maximum(b, 0)
                maximum(b, 1)
                if not last:
                    norm(b + 1)
                for u in range(UNITS):
                    if u + 2 < UNITS:
                        maximum(b, u + 2)
                    if u % 2 == 0:
                        copy_pT(b, u)
                    if u == 1 and not first:
                        hold(a_x, NT * b)
                        token_stats(b - 1)
                    if u == 3 and not first:
                        token_norm(b - 1, b - 1)
                    for i in range(KT + NT):
                        if u == KQ_UNIT[i] + 2 and not last:
                            head_sums(b + 1, i)
                        if u == KQ_UNIT[i] + 3 and not last:
                            unit_norm(b + 1, i)
                    if u == HA + 1:
                        divide(b, 0)
                out_stats(b, 0)

            dve.wait_ge(c_in[0], 16)
            dve.wait_ge(x_in[0], 16)
            stats(0)
            norm(0)
            dve.wait_ge(small_in, SMALL * 16)
            ch.step(dve_.tensor_tensor(qk_scale[:, 0, :], qk_scale[:, 0, :], qk_scale[:, 1, :], ALU.mult))
            for i in range(KT + NT + 1):
                if i < KT + NT:
                    head_sums(0, i)
                if i:
                    unit_norm(0, i - 1)
            for i in range(1, 4):
                dve.wait_ge(c_in[i], 16)
                dve.wait_ge(x_in[i], 16)
            batch(0, first=True)
            batch(1)
            fore, per = ch.n, 19
            with dve.Fori(2, B - 1) as b:
                ch.base, ch.n = fore + per * (b - 2), 0
                batch(b)
                assert ch.n == per, ch.n
            ch.leave(fore + per * (B - 3))
            batch(B - 1, last=True)
            divide(B - 1, 1)
            out_norm(B - 1, 0)
            out_stats(B - 1, 1)
            out_norm(B - 1, 1)
            dve_late(dve, ch, token_stats, token_norm)

        @block.scalar
        def _(act):
            def row(ap):
                return ap.unsqueeze(0).broadcast_to([P, ap.shape[0]])

            pre = "L0_xattn_"
            act.dma_start(ln_cols[:, :, :], io["ln_cols"]).then_inc(cols_in, 16)
            small = [(gates[:, 0:2], row(io["g_xattn"])), (gates[:, 2:4], row(io["g_ffn"])),
                     (qk_scale[:, 0, :], row(io[pre + "q_scale"])), (qk_scale[:, 1, :], row(io[pre + "k_scale"])),
                     (ln_o[:, 0, :], row(io[pre + "ln_o_w"])), (ln_o[:, 1, :], row(io[pre + "ln_o_b"])),
                     (mask8[:, :, :], io["mask_BxS2_bk0"].unsqueeze(0).broadcast_to([P, B, S]))]
            assert len(small) == SMALL
            for dst, src in small:
                act.dma_start(dst, src).then_inc(small_in, 16)

            def copy_xT(b):
                for dt in range(ND):
                    need(act, a_xT_ps, ND * b + dt + 1)
                    for part in range(2):
                        w, c = ln_cols[:, 2 * part, dt:dt + 1], ln_cols[:, 2 * part + 1, dt:dt + 1]
                        cut = slice(S * part, S * part + S)
                        last = act_.activation(xT_a[:, dt, cut], banks[dt][:, cut], ACT.Identity, bias=c, scale=w)
                    last.then_inc(a_xT, 1)

            def squares(b, i):
                need(act, a_kq_ps, 6 * b + i + 1)
                need(act, a_ss, 6 * b + i - 1)
                act_.activation(square[:, i % 2, :], banks[KQ_BANK[i]][:, :], ACT.Square).then_inc(a_sq, 1)

            def high(b, i):
                need(act, a_kn, 6 * b + i + 1)
                n = heads(normed[:, i % 2, :])
                if i < KT:
                    act_.activation(kk16[:, i, :, 0:DH], n, ACT.Copy).then_inc(a_hi, 1)
                else:
                    q = qq16[:, i - KT, :, :]
                    act_.activation(q[:, :, 0:DH], n, ACT.Copy)
                    act_.activation(q[:, :, 2 * DH:3 * DH], n, ACT.Copy).then_inc(a_hi, 1)

            def copy_hT(b, g, bank, sums=False, keep=False):
                loop = not isinstance(b, int)
                if keep:
                    act.wait_ge(n_h, g + 1)
                    if loop:
                        act.sem_inc(held_act, 1)
                    act_.activation(h_all[:, bass.ds(NT * b, NT), :], h_cur[:, :, :], ACT.Copy)
                act.wait_ge(n_ps, g + 1)
                if loop:
                    act.sem_inc(held_act, 1)
                for dt in range(ND):
                    extra = dict(accum_out=h_sum[:, dt, bass.ds(b, 1)]) if sums else {}
                    last = act_.activation(hT_all[:, bass.ds(b, 1), dt, :],
                                           banks[bank][:, S * dt:S * dt + S].unsqueeze(1), ACT.Copy, **extra)
                last.then_inc(n_hT, 1)

            def copy_v(b, t):
                need(act, a_v_ps, KT * b + t + 1)
                act_.activation(v_a[:, t, :], banks[6 + t % 2][:, :], ACT.Copy).then_inc(a_v, 1)

            def exps(b, u):
                need(act, a_max, UNITS * b + u + 1)
                need(act, a_pT_ps, UNITS * b + u - 1)
                act_.activation(probs[:, u % 2, :], scores[:, u % 2, :], ACT.Exp, bias=negmax[:, u:u + 1], scale=-1.0,
                                accum_out=rowsum[:, u:u + 1]).then_inc(a_ex, 1)

            def copy_pT(b, u):
                need(act, a_pT_ps, UNITS * b + u + 1)
                need(act, a_pv, UNITS * b + u - 1)
                act_.activation(probsT[:, u % 2, :], banks[4 + u % 2][:, :], ACT.Copy).then_inc(a_pT[1], 1)

            def copy_oT(b, qt):
                need(act, a_oT_ps, NT * b + qt + 1)
                need(act, a_wo_ps, NT * b + qt)
                act_.activation(oT_a[:, :, :], banks[4 * qt][:, :].rearrange("p (k n) -> p k n", n=P), ACT.Copy)\
                    .then_inc(a_oT, 1)

            def batch(b, first=False, last=False):
                if not first:
                    copy_v(b, 0)
                    copy_oT(b - 1, 1)
                    for t in range(1, KT):
                        copy_v(b, t)
                exps(b, 0)
                for u in range(UNITS):
                    if u + 1 < UNITS:
                        exps(b, u + 1)
                    if u == 0 and not last:
                        copy_xT(b + 1)
                    if u % 2:
                        copy_pT(b, u)
                    if u - 1 in KQ_UNIT and not last:
                        squares(b + 1, KQ_UNIT.index(u - 1))
                    if u - 3 in KQ_UNIT[:-1] and not last:
                        high(b + 1, KQ_UNIT.index(u - 3))
                    if u == HA + 5:
                        copy_oT(b, 0)
                if not last:
                    high(b + 1, KT + NT - 1)
                if not first:
                    copy_hT(b - 1, b - 1, 5, sums=True)

            act.wait_ge(cols_in, 16)
            copy_xT(0)
            act.wait_ge(small_in, SMALL * 16)
            act_.activation(gates[:, :], gates[:, :], ACT.Tanh).then_inc(gates_ready, 1)
            n = KT + NT
            for i in range(n + 2):
                if i < n:
                    squares(0, i)
                if i > 1:
                    high(0, i - 2)
                if 0 < i <= KT:
                    copy_v(0, i - 1)
            batch(0, first=True)
            with act.Fori(1, B - 1) as b:
                batch(b)
            batch(B - 1, last=True)
            copy_oT(B - 1, 1)
            act_late(act, copy_hT)

        @block.tensor
        def _(pe):
            def transposes_x(b):
                need(pe, a_xn, b + 1)
                need(pe, a_kqT, 8 * b)
                for dt in range(ND):
                    for t in range(KT):
                        last = pe_.transpose(banks[dt][:, P * t:P * t + P], xn_a[:, t, P * dt:P * dt + P],
                                             ident[:, :])
                    last.then_inc(a_xT_ps, 1)

            def transposes_h(g, bank):
                need(pe, n_h, g + 1)
                for dt in range(ND):
                    for t in range(NT):
                        last = pe_.transpose(banks[bank][:, S * dt + P * t:S * dt + P * t + P],
                                             h_cur[:, t, P * dt:P * dt + P], ident[:, :])
                last.then_inc(n_ps, 1)

            def project(bank, t, w, done):
                for k in range(ND):
                    last = pe_.matmul(banks[bank][:, :], xT_a[:, k, P * t:P * t + P], w[:, k, :], start=k == 0,
                                      stop=k == ND - 1)
                last.then_inc(done, 1)

            def project_kq(b, i):
                if i == 0:
                    need(pe, a_xT, ND * b + ND)
                else:
                    before = max((k for k in range(i) if KQ_BANK[k] == KQ_BANK[i]), default=-1)
                    if before >= 0:
                        need(pe, a_kn, 6 * b + before + 1)
                if i < KT:
                    project(KQ_BANK[i], i, wkv_a[:, :, 0:INNER], a_kq_ps)
                else:
                    project(KQ_BANK[i], i - KT + NT, wq_a, a_kq_ps)

            def project_v(b, t):
                need(pe, a_v, KT * b + t - 1)
                project(6 + t % 2, t, wkv_a[:, :, INNER:], a_v_ps)

            def transposes_kq(b, j):
                qt, v = divmod(j - KT, 2)
                need(pe, a_lo, 6 * b + (j if j < KT else KT + qt) + 1)
                if j == 0:
                    need(pe, a_kn, 6 * b + KT + NT)
                if j == 3:
                    need(pe, a_y, NT * (b - 1) + 1)
                if j >= 4:
                    need(pe, a_kqT, 8 * b + j - 3)
                dst = bank16((j + 1) % 4)
                src = kk16[:, j, :, :] if j < KT else qq16[:, qt, :, DH * v:DH * v + 2 * DH]
                for h in range(HA):
                    last = pe_.transpose(dst[:, P * h:P * h + P], src[:, h, :], ident16[:, :])
                last.then_inc(a_kqT_ps, 1)

            def scores_of(b, u):
                qt, h = divmod(u, HA)
                if u == 0:
                    need(pe, a_kqT, 8 * b + 8)
                if u >= 2:
                    need(pe, a_max, UNITS * b + u - 1)
                for v in range(2):
                    last = pe_.matmul(banks[2 + u % 2][:, :], qT16[:, v, h, P * qt:P * qt + P], kT16[:, h, :],
                                      start=v == 0, stop=v == 1)
                last.then_inc(a_s_ps, 1)

            def transposes_p(b, u):
                need(pe, a_ex, UNITS * b + u + 1)
                if u >= 2:
                    need(pe, a_pT[u % 2], UNITS // 2 * b + u // 2)
                if u == 1:
                    need(pe, a_y, NT * b)
                for kt in range(KT):
                    last = pe_.transpose(banks[4 + u % 2][:, P * kt:P * kt + P], probs[:, u % 2, P * kt:P * kt + P],
                                         ident[:, :])
                last.then_inc(a_pT_ps, 1)

            def values(b, u):
                qt, h = divmod(u, HA)
                need(pe, a_pT[u % 2], UNITS // 2 * b + u // 2 + 1)
                if u == 0:
                    need(pe, a_v, KT * b + KT)
                for kt in range(KT):
                    last = pe_.matmul(banks[6 + qt][:, DH * h:DH * h + DH], probsT[:, u % 2, P * kt:P * kt + P],
                                      v_a[:, kt, DH * h:DH * h + DH], start=kt == 0, stop=kt == KT - 1)
                last.then_inc(a_pv, 1)

            def transposes_o(b, qt):
                need(pe, a_on, NT * b + qt + 1)
                for k in range(INNER // P):
                    last = pe_.transpose(banks[4 * qt][:, P * k:P * k + P], o_a[:, P * k:P * k + P], ident[:, :])
                last.then_inc(a_oT_ps, 1)

            def out_project(b, qt):
                need(pe, a_oT, NT * b + qt + 1)
                need(pe, a_y, NT * b + qt)
                for k in range(INNER // P):
                    last = pe_.matmul(banks[5 * qt][:, 0:D], oT_a[:, k, :], wo_a[:, k, :], start=k == 0,
                                      stop=k == INNER // P - 1)
                last.then_inc(a_wo_ps, 1)

            def batch(b, first=False, last=False):
                if not first:
                    project_v(b, 0)
                transposes_kq(b, 0)
                if not first:
                    transposes_o(b - 1, 1)
                transposes_kq(b, 1)
                if not first:
                    project_v(b, 1)
                transposes_kq(b, 2)
                if not first:
                    need(pe, n_hT, b - 1)
                    out_project(b - 1, 1)
                transposes_kq(b, 3)
                if not first:
                    project_v(b, 2)
                for j in range(4, 8):
                    transposes_kq(b, j)
                if not first:
                    project_v(b, 3)
                scores_of(b, 0)
                scores_of(b, 1)
                for u in range(UNITS):
                    if u + 2 < UNITS:
                        scores_of(b, u + 2)
                    transposes_p(b, u)
                    if u == 0 and not last:
                        transposes_x(b + 1)
                    if u == HA + 5:
                        if not last:
                            need(pe, a_kn, 6 * b + 6 + KT + 1)
                        transposes_o(b, 0)
                    if u == HA + 7:
                        if first:
                            pe.wait_ge(w2_in, 16)
                        out_project(b, 0)
                    if u in KQ_UNIT and not last:
                        project_kq(b + 1, KQ_UNIT.index(u))
                    if u:
                        values(b, u - 1)
                values(b, UNITS - 1)
                if not first:
                    transposes_h(b - 1, 5)

            pe.wait_ge(ident_ready, 1)
            transposes_x(0)
            pe.wait_ge(wk_in, 16)
            pe.wait_ge(wq_in, 16)
            for i in range(KT + NT):
                project_kq(0, i)
                if i == 1:
                    pe.wait_ge(wv_in, 16)
                if 0 < i <= KT:
                    project_v(0, i - 1)
            batch(0, first=True)
            batch(1)
            with pe.Fori(2, B - 1) as b:
                batch(b)
            batch(B - 1, last=True)
            need(pe, n_hT, B - 1)
            transposes_o(B - 1, 1)
            out_project(B - 1, 1)
            pe_late(pe, transposes_h)



def kernel(**inputs):
    import numpy as np
    import concourse.bacc as bacc
    from concourse.bass_utils import run_bass_kernel_spmd as run

    nc = bacc.Bacc("TRN2", target_bir_lowering=False, num_devices=1)
    arrays, io = {}, {}
    laid = {name: np.asarray(value) for name, value in inputs.items()}
    by_width = [laid.pop("L0_xattn_" + n).reshape(ND, P).T for n in ("ln_x_w", "ln_x_b", "ln_l_w", "ln_l_b")]
    laid["ln_cols"] = np.stack(by_width, axis=1)
    by_head = [laid.pop("L0_ffn_W" + n).reshape(ND, P, NH_B, DH).transpose(1, 2, 0, 3) for n in "qkv"]
    laid["head_weights"] = np.stack(by_head, axis=2).reshape(P, NH_B, 6 * DH)
    biases = np.stack([laid.pop("L0_ffn_b" + n).reshape(NH_B, DH).T for n in "qk"], axis=2)
    laid["head_biases"] = np.concatenate([biases, biases], axis=0)
    laid["norm_cols"] = np.stack([laid["L1_xattn_ln_" + n].reshape(ND, P).T for n in ("gamma", "beta")], axis=1)
    laid["em"] = laid.pop("mask_BxS2_ff1").reshape(B * NT, P).T
    for name, value in laid.items():
        a = np.ascontiguousarray(value)
        arrays[f"in_{name}"] = a
        io[name] = nc.dram_tensor(f"in_{name}", a.shape, mybir.dt.from_np(a.dtype), kind="ExternalInput").ap()
    io["out"] = nc.dram_tensor("out_0", (B, S, D), F32, kind="ExternalOutput").ap()
    build(nc, io)
    return run(nc, [arrays], core_ids=[0]).results[0]["out_0"]
```
